# Optimizing a Trainium2 kernel written in Bass

```python
import numpy as np
import jax
import jax.numpy as jnp

def _softmax(x, axis=-1):
    return jax.nn.softmax(x, axis=axis)

def _gelu(x):
    return jax.nn.gelu(x, approximate=True)

def _silu(x):
    return jax.nn.silu(x)

def _sigmoid(x):
    return jax.nn.sigmoid(x)

def _layernorm(x, axis=-1, eps=1e-05):
    m = jnp.mean(x, axis=axis, keepdims=True)
    v = jnp.var(x, axis=axis, keepdims=True)
    return (x - m) / jnp.sqrt(v + eps)

def _scatter_add(tgt, idx, src, axis=0):
    return tgt.at[idx].add(src)

def _segment_sum(src, seg, n):
    return jax.ops.segment_sum(src, seg, n)
kernel_name = 'mk_pixart_seq_d4_seqx_r4_530cda'

def setup_inputs(seed: int=0):
    np.random.seed(seed)
    _w = jnp.asarray

    def _rec_inputs():
        import jax
        import jax.numpy as jnp
        _rk = jax.random.key(seed)
        x = -0.0003929 + 0.9999 * jax.random.normal(jax.random.fold_in(_rk, 1), (1, 2048, 256), jnp.float32)
        _lenS = 2048 - jax.random.randint(jax.random.fold_in(_rk, 7), (1,), 0, max(1, 2048 // 4) + 1, jnp.int32)
        _lenS2 = 1601 - jax.random.randint(jax.random.fold_in(_rk, 8), (1,), 0, max(1, 1601 // 4) + 1, jnp.int32)
        _ctx_1024P = jax.random.normal(jax.random.fold_in(_rk, 11), (1, 16, 256), jnp.float32)
        _ctx_1024c = jax.random.dirichlet(jax.random.fold_in(_rk, 511), 0.3 * jnp.ones((16,), jnp.float32), (1, 1601))
        _ctx_1024t = jnp.einsum('bsk,bkd->bsd', _ctx_1024c, _ctx_1024P)
        _ctx_1024t = _ctx_1024t * jax.lax.rsqrt(jnp.mean(jnp.square(_ctx_1024t)) + 1e-12) * 0.953939
        ctx_1024 = -1.39393e-06 + 0.999914 * (_ctx_1024t + 0.3 * jax.random.normal(jax.random.fold_in(_rk, 611), (1, 1601, 256), jnp.float32))
        cond_1024 = -0.00920427 + 1.00102 * jax.random.normal(jax.random.fold_in(_rk, 12), (1, 256), jnp.float32)
        _validS = jnp.arange(2048)[None, :] < _lenS[:, None]
        _validS2 = jnp.arange(1601)[None, :] < _lenS2[:, None]
        _causal = jnp.tril(jnp.ones((2048, 2048), dtype=bool))
        mask_BxS2_bf0 = jnp.logical_not(jnp.ones((1, 1601), dtype=bool))
        return (x, ctx_1024, cond_1024, mask_BxS2_bf0)
    x, ctx_1024, cond_1024, mask_BxS2_bf0 = _rec_inputs()

    def _L0_xcond_setup():
        import jax, jax.numpy as jnp
        import numpy as np
        EPS = 1e-05

        def _ada_ln(x, c, W_ss, b_ss):
            mu = jnp.mean(x, axis=-1, keepdims=True)
            var = jnp.mean((x - mu) ** 2, axis=-1, keepdims=True)
            h = (x - mu) / jnp.sqrt(var + EPS)
            ss = jax.nn.silu(c) @ W_ss + b_ss
            scale, bias = jnp.split(ss, 2, axis=-1)
            return (1.0 + scale)[:, None, :] * h + bias[:, None, :]
        key = jax.random.key(seed)
        ks = jax.random.split(key, 12)
        B, Lq, Lkv, H = (8, 512, 128, 256)
        s = 0.02
        return {'x_q': jax.random.normal(ks[0], (B, Lq, H), jnp.float32), 'x_kv': jax.random.normal(ks[1], (B, Lkv, H), jnp.float32), 't_vec': jax.random.normal(ks[2], (B, H), jnp.float32), 'Wq': jax.random.normal(ks[3], (H, H), jnp.float32) * s, 'bq': jnp.zeros((H,), jnp.float32), 'Wkv': jax.random.normal(ks[4], (H, 2 * H), jnp.float32) * s, 'bkv': jnp.zeros((2 * H,), jnp.float32), 'Wp': jax.random.normal(ks[5], (H, H), jnp.float32) * s, 'bp': jnp.zeros((H,), jnp.float32), 'Wss_q': jax.random.normal(ks[6], (H, 2 * H), jnp.float32) * s, 'bss_q': jnp.zeros((2 * H,), jnp.float32), 'Wss_kv': jax.random.normal(ks[7], (H, 2 * H), jnp.float32) * s, 'bss_kv': jnp.zeros((2 * H,), jnp.float32)}
    _L0_xcond_all = _L0_xcond_setup()
    _L0_xcond_in = {k: v for k, v in _L0_xcond_all.items() if k in ('Wq', 'bq', 'Wkv', 'bkv', 'Wp', 'bp', 'Wss_q', 'bss_q', 'Wss_kv', 'bss_kv')}
    del _L0_xcond_all

    def _L1_xcond_setup():
        import jax, jax.numpy as jnp
        import numpy as np
        H = 256
        RH = 2 * H
        E = 3
        B, T, P = (8, 512, 64)
        LN_EPS = 1e-05

        def _layer_norm(x, gamma, beta):
            mu = jnp.mean(x, axis=-1, keepdims=True)
            var = jnp.mean(jnp.square(x - mu), axis=-1, keepdims=True)
            return (x - mu) * jax.lax.rsqrt(var + LN_EPS) * gamma + beta
        key = jax.random.key(seed)
        ks = jax.random.split(key, 24)
        s = lambda fan_in: 1.0 / np.sqrt(fan_in)
        inp = {'mix_hidden_states': jax.random.normal(ks[0], (B, T, H), jnp.float32), 'global_anchor': jax.random.normal(ks[1], (B, H), jnp.float32), 'prototype_bank': jax.random.normal(ks[2], (B, P, H), jnp.float32), 'ln_gamma': jnp.ones((H,), jnp.float32), 'ln_beta': jnp.zeros((H,), jnp.float32), 'Wq': jax.random.normal(ks[3], (H, H), jnp.float32) * s(H), 'Wk': jax.random.normal(ks[4], (H, H), jnp.float32) * s(H), 'Wv': jax.random.normal(ks[5], (H, H), jnp.float32) * s(H), 'router_W': jax.random.normal(ks[6], (3 * H, E), jnp.float32) * s(3 * H), 'router_b': jnp.zeros((E,), jnp.float32), 'e_w1': jax.random.normal(ks[7], (E, 3 * H, RH), jnp.float32) * s(3 * H), 'e_b1': jnp.zeros((E, RH), jnp.float32), 'e_w2': jax.random.normal(ks[8], (E, RH, H), jnp.float32) * s(RH), 'e_b2': jnp.zeros((E, H), jnp.float32), 'gate_w1': jax.random.normal(ks[9], (3 * H, H), jnp.float32) * s(3 * H), 'gate_b1': jnp.zeros((H,), jnp.float32), 'gate_w2': jax.random.normal(ks[10], (H, H), jnp.float32) * s(H), 'gate_b2': jnp.zeros((H,), jnp.float32), 'out_w': jax.random.normal(ks[11], (H, H), jnp.float32) * s(H), 'out_b': jnp.zeros((H,), jnp.float32)}
        return inp
    _L1_xcond_all = _L1_xcond_setup()
    _L1_xcond_in = {k: v for k, v in _L1_xcond_all.items() if k in ('ln_gamma', 'ln_beta', 'Wq', 'Wk', 'Wv', 'router_W', 'router_b', 'e_w1', 'e_b1', 'e_w2', 'e_b2', 'gate_w1', 'gate_b1', 'gate_w2', 'gate_b2', 'out_w', 'out_b')}
    del _L1_xcond_all

    def _L2_xcond_setup():
        import jax, jax.numpy as jnp
        import numpy as np
        LN_EPS = 1e-06

        def _ln(x):
            mu = jnp.mean(x, axis=-1, keepdims=True)
            var = jnp.var(x, axis=-1, keepdims=True)
            return (x - mu) * jax.lax.rsqrt(var + LN_EPS)
        key = jax.random.key(seed)
        H, NH = (256, 16)
        B, N, S = (4, 256, 77)
        MLP = int(H * 4.0)
        ks = jax.random.split(key, 20)
        s = 1.0 / np.sqrt(H)
        return {'x': jax.random.normal(ks[0], (B, N, H), jnp.float32), 'c': jax.random.normal(ks[1], (B, H), jnp.float32), 'context': jax.random.normal(ks[2], (B, S, H), jnp.float32), 'W_mod': jax.random.normal(ks[3], (H, 6 * H), jnp.float32) * s, 'b_mod': jnp.zeros((6 * H,), jnp.float32), 'W_qkv': jax.random.normal(ks[4], (H, 3 * H), jnp.float32) * s, 'b_qkv': jnp.zeros((3 * H,), jnp.float32), 'W_proj': jax.random.normal(ks[5], (H, H), jnp.float32) * s, 'b_proj': jnp.zeros((H,), jnp.float32), 'W_qc': jax.random.normal(ks[6], (H, H), jnp.float32) * s, 'b_qc': jnp.zeros((H,), jnp.float32), 'W_kvc': jax.random.normal(ks[7], (H, 2 * H), jnp.float32) * s, 'b_kvc': jnp.zeros((2 * H,), jnp.float32), 'W_cproj': jax.random.normal(ks[8], (H, H), jnp.float32) * s, 'b_cproj': jnp.zeros((H,), jnp.float32), 'W_mlp1': jax.random.normal(ks[9], (H, MLP), jnp.float32) * s, 'b_mlp1': jnp.zeros((MLP,), jnp.float32), 'W_mlp2': jax.random.normal(ks[10], (MLP, H), jnp.float32) * (1.0 / np.sqrt(MLP)), 'b_mlp2': jnp.zeros((H,), jnp.float32)}
    _L2_xcond_all = _L2_xcond_setup()
    _L2_xcond_in = {k: v for k, v in _L2_xcond_all.items() if k in ('W_mod', 'b_mod', 'W_qkv', 'b_qkv', 'W_proj', 'b_proj', 'W_qc', 'b_qc', 'W_kvc', 'b_kvc', 'W_cproj', 'b_cproj', 'W_mlp1', 'b_mlp1', 'W_mlp2', 'b_mlp2')}
    del _L2_xcond_all

    def _L3_xcond_setup():
        import jax, jax.numpy as jnp
        import numpy as np
        D, H, B, N, S = (256, 16, 4, 256, 77)
        HD = D // H
        DF = 4 * D
        EPS = 1e-06
        SCALE = HD ** (-0.5)

        def _ln(x):
            m = jnp.mean(x, axis=-1, keepdims=True)
            v = jnp.mean((x - m) ** 2, axis=-1, keepdims=True)
            return (x - m) / jnp.sqrt(v + EPS)
        key = jax.random.key(seed)
        ks = jax.random.split(key, 24)
        s = 0.02
        inp = {'x': jax.random.normal(ks[0], (B, N, D), jnp.float32), 't_emb': jax.random.normal(ks[1], (B, D), jnp.float32), 'context': jax.random.normal(ks[2], (B, S, D), jnp.float32), 'context_mask': jnp.zeros((B, S), jnp.bool_), 'ada_w': jax.random.normal(ks[3], (D, 6 * D), jnp.float32) * s, 'ada_b': jnp.zeros((6 * D,), jnp.float32), 'qkv_w': jax.random.normal(ks[4], (D, 3 * D), jnp.float32) * s, 'qkv_b': jnp.zeros((3 * D,), jnp.float32), 'sa_proj_w': jax.random.normal(ks[5], (D, D), jnp.float32) * s, 'sa_proj_b': jnp.zeros((D,), jnp.float32), 'q_w': jax.random.normal(ks[6], (D, D), jnp.float32) * s, 'q_b': jnp.zeros((D,), jnp.float32), 'kv_w': jax.random.normal(ks[7], (D, 2 * D), jnp.float32) * s, 'kv_b': jnp.zeros((2 * D,), jnp.float32), 'ca_proj_w': jax.random.normal(ks[8], (D, D), jnp.float32) * s, 'ca_proj_b': jnp.zeros((D,), jnp.float32), 'fc1_w': jax.random.normal(ks[9], (D, DF), jnp.float32) * s, 'fc1_b': jnp.zeros((DF,), jnp.float32), 'fc2_w': jax.random.normal(ks[10], (DF, D), jnp.float32) * s, 'fc2_b': jnp.zeros((D,), jnp.float32)}
        return inp
    _L3_xcond_all = _L3_xcond_setup()
    _L3_xcond_in = {k: v for k, v in _L3_xcond_all.items() if k in ('ada_w', 'ada_b', 'qkv_w', 'qkv_b', 'sa_proj_w', 'sa_proj_b', 'q_w', 'q_b', 'kv_w', 'kv_b', 'ca_proj_w', 'ca_proj_b', 'fc1_w', 'fc1_b', 'fc2_w', 'fc2_b')}
    del _L3_xcond_all
    return {'x': x, 'ctx_1024': ctx_1024, 'cond_1024': cond_1024, 'mask_BxS2_bf0': mask_BxS2_bf0, 'L0_xcond_Wq': _L0_xcond_in['Wq'], 'L0_xcond_bq': _L0_xcond_in['bq'], 'L0_xcond_Wkv': _L0_xcond_in['Wkv'], 'L0_xcond_bkv': _L0_xcond_in['bkv'], 'L0_xcond_Wp': _L0_xcond_in['Wp'], 'L0_xcond_bp': _L0_xcond_in['bp'], 'L0_xcond_Wss_q': _L0_xcond_in['Wss_q'], 'L0_xcond_bss_q': _L0_xcond_in['bss_q'], 'L0_xcond_Wss_kv': _L0_xcond_in['Wss_kv'], 'L0_xcond_bss_kv': _L0_xcond_in['bss_kv'], 'L1_xcond_ln_gamma': _L1_xcond_in['ln_gamma'], 'L1_xcond_ln_beta': _L1_xcond_in['ln_beta'], 'L1_xcond_Wq': _L1_xcond_in['Wq'], 'L1_xcond_Wk': _L1_xcond_in['Wk'], 'L1_xcond_Wv': _L1_xcond_in['Wv'], 'L1_xcond_router_W': _L1_xcond_in['router_W'], 'L1_xcond_router_b': _L1_xcond_in['router_b'], 'L1_xcond_e_w1': _L1_xcond_in['e_w1'], 'L1_xcond_e_b1': _L1_xcond_in['e_b1'], 'L1_xcond_e_w2': _L1_xcond_in['e_w2'], 'L1_xcond_e_b2': _L1_xcond_in['e_b2'], 'L1_xcond_gate_w1': _L1_xcond_in['gate_w1'], 'L1_xcond_gate_b1': _L1_xcond_in['gate_b1'], 'L1_xcond_gate_w2': _L1_xcond_in['gate_w2'], 'L1_xcond_gate_b2': _L1_xcond_in['gate_b2'], 'L1_xcond_out_w': _L1_xcond_in['out_w'], 'L1_xcond_out_b': _L1_xcond_in['out_b'], 'L2_xcond_W_mod': _L2_xcond_in['W_mod'], 'L2_xcond_b_mod': _L2_xcond_in['b_mod'], 'L2_xcond_W_qkv': _L2_xcond_in['W_qkv'], 'L2_xcond_b_qkv': _L2_xcond_in['b_qkv'], 'L2_xcond_W_proj': _L2_xcond_in['W_proj'], 'L2_xcond_b_proj': _L2_xcond_in['b_proj'], 'L2_xcond_W_qc': _L2_xcond_in['W_qc'], 'L2_xcond_b_qc': _L2_xcond_in['b_qc'], 'L2_xcond_W_kvc': _L2_xcond_in['W_kvc'], 'L2_xcond_b_kvc': _L2_xcond_in['b_kvc'], 'L2_xcond_W_cproj': _L2_xcond_in['W_cproj'], 'L2_xcond_b_cproj': _L2_xcond_in['b_cproj'], 'L2_xcond_W_mlp1': _L2_xcond_in['W_mlp1'], 'L2_xcond_b_mlp1': _L2_xcond_in['b_mlp1'], 'L2_xcond_W_mlp2': _L2_xcond_in['W_mlp2'], 'L2_xcond_b_mlp2': _L2_xcond_in['b_mlp2'], 'L3_xcond_ada_w': _L3_xcond_in['ada_w'], 'L3_xcond_ada_b': _L3_xcond_in['ada_b'], 'L3_xcond_qkv_w': _L3_xcond_in['qkv_w'], 'L3_xcond_qkv_b': _L3_xcond_in['qkv_b'], 'L3_xcond_sa_proj_w': _L3_xcond_in['sa_proj_w'], 'L3_xcond_sa_proj_b': _L3_xcond_in['sa_proj_b'], 'L3_xcond_q_w': _L3_xcond_in['q_w'], 'L3_xcond_q_b': _L3_xcond_in['q_b'], 'L3_xcond_kv_w': _L3_xcond_in['kv_w'], 'L3_xcond_kv_b': _L3_xcond_in['kv_b'], 'L3_xcond_ca_proj_w': _L3_xcond_in['ca_proj_w'], 'L3_xcond_ca_proj_b': _L3_xcond_in['ca_proj_b'], 'L3_xcond_fc1_w': _L3_xcond_in['fc1_w'], 'L3_xcond_fc1_b': _L3_xcond_in['fc1_b'], 'L3_xcond_fc2_w': _L3_xcond_in['fc2_w'], 'L3_xcond_fc2_b': _L3_xcond_in['fc2_b']}

def reference(x, ctx_1024, cond_1024, mask_BxS2_bf0, L0_xcond_Wq, L0_xcond_bq, L0_xcond_Wkv, L0_xcond_bkv, L0_xcond_Wp, L0_xcond_bp, L0_xcond_Wss_q, L0_xcond_bss_q, L0_xcond_Wss_kv, L0_xcond_bss_kv, L1_xcond_ln_gamma, L1_xcond_ln_beta, L1_xcond_Wq, L1_xcond_Wk, L1_xcond_Wv, L1_xcond_router_W, L1_xcond_router_b, L1_xcond_e_w1, L1_xcond_e_b1, L1_xcond_e_w2, L1_xcond_e_b2, L1_xcond_gate_w1, L1_xcond_gate_b1, L1_xcond_gate_w2, L1_xcond_gate_b2, L1_xcond_out_w, L1_xcond_out_b, L2_xcond_W_mod, L2_xcond_b_mod, L2_xcond_W_qkv, L2_xcond_b_qkv, L2_xcond_W_proj, L2_xcond_b_proj, L2_xcond_W_qc, L2_xcond_b_qc, L2_xcond_W_kvc, L2_xcond_b_kvc, L2_xcond_W_cproj, L2_xcond_b_cproj, L2_xcond_W_mlp1, L2_xcond_b_mlp1, L2_xcond_W_mlp2, L2_xcond_b_mlp2, L3_xcond_ada_w, L3_xcond_ada_b, L3_xcond_qkv_w, L3_xcond_qkv_b, L3_xcond_sa_proj_w, L3_xcond_sa_proj_b, L3_xcond_q_w, L3_xcond_q_b, L3_xcond_kv_w, L3_xcond_kv_b, L3_xcond_ca_proj_w, L3_xcond_ca_proj_b, L3_xcond_fc1_w, L3_xcond_fc1_b, L3_xcond_fc2_w, L3_xcond_fc2_b):
    import jax
    import jax.numpy as jnp

    def _L0_xcond_ref(x_q, x_kv, t_vec, Wq, bq, Wkv, bkv, Wp, bp, Wss_q, bss_q, Wss_kv, bss_kv):
        import jax, jax.numpy as jnp
        import numpy as np
        EPS = 1e-05

        def _ada_ln(x, c, W_ss, b_ss):
            mu = jnp.mean(x, axis=-1, keepdims=True)
            var = jnp.mean((x - mu) ** 2, axis=-1, keepdims=True)
            h = (x - mu) / jnp.sqrt(var + EPS)
            ss = jax.nn.silu(c) @ W_ss + b_ss
            scale, bias = jnp.split(ss, 2, axis=-1)
            return (1.0 + scale)[:, None, :] * h + bias[:, None, :]
        B, Lq, H = x_q.shape
        Lkv = x_kv.shape[1]
        nh = 16
        dh = H // nh
        xq = _ada_ln(x_q, t_vec, Wss_q, bss_q)
        xkv = _ada_ln(x_kv, t_vec, Wss_kv, bss_kv)
        q = (xq @ Wq + bq).reshape(B, Lq, nh, dh)
        kv = (xkv @ Wkv + bkv).reshape(B, Lkv, 2, nh, dh)
        k = kv[:, :, 0]
        v = kv[:, :, 1]
        scores = jnp.einsum('bqhd,bkhd->bhqk', q, k) / jnp.sqrt(jnp.float32(dh))
        attn = jax.nn.softmax(scores, axis=-1)
        out = jnp.einsum('bhqk,bkhd->bqhd', attn, v).reshape(B, Lq, H)
        return x_q + (out @ Wp + bp)

    def _L1_xcond_ref(mix_hidden_states, global_anchor, prototype_bank, ln_gamma, ln_beta, Wq, Wk, Wv, router_W, router_b, e_w1, e_b1, e_w2, e_b2, gate_w1, gate_b1, gate_w2, gate_b2, out_w, out_b):
        import jax, jax.numpy as jnp
        import numpy as np
        H = 256
        RH = 2 * H
        E = 3
        B, T, P = (8, 512, 64)
        LN_EPS = 1e-05

        def _layer_norm(x, gamma, beta):
            mu = jnp.mean(x, axis=-1, keepdims=True)
            var = jnp.mean(jnp.square(x - mu), axis=-1, keepdims=True)
            return (x - mu) * jax.lax.rsqrt(var + LN_EPS) * gamma + beta
        x = mix_hidden_states
        nx = _layer_norm(x, ln_gamma, ln_beta)
        q = nx @ Wq
        k = prototype_bank @ Wk
        v = prototype_bank @ Wv
        scores = jnp.einsum('bth,bph->btp', q, k) * H ** (-0.5)
        weights = jax.nn.softmax(scores, axis=-1)
        evidence = jnp.einsum('btp,bph->bth', weights, v)
        anchor = jnp.broadcast_to(global_anchor[:, None, :], nx.shape)
        combined = jnp.concatenate([nx, evidence, anchor], axis=-1)
        router_logits = combined @ router_W + router_b
        router_probs = jax.nn.softmax(router_logits, axis=-1)
        h = jax.nn.silu(jnp.einsum('btc,ecr->bter', combined, e_w1) + e_b1)
        expert_out = jnp.einsum('bter,erh->bteh', h, e_w2) + e_b2
        routed = jnp.sum(expert_out * router_probs[..., None], axis=-2)
        g = jax.nn.sigmoid(jax.nn.silu(combined @ gate_w1 + gate_b1) @ gate_w2 + gate_b2)
        refined_delta = g * (routed @ out_w + out_b)
        return x + refined_delta

    def _L2_xcond_ref(x, c, context, W_mod, b_mod, W_qkv, b_qkv, W_proj, b_proj, W_qc, b_qc, W_kvc, b_kvc, W_cproj, b_cproj, W_mlp1, b_mlp1, W_mlp2, b_mlp2):
        import jax, jax.numpy as jnp
        import numpy as np
        LN_EPS = 1e-06

        def _ln(x):
            mu = jnp.mean(x, axis=-1, keepdims=True)
            var = jnp.var(x, axis=-1, keepdims=True)
            return (x - mu) * jax.lax.rsqrt(var + LN_EPS)
        B, N, H = x.shape
        NH = 16
        hd = H // NH
        scale = hd ** (-0.5)
        c_proj = jax.nn.silu(c) @ W_mod + b_mod
        shift_a, scale_a, gate_a, shift_m, scale_m, gate_m = jnp.split(c_proj, 6, axis=-1)

        def modulate(t, shift, sc):
            return t * (1 + sc[:, None]) + shift[:, None]
        x_norm = modulate(_ln(x), shift_a, scale_a)
        qkv = x_norm @ W_qkv + b_qkv
        q, k, v = jnp.split(qkv, 3, axis=-1)
        q = q.reshape(B, N, NH, hd).transpose(0, 2, 1, 3)
        k = k.reshape(B, N, NH, hd).transpose(0, 2, 1, 3)
        v = v.reshape(B, N, NH, hd).transpose(0, 2, 1, 3)
        attn_w = jax.nn.softmax(jnp.einsum('bhqd,bhkd->bhqk', q, k) * scale, axis=-1)
        attn_out = jnp.einsum('bhqk,bhkd->bhqd', attn_w, v)
        attn_out = attn_out.transpose(0, 2, 1, 3).reshape(B, N, H)
        attn_out = attn_out @ W_proj + b_proj
        x = x + gate_a[:, None] * attn_out
        S = context.shape[1]
        q_c = _ln(x) @ W_qc + b_qc
        kv_c = _ln(context) @ W_kvc + b_kvc
        k_c, v_c = jnp.split(kv_c, 2, axis=-1)
        q_c = q_c.reshape(B, N, NH, hd).transpose(0, 2, 1, 3)
        k_c = k_c.reshape(B, S, NH, hd).transpose(0, 2, 1, 3)
        v_c = v_c.reshape(B, S, NH, hd).transpose(0, 2, 1, 3)
        c_attn_w = jax.nn.softmax(jnp.einsum('bhqd,bhsd->bhqs', q_c, k_c) * scale, axis=-1)
        c_attn_out = jnp.einsum('bhqs,bhsd->bhqd', c_attn_w, v_c)
        c_attn_out = c_attn_out.transpose(0, 2, 1, 3).reshape(B, N, H)
        c_attn_out = c_attn_out @ W_cproj + b_cproj
        x = x + c_attn_out
        x_norm2 = modulate(_ln(x), shift_m, scale_m)
        h = jax.nn.gelu(x_norm2 @ W_mlp1 + b_mlp1)
        h = h @ W_mlp2 + b_mlp2
        x = x + gate_m[:, None] * h
        return x

    def _L3_xcond_ref(x, t_emb, context, context_mask, ada_w, ada_b, qkv_w, qkv_b, sa_proj_w, sa_proj_b, q_w, q_b, kv_w, kv_b, ca_proj_w, ca_proj_b, fc1_w, fc1_b, fc2_w, fc2_b):
        import jax, jax.numpy as jnp
        import numpy as np
        D, H, B, N, S = (256, 16, 4, 256, 77)
        HD = D // H
        DF = 4 * D
        EPS = 1e-06
        SCALE = HD ** (-0.5)

        def _ln(x):
            m = jnp.mean(x, axis=-1, keepdims=True)
            v = jnp.mean((x - m) ** 2, axis=-1, keepdims=True)
            return (x - m) / jnp.sqrt(v + EPS)
        Bx, Nx, C = x.shape
        Sx = context.shape[1]
        mod = jax.nn.silu(t_emb) @ ada_w + ada_b
        shift_sa, scale_sa, gate_sa, shift_ff, scale_ff, gate_ff = [m[:, None, :] for m in jnp.split(mod, 6, axis=-1)]
        xm1 = _ln(x) * (1 + scale_sa) + shift_sa
        qkv = (xm1 @ qkv_w + qkv_b).reshape(Bx, Nx, 3, H, HD)
        q, k, v = (qkv[:, :, 0], qkv[:, :, 1], qkv[:, :, 2])
        attn = jnp.einsum('bnhd,bmhd->bhnm', q, k) * SCALE
        attn = jax.nn.softmax(attn, axis=-1)
        sa = jnp.einsum('bhnm,bmhd->bnhd', attn, v).reshape(Bx, Nx, C)
        sa = sa @ sa_proj_w + sa_proj_b
        x = x + gate_sa * sa
        xn2 = _ln(x)
        qc = (xn2 @ q_w + q_b).reshape(Bx, Nx, H, HD)
        kvc = (context @ kv_w + kv_b).reshape(Bx, Sx, 2, H, HD)
        kc, vc = (kvc[:, :, 0], kvc[:, :, 1])
        attn_c = jnp.einsum('bnhd,bshd->bhns', qc, kc) * SCALE
        attn_c = jnp.where(context_mask[:, None, None, :], -jnp.inf, attn_c)
        attn_c = jax.nn.softmax(attn_c, axis=-1)
        ca = jnp.einsum('bhns,bshd->bnhd', attn_c, vc).reshape(Bx, Nx, C)
        ca = ca @ ca_proj_w + ca_proj_b
        x = x + ca
        xm3 = _ln(x) * (1 + scale_ff) + shift_ff
        h = jax.nn.gelu(xm3 @ fc1_w + fc1_b, approximate=False)
        ff = h @ fc2_w + fc2_b
        x = x + gate_ff * ff
        return x
    x = _L0_xcond_ref(x, ctx_1024, cond_1024, L0_xcond_Wq, L0_xcond_bq, L0_xcond_Wkv, L0_xcond_bkv, L0_xcond_Wp, L0_xcond_bp, L0_xcond_Wss_q, L0_xcond_bss_q, L0_xcond_Wss_kv, L0_xcond_bss_kv)
    x = _L1_xcond_ref(x, cond_1024, ctx_1024, L1_xcond_ln_gamma, L1_xcond_ln_beta, L1_xcond_Wq, L1_xcond_Wk, L1_xcond_Wv, L1_xcond_router_W, L1_xcond_router_b, L1_xcond_e_w1, L1_xcond_e_b1, L1_xcond_e_w2, L1_xcond_e_b2, L1_xcond_gate_w1, L1_xcond_gate_b1, L1_xcond_gate_w2, L1_xcond_gate_b2, L1_xcond_out_w, L1_xcond_out_b)
    x = _L2_xcond_ref(x, cond_1024, ctx_1024, L2_xcond_W_mod, L2_xcond_b_mod, L2_xcond_W_qkv, L2_xcond_b_qkv, L2_xcond_W_proj, L2_xcond_b_proj, L2_xcond_W_qc, L2_xcond_b_qc, L2_xcond_W_kvc, L2_xcond_b_kvc, L2_xcond_W_cproj, L2_xcond_b_cproj, L2_xcond_W_mlp1, L2_xcond_b_mlp1, L2_xcond_W_mlp2, L2_xcond_b_mlp2)
    x = _L3_xcond_ref(x, cond_1024, ctx_1024, mask_BxS2_bf0, L3_xcond_ada_w, L3_xcond_ada_b, L3_xcond_qkv_w, L3_xcond_qkv_b, L3_xcond_sa_proj_w, L3_xcond_sa_proj_b, L3_xcond_q_w, L3_xcond_q_b, L3_xcond_kv_w, L3_xcond_kv_b, L3_xcond_ca_proj_w, L3_xcond_ca_proj_b, L3_xcond_fc1_w, L3_xcond_fc1_b, L3_xcond_fc2_w, L3_xcond_fc2_b)
    return x

_drawn_inputs = setup_inputs


def setup_inputs(seed=0):
    import zlib

    import numpy as np

    out = dict(_drawn_inputs(seed))
    spreads = {'L0_xcond_bq': (0.0, 2.0),
     'L0_xcond_bkv': (0.0, 0.275),
     'L0_xcond_bp': (0.0, 0.1),
     'L0_xcond_bss_q': (0.0, 0.8),
     'L0_xcond_bss_kv': (0.0, 0.652),
     'L1_xcond_ln_gamma': (1.0, 0.6),
     'L1_xcond_ln_beta': (0.0, 0.595),
     'L1_xcond_router_b': (0.0, 0.475),
     'L1_xcond_e_b1': (0.0, 0.458),
     'L1_xcond_e_b2': (0.0, 0.1),
     'L1_xcond_gate_b1': (0.0, 0.8),
     'L1_xcond_gate_b2': (0.0, 0.8),
     'L1_xcond_out_b': (0.0, 0.1),
     'L2_xcond_b_mod': (0.0, 0.1),
     'L2_xcond_b_qkv': (0.0, 0.1),
     'L2_xcond_b_proj': (0.0, 0.1),
     'L2_xcond_b_qc': (0.0, 0.644),
     'L2_xcond_b_kvc': (0.0, 0.1),
     'L2_xcond_b_cproj': (0.0, 0.1),
     'L2_xcond_b_mlp1': (0.0, 0.1),
     'L2_xcond_b_mlp2': (0.0, 0.1),
     'L3_xcond_ada_b': (0.0, 0.641),
     'L3_xcond_qkv_b': (0.0, 0.8),
     'L3_xcond_sa_proj_b': (0.0, 0.5),
     'L3_xcond_q_b': (0.0, 2.0),
     'L3_xcond_kv_b': (0.0, 0.375),
     'L3_xcond_ca_proj_b': (0.0, 0.1),
     'L3_xcond_fc1_b': (0.0, 0.8),
     'L3_xcond_fc2_b': (0.0, 0.589)}
    factors = {'L0_xcond_Wq': 8.0,
     'L0_xcond_Wss_q': 8.0,
     'L3_xcond_qkv_w': 5.449,
     'L3_xcond_sa_proj_w': 5.642,
     'L3_xcond_q_w': 64.0,
     'L3_xcond_fc1_w': 3.212,
     'L3_xcond_fc2_w': 2.97,
     'L3_xcond_kv_w': 3.371}
    for name, (base, spread) in spreads.items():
        noise = np.random.default_rng([zlib.crc32(name.encode()), seed]).standard_normal(out[name].shape)
        drawn = base * np.exp(spread * noise) if base else spread * noise
        out[name] = jnp.asarray(drawn.astype(out[name].dtype))
    for name, factor in factors.items():
        out[name] = (out[name] * factor).astype(out[name].dtype)
    return out
```

```python
from collections import namedtuple
from contextlib import ExitStack, contextmanager

import concourse.bass as bass
from concourse import mybir

ALU = mybir.AluOpType
ACT = mybir.ActivationFunctionType
AX = mybir.AxisListType
F32 = mybir.dt.float32
BF16 = mybir.dt.bfloat16

P = 128
D = 256
KC = D // P
NH = 16
DH = D // NH
TOK = 2048
TT = TOK // P
CTX = 1601
CT = -(-CTX // P)
BANK = 512
MASKED = -3.0e38


def cut(n, step):
    return [(i, min(step, n - i)) for i in range(0, n, step)]


def named(names, values):
    return namedtuple("Named", names)(*values)


@contextmanager
def stage(nc, name, sems, tiles=(), psum=()):
    with ExitStack() as ctx:
        handles = [ctx.enter_context(nc.semaphore(f"{name}_{n}")) for n in sems]
        s = named(sems, handles)
        b = named([t[0] for t in (*tiles, *psum)],
                  [ctx.enter_context(nc.sbuf_tensor(f"{name}_{n}", shape, dt)) for n, shape, dt in tiles]
                  + [ctx.enter_context(nc.psum_tensor(f"{name}_{n}", shape, dt)) for n, shape, dt in psum])
        yield s, b
        with nc.Block() as end:
            @end.gpsimd
            def _(pool):
                for h in handles:
                    pool.sem_clear(h)



def load_and_modulate(nc, g, a):
    mods = [("L0q", a.L0_xcond_Wss_q, a.L0_xcond_bss_q, 4), ("L0kv", a.L0_xcond_Wss_kv, a.L0_xcond_bss_kv, 4),
            ("L2", a.L2_xcond_W_mod, a.L2_xcond_b_mod, 12), ("L3", a.L3_xcond_ada_w, a.L3_xcond_ada_b, 12)]
    ncol = sum(m[3] for m in mods)
    base, at = {}, 0
    for n, _, _, c in mods:
        base[n] = at
        at += c
    scales = [base["L0q"], base["L0kv"], base["L2"] + 2, base["L2"] + 8, base["L3"] + 2, base["L3"] + 8]
    gates = [("L2", 2), ("L2", 5), ("L3", 2), ("L3", 5)]
    with stage(nc, "mod", ["loaded", "cond_in", "ones_set", "ident_zero", "ident_set", "silu_done", "bcast",
                           "cols_ready", "gates_ready", "dve_done"],
               [("w", [P, KC, ncol * P], F32), ("bcol", [P, ncol], F32), ("brow", [1, 4, D], F32),
                ("silu_b", [P, KC, P], F32), ("silu", [P, KC], F32)],
               [("cols", [P, BANK], F32), ("gate", [P, 4, BANK], F32)]) as (s, b):
        block = nc.Block()
        with block:
            @block.sync
            def _(sp):
                with nc.allow_non_contiguous_dma("a condition vector, one word per partition"):
                    sp.dma_start(g.cond[:, :], a.cond_1024.rearrange("o (k p) -> p (o k)", p=P)).then_inc(s.cond_in, 16)
                for n, w, bias, c in mods:
                    at = base[n]
                    sp.dma_start(b.w[:, :, at * P:(at + c) * P], w.rearrange("(k p) n -> p k n", p=P)).then_inc(s.loaded, 16)
                    with nc.allow_non_contiguous_dma("bias vectors, one word per partition"):
                        sp.dma_start(b.bcol[:, at:at + c], bias.rearrange("(k p) -> p k", p=P)).then_inc(s.loaded, 16)
                for i, (n, v) in enumerate(gates):
                    bias = a.L2_xcond_b_mod if n == "L2" else a.L3_xcond_ada_b
                    sp.dma_start(b.brow[:, i, :], bias[v * D:(v + 1) * D].rearrange("(o n) -> o n", o=1)).then_inc(s.loaded, 16)
                full = CTX // P
                sp.dma_start(g.x[:, :, :], a.x[0].rearrange("(t p) d -> p t d", p=P)).then_inc(s.loaded, 16)
                sp.dma_start(g.ctx[:, 0:full, :], a.ctx_1024[0, 0:full * P].rearrange("(t p) d -> p t d", p=P)).then_inc(s.loaded, 16)
                sp.dma_start(g.ctx[0:CTX - full * P, full, :], a.ctx_1024[0, full * P:CTX]).then_inc(s.loaded, 16)
                sp.wait_ge(s.loaded, 16 * (2 * len(mods) + len(gates) + 3))

            @block.gpsimd
            def _(pool):
                nc.gpsimd.memset(g.ones[:, :], 1.0).then_inc(s.ones_set, 1)
                nc.gpsimd.memset(g.ident[:, :], 0.0).then_inc(s.ident_zero, 1)
                pool.wait_ge(s.ident_zero, 1)
                nc.gpsimd.affine_select(out=g.ident[:, :], in_=g.ident[:, :], compare_op=ALU.not_equal, fill=1.0,
                                        base=0, pattern=[[-1, P]], channel_multiplier=1).then_inc(s.ident_set, 1)
                pool.wait_ge(s.ident_set, 1)
                nc.gpsimd.tensor_copy(g.ident_b[:, :], g.ident[:, :]).then_inc(s.ident_set, 1)

            @block.scalar
            def _(act):
                act.wait_ge(s.cond_in, 16)
                nc.scalar.activation(b.silu[:, :], g.cond[:, :], ACT.Silu).then_inc(s.silu_done, 1)

            @block.tensor
            def _(pe):
                pe.wait_ge(s.bcast, KC)
                pe.wait_ge(s.ones_set, 1)
                pe.wait_ge(s.loaded, 16 * (2 * len(mods) + len(gates) + 3))
                for c in range(ncol):
                    for k in range(KC):
                        mm = nc.tensor.matmul(b.cols[:, c:c + 1], b.w[:, k, c * P:(c + 1) * P], b.silu[:, k:k + 1],
                                              start=(k == 0), stop=(k == KC - 1))
                mm.then_inc(s.cols_ready, 1)
                for i, (n, v) in enumerate(gates):
                    at = (base[n] + v * KC) * P
                    for k in range(KC):
                        nc.tensor.matmul(b.gate[:, i, 0:D], b.silu_b[:, k, :], b.w[:, k, at:at + D], start=(k == 0), stop=False)
                    mm = nc.tensor.matmul(b.gate[:, i, 0:D], g.ones[0:1, :], b.brow[0:1, i, :], start=False, stop=True)
                mm.then_inc(s.gates_ready, 1)

            @block.vector
            def _(dve):
                dve.wait_ge(s.silu_done, 1)
                dve.wait_ge(s.ones_set, 1)
                for k in range(KC):
                    nc.vector.tensor_scalar(b.silu_b[:, k, :], g.ones[:, :], b.silu[:, k:k + 1], None, ALU.mult).then_inc(s.bcast, 1)
                dve.wait_ge(s.cols_ready, 1)
                nc.vector.tensor_tensor(g.mod[:, :], b.cols[:, 0:ncol], b.bcol[:, :], ALU.add).then_inc(s.dve_done, 1)
                dve.wait_ge(s.dve_done, 1)
                for c in scales:
                    nc.vector.tensor_scalar(g.mod[:, c:c + KC], g.mod[:, c:c + KC], 1.0, None, ALU.add).then_inc(s.dve_done, 1)
                dve.wait_ge(s.gates_ready, 1)
                nc.vector.tensor_copy(g.gate[:, :, :], b.gate[:, :, 0:D]).then_inc(s.dve_done, 1)
    return base



def norm_transpose(nc, g, name, src, n, dst, eps=None, scale=None, shift=None):
    tiles = cut(n, P)
    nt = len(tiles)
    groups = cut(nt, 4)
    jobs = [(k, t0, m) for t0, m in groups for k in range(KC)]
    NB = 8
    with stage(nc, name, ["stats", "aggr", "eps_added", "std", "rstd", "normed", "turned", "out_dve", "out_act", "set"],
               [("st", [P, nt, 6], F32), ("mv", [P, nt, 2], F32), ("sd", [P, nt], F32), ("rs", [P, nt], F32)]
               + ([("y", [P, nt, D], F32)] if eps is not None else []),
               [("ps", [P, NB, BANK], F32)]) as (s, b):
        y = b.y if eps is not None else src
        block = nc.Block()
        with block:
            @block.vector
            def _(dve):
                if eps is not None:
                    nc.vector.memset(b.mv[:, :, :], 1.0).then_inc(s.set, 1)
                    for t, (_, r) in enumerate(tiles):
                        nc.vector.bn_stats(b.st[0:r, t, :], src[0:r, t, :]).then_inc(s.stats, 1)
                    dve.wait_ge(s.set, 1)
                    for t, (_, r) in enumerate(tiles):
                        dve.wait_ge(s.stats, t + 1)
                        nc.vector.bn_aggr(b.mv[0:r, t, :], b.st[0:r, t, :]).then_inc(s.aggr, 1)
                    dve.wait_ge(s.aggr, nt)
                    nc.vector.tensor_scalar(b.sd[:, :], b.mv[:, :, 1], eps, None, ALU.add).then_inc(s.eps_added, 1)
                    dve.wait_ge(s.std, 1)
                    nc.vector.reciprocal(b.rs[:, :], b.sd[:, :]).then_inc(s.rstd, 1)
                    dve.wait_ge(s.rstd, 1)
                    for t, (_, r) in enumerate(tiles):
                        nc.vector.tensor_scalar(y[0:r, t, :], src[0:r, t, :], b.mv[0:r, t, 0:1], b.rs[0:r, t:t + 1],
                                                ALU.subtract, ALU.mult).then_inc(s.normed, 1)
                for j, (k, t0, m) in enumerate(jobs):
                    if j % 2 == 0:
                        dve.wait_ge(s.turned, j + 1)
                        w = sum(r for _, r in tiles[t0:t0 + m])
                        o, i = dst[:, k, t0 * P:t0 * P + w], b.ps[:, j % NB, 0:w]
                        if scale is None:
                            nc.vector.tensor_copy(o, i).then_inc(s.out_dve, 1)
                        else:
                            nc.vector.tensor_scalar(o, i, scale[:, k:k + 1], shift[:, k:k + 1], ALU.mult, ALU.add).then_inc(s.out_dve, 1)

            @block.scalar
            def _(act):
                if eps is not None:
                    act.wait_ge(s.eps_added, 1)
                    nc.scalar.activation(b.sd[:, :], b.sd[:, :], ACT.Sqrt).then_inc(s.std, 1)
                for j, (k, t0, m) in enumerate(jobs):
                    if j % 2 == 1:
                        act.wait_ge(s.turned, j + 1)
                        w = sum(r for _, r in tiles[t0:t0 + m])
                        o, i = dst[:, k, t0 * P:t0 * P + w], b.ps[:, j % NB, 0:w]
                        if scale is None:
                            nc.scalar.activation(o, i, ACT.Copy).then_inc(s.out_act, 1)
                        else:
                            nc.scalar.activation(o, i, ACT.Identity, bias=shift[:, k:k + 1], scale=scale[:, k:k + 1]).then_inc(s.out_act, 1)

            @block.tensor
            def _(pe):
                for j, (k, t0, m) in enumerate(jobs):
                    if eps is not None:
                        pe.wait_ge(s.normed, t0 + m)
                    if j >= NB:
                        pe.wait_ge(s.out_act if j % 2 else s.out_dve, (j - NB) // 2 + 1)
                    for q in range(m):
                        r = tiles[t0 + q][1]
                        mm = nc.tensor.transpose(b.ps[:, j % NB, q * P:q * P + r], y[0:r, t0 + q, k * P:(k + 1) * P], g.ident[0:r, 0:r])
                    mm.then_inc(s.turned, 1)



def split_projections(nc, g, name, jobs_in):
    blocks = [(w, m, c0, cs) for w in range(len(jobs_in)) for m in range(KC) for c0, cs in cut(jobs_in[w][1], BANK)]
    last = {}
    for j, (w, m, _, _) in enumerate(blocks):
        last[(w, m)] = j
    NB = 8
    NW = len(jobs_in)
    with stage(nc, name, ["w_in", "ready", "evac", "hi", "rest", "mid", "low", "stored"],
               [("w", [P, NW, KC, D], F32), ("bias", [P, NW, KC], F32),
                ("full", [P, 2, TOK], F32), ("rest", [P, 2, TOK], F32), ("part", [P, 2, 3, TOK], BF16)],
               [("ps", [P, NB, BANK], F32)]) as (s, b):
        groups = [(w, m) for w in range(NW) for m in range(KC)]
        block = nc.Block()
        with block:
            @block.sync
            def _(sp):
                for w, (_, _, wt, bias, _) in enumerate(jobs_in):
                    sp.dma_start(b.w[:, w], wt.rearrange("(k p) n -> p k n", p=P)).then_inc(s.w_in, 16)
                    with nc.allow_non_contiguous_dma("a bias vector, one word per partition"):
                        sp.dma_start(b.bias[:, w], bias.rearrange("(k p) -> p k", p=P)).then_inc(s.w_in, 16)
                for gi, (w, m) in enumerate(groups):
                    _, n, _, _, scr = jobs_in[w]
                    j = last[(w, m)]
                    sp.wait_ge(s.mid, j + 1)
                    sp.wait_ge(s.low, j + 1)
                    sp.dma_start(scr[:, m * P:(m + 1) * P, 0:n].rearrange("i p n -> p i n"), b.part[:, gi % 2, :, 0:n]).then_inc(s.stored, 16)
                    sp.wait_ge(s.stored, 16 * (gi + 1))

            @block.tensor
            def _(pe):
                pe.wait_ge(s.w_in, 32 * NW)
                for j, (w, m, c0, cs) in enumerate(blocks):
                    x = jobs_in[w][0]
                    if j >= NB:
                        pe.wait_ge(s.hi, j - NB + 1)
                    for k in range(KC):
                        mm = nc.tensor.matmul(b.ps[:, j % NB, 0:cs], b.w[:, w, k, m * P:(m + 1) * P], x[:, k, c0:c0 + cs],
                                              start=(k == 0), stop=(k == KC - 1))
                    mm.then_inc(s.ready, 1)

            @block.scalar
            def _(act):
                for j, (w, m, c0, cs) in enumerate(blocks):
                    gi = groups.index((w, m))
                    act.wait_ge(s.ready, j + 1)
                    if gi >= 2:
                        act.wait_ge(s.stored, 16 * (gi - 1))
                        act.wait_ge(s.low, last[groups[gi - 2]] + 1)
                    bias = b.bias[:, w, m:m + 1]
                    nc.scalar.activation(b.full[:, gi % 2, c0:c0 + cs], b.ps[:, j % NB, 0:cs], ACT.Identity, bias=bias).then_inc(s.evac, 1)
                    nc.scalar.activation(b.part[:, gi % 2, 0, c0:c0 + cs], b.ps[:, j % NB, 0:cs], ACT.Identity, bias=bias).then_inc(s.hi, 1)
                    act.wait_ge(s.rest, j + 1)
                    nc.scalar.activation(b.part[:, gi % 2, 1, c0:c0 + cs], b.rest[:, gi % 2, c0:c0 + cs], ACT.Copy).then_inc(s.mid, 1)

            @block.vector
            def _(dve):
                for j, (w, m, c0, cs) in enumerate(blocks):
                    gi = groups.index((w, m))
                    dve.wait_ge(s.evac, j + 1)
                    dve.wait_ge(s.hi, j + 1)
                    r = b.rest[:, gi % 2, c0:c0 + cs]
                    nc.vector.tensor_tensor(r, b.full[:, gi % 2, c0:c0 + cs], b.part[:, gi % 2, 0, c0:c0 + cs], ALU.subtract).then_inc(s.rest, 1)
                    dve.wait_ge(s.mid, j + 1)
                    nc.vector.tensor_tensor(b.part[:, gi % 2, 2, c0:c0 + cs], r, b.part[:, gi % 2, 1, c0:c0 + cs], ALU.subtract).then_inc(s.low, 1)


def value_projection(nc, g, name, x, n, wt, bias, keep=None):
    tiles = cut(n, P)
    NB = 8
    with stage(nc, name, ["w_in", "ready", "done", "set", "kept"],
               [("w", [P, KC, D], F32), ("bias", [P, D], F32)], [("ps", [P, NB, BANK], F32)]) as (s, b):
        block = nc.Block()
        with block:
            @block.sync
            def _(sp):
                sp.dma_start(b.w[:, :, :], wt.rearrange("(k p) n -> p k n", p=P)).then_inc(s.w_in, 16)
                sp.dma_start(b.bias[:, :], bias.partition_broadcast(P)).then_inc(s.w_in, 16)

            @block.gpsimd
            def _(pool):
                if n % P:
                    nc.gpsimd.memset(g.v[:, :, len(tiles) - 1, :], 0.0).then_inc(s.set, 1)

            @block.tensor
            def _(pe):
                pe.wait_ge(s.w_in, 32)
                for t, (c0, r) in enumerate(tiles):
                    if t >= NB:
                        pe.wait_ge(s.done, t - NB + 1)
                    for k in range(KC):
                        mm = nc.tensor.matmul(b.ps[0:r, t % NB, 0:D], x[:, k, c0:c0 + r], b.w[:, k, :], start=(k == 0), stop=(k == KC - 1))
                    mm.then_inc(s.ready, 1)

            @block.vector
            def _(dve):
                dve.wait_ge(s.w_in, 32)
                if n % P:
                    dve.wait_ge(s.set, 1)
                for t, (c0, r) in enumerate(tiles):
                    dve.wait_ge(s.ready, t + 1)
                    nc.vector.tensor_tensor(g.v[0:r, :, t, :], b.ps[0:r, t % NB, 0:D].rearrange("p (h d) -> p h d", h=NH),
                                            b.bias[0:r, :].rearrange("p (h d) -> p h d", h=NH), ALU.add).then_inc(s.done, 1)
                if keep is not None:
                    dve.wait_ge(s.done, len(tiles))
                    for t, (c0, r) in enumerate(tiles):
                        nc.vector.tensor_scalar(g.v[0:r, :, t, :], g.v[0:r, :, t, :], keep[0:r, t:t + 1], None, ALU.mult).then_inc(s.kept, 1)



def attention(nc, g, name, n, out, keep=None, mask_row=None):
    tiles = cut(n, P)
    NT = len(tiles)
    PARTS = 96
    MASKROW, ONEROWS = 96, 97
    ROWS = ONEROWS + 3
    RING = 3
    CH = 4
    step = -(-n // CH)
    chunks = cut(n, step)
    UNITS = TT * CH
    SCALE = float(DH) ** -0.5
    HALF = UNITS // 2
    FLIP = NT // 2

    RB = 3

    def entries(h, kt, ahead=2, first=False):
        if kt < FLIP:
            lo, hi = HALF + HALF * kt // FLIP, HALF + HALF * (kt + 1) // FLIP
            found = [("unit", 1, u) for u in range(lo, hi)]
        else:
            m = NT - FLIP
            lo, hi = HALF * (kt - FLIP) // m, HALF * (kt - FLIP + 1) // m
            found = [("unit", 2, u) for u in range(lo, hi)]
        found = [f for f in found if f[1] <= ahead]
        if kt == FLIP and ahead >= 1:
            found.append(("max", 1, 0))
        if kt == 2 and not first:
            found.insert(1 if found else 0, ("out", -1, 0))
        return [(kind, h + d, u) for kind, d, u in found]

    PER = UNITS + 2
    LEAD = UNITS + 1 + HALF

    def first_entry(h):
        if isinstance(h, int) and h == 0:
            return LEAD
        if isinstance(h, int) and h == NH - 1:
            return LEAD - 1 + PER * (NH - 2) + HALF + 2
        return PER * h + (LEAD - 1)

    assert PER % RB == 0 and (LEAD - 1) % RB == 0

    def entry_of_last_unit(h):
        if isinstance(h, int) and h == 0:
            return UNITS
        if isinstance(h, int) and h == 1:
            return LEAD + HALF
        return first_entry_inner(h - 1) + (HALF + 1)

    def first_entry_inner(h):
        return PER * h + (LEAD - 1)

    before_max = sum(len(entries(0, kt)) for kt in range(FLIP + 1)) - 1

    def entry_of_max(h):
        if isinstance(h, int) and h == 0:
            return UNITS
        if isinstance(h, int) and h == 1:
            return LEAD + before_max - 1
        if isinstance(h, int) and h == NH - 1:
            return first_entry_inner(h - 1) + HALF + 1
        return first_entry_inner(h - 1) + before_max

    out_at = len(entries(0, 0)) + len(entries(0, 1)) + 1
    def entry_of_out(h):
        if isinstance(h, int) and h == NH - 1:
            return first_entry(NH - 1) + 1
        if isinstance(h, int) and h == NH - 2:
            return first_entry(NH - 1)
        return first_entry_inner(h + 1) + out_at

    with stage(nc, name, ["q_in0", "q_in1", "q_in2", "v_in", "consts", "scores", "probs", "pv",
                          "ring_in", "ring_out", "neg_max", "split", "m_in", "acc_out", "rsum", "mask_in"],
               [("q", [P, RING, TOK], BF16), ("k", [P, RING, NT * P], BF16), ("v", [P, RING, NT, 2 * DH], F32),
                ("p", [P, 2, 2, 2 * BANK], F32), ("mx", [P, 2, TT, CH], F32), ("nm", [P, TT], F32),
                ("rest", [P, 2, TT], F32), ("mparts", [P, P // TT, TT], BF16), ("mt", [3 * TT, P], BF16),
                ("o_t", [P, BANK], F32), ("rs", [P, TT], F32)],
               [("s", [P, 2, 2, BANK], F32), ("ring", [P, RB, BANK], F32), ("acc", [P, BANK], F32)]) as (s, b):
        q_in = [s.q_in0, s.q_in1, s.q_in2]
        LOAD = 6 * 16
        CONSTS = 5 + (NT if keep is not None else 0)

        block = nc.Block()
        with block:
            def load_head(sp, h, r):
                qs = g.q_scr[:, bass.ds(h * DH, DH), :]
                ks = g.k_scr[:, bass.ds(h * DH, DH), 0:n]
                sp.dma_start(b.q[0:48, r, :], qs[0:1].broadcast_to([3, DH, TOK])).then_inc(q_in[r], 16)
                sp.dma_start(b.q[48:80, r, :], qs[1:2].broadcast_to([2, DH, TOK])).then_inc(q_in[r], 16)
                sp.dma_start(b.q[80:96, r, :], qs[2:3]).then_inc(q_in[r], 16)
                sp.dma_start(b.k[0:48, r, 0:n], ks).then_inc(q_in[r], 16)
                sp.dma_start(b.k[48:80, r, 0:n], ks[0:2]).then_inc(q_in[r], 16)
                sp.dma_start(b.k[80:96, r, 0:n], ks[0:1]).then_inc(q_in[r], 16)

            def max_rows(sp, h, r):
                sp.wait_ge(s.ring_out, entry_of_max(h) + 1)
                sp.dma_start(b.q[ONEROWS:ROWS, r, :].rearrange("i (t c) -> i t c", t=TT), b.mt[:, :]).then_inc(s.m_in, 16)

            @block.sync
            def _(sp):
                sp.wait_ge(s.consts, 4)
                if mask_row is not None:
                    for r in range(RING):
                        sp.dma_start(b.k[MASKROW:MASKROW + 1, r, 0:n], mask_row).then_inc(s.mask_in, 16)
                for h in range(RING):
                    load_head(sp, h, h)
                max_rows(sp, 0, 0)
                def body(h, r):
                    max_rows(sp, h + 1, (r + 1) % RING)
                    sp.wait_ge(s.pv, NT * (h + 1))
                    load_head(sp, h + RING, r)
                with sp.Fori(0, 4) as i:
                    for r in range(RING):
                        body(i * RING + r, r)
                body(NH - 4, (NH - 4) % RING)
                for h in range(NH - 3, NH - 1):
                    max_rows(sp, h + 1, (h + 1) % RING)
                sp.wait_ge(s.m_in, 16 * NH)

            @block.gpsimd
            def _(pool):
                nc.gpsimd.memset(b.q[PARTS:ROWS, :, :], 1.0).then_inc(s.consts, 1)
                pool.wait_ge(s.consts, 1)
                nc.gpsimd.memset(b.k[PARTS:ROWS, :, :], 1.0).then_inc(s.consts, 1)
                pool.wait_ge(s.consts, 2)
                nc.gpsimd.memset(b.k[MASKROW:MASKROW + 1, :, :], 0.0).then_inc(s.consts, 1)
                pool.wait_ge(s.consts, 3)
                nc.gpsimd.memset(b.mparts[:, 3:, :], 0.0).then_inc(s.consts, 1)
                pool.wait_ge(s.consts, 4)
                nc.gpsimd.memset(b.v[:, :, :, DH:2 * DH], 1.0).then_inc(s.consts, 1)
                pool.wait_ge(s.consts, 5)
                if keep is not None:
                    for t, (_, rows) in enumerate(tiles):
                        nc.gpsimd.tensor_scalar(b.v[0:rows, :, t, DH:2 * DH], b.v[0:rows, :, t, DH:2 * DH],
                                                keep[0:rows, t:t + 1], None, ALU.mult).then_inc(s.consts, 1)
                        pool.wait_ge(s.consts, 5 + t + 1)

                def values(h, r):
                    nc.gpsimd.tensor_copy(b.v[:, r, :, 0:DH], g.v[:, bass.ds(h, 1), 0:NT, :].rearrange("p o t d -> p (o t) d")).then_inc(s.v_in, 1)
                    pool.wait_ge(s.v_in, h + 1)
                for h in range(RING):
                    values(h, h)
                with pool.Fori(0, 4) as i:
                    for r in range(RING):
                        pool.wait_ge(s.pv, (i * RING + r + 1) * NT)
                        values(i * RING + r + RING, r)
                pool.wait_ge(s.pv, (NH - RING) * NT)
                values(NH - 1, (NH - 1) % RING)

            def pe_scores(h, r, kt, half):
                rows = tiles[kt][1]
                if kt == 0 and half == 0:
                    nc.tensor.wait_ge(s.m_in, (h + 1) * 16)
                if not (isinstance(h, int) and h == 0 and kt == 0):
                    nc.tensor.wait_ge(s.probs, h * (2 * NT) + (2 * kt - 1 + half))
                for c in range(2):
                    mm = nc.tensor.matmul(b.s[0:rows, half, c, :], b.k[0:ROWS, r, kt * P:kt * P + rows],
                                          b.q[0:ROWS, r, (2 * half + c) * BANK:(2 * half + c + 1) * BANK],
                                          start=True, stop=True)
                mm.then_inc(s.scores, 1)

            def pe_pv(h, r, kt):
                rows = tiles[kt][1]
                nc.tensor.wait_ge(s.probs, h * (2 * NT) + (2 * kt + 2))
                if kt == 0:
                    nc.tensor.wait_ge(s.v_in, h + 1)
                    if not (isinstance(h, int) and h == 0):
                        nc.tensor.wait_ge(s.acc_out, h)
                for j in range(4):
                    mm = nc.tensor.matmul(b.acc[32 * j:32 * j + 2 * DH, :], b.v[0:rows, r, kt, :], b.p[0:rows, kt % 2, j // 2, (j % 2) * BANK:(j % 2 + 1) * BANK],
                                          start=(kt == 0), stop=(kt == NT - 1))
                mm.then_inc(s.pv, 1)

            def pe_entry(e, n, bank):
                kind, h, u = e
                if not (isinstance(n, int) and n < RB):
                    nc.tensor.wait_ge(s.ring_out, n - (RB - 1))
                if kind == "unit":
                    t, (c0, cs) = u // CH, chunks[u % CH]
                    r = slot[0]
                    nc.tensor.matmul(b.ring[:, bank, 0:cs], b.q[0:ONEROWS, r, t * P:(t + 1) * P], b.k[0:ONEROWS, r, c0:c0 + cs],
                                     start=True, stop=True).then_inc(s.ring_in, 1)
                elif kind == "max":
                    nc.tensor.wait_ge(s.split, 5 * (h + 1))
                    nc.tensor.transpose(b.ring[:, bank, 0:P // 2].bitcast(BF16), b.mparts[:, :, :].rearrange("p i t -> p (i t)"),
                                        g.ident_b[:, :]).then_inc(s.ring_in, 1)
                else:
                    nc.tensor.wait_ge(s.acc_out, h + 1)
                    for c in range(4):
                        mm = nc.tensor.transpose(b.ring[:, bank, c * P:(c + 1) * P], b.o_t[:, c * P:(c + 1) * P], g.ident[:, :])
                    mm.then_inc(s.ring_in, 1)

            def pe_loaded(r, turn):
                nc.tensor.wait_ge(q_in[r], turn * LOAD)

            slot = [0]

            @block.tensor
            def _(pe):
                pe.wait_ge(s.consts, CONSTS)
                if mask_row is not None:
                    pe.wait_ge(s.mask_in, 16 * RING)
                pe_loaded(0, 1)
                for n in range(UNITS):
                    pe_entry(("unit", 0, n), n, n % RB)
                pe_entry(("max", 0, 0), UNITS, UNITS % RB)
                pe_loaded(1, 1)
                slot[0] = 1
                for u in range(HALF):
                    pe_entry(("unit", 1, u), UNITS + 1 + u, (UNITS + 1 + u) % RB)

                def head(h, r, turns, first=False, ahead=2):
                    n0 = first_entry(h)
                    bank0 = n0 % RB if isinstance(n0, int) else 0
                    i = 0
                    for kt in range(NT):
                        todo = entries(h, kt, ahead, first)
                        slot[0] = (r + (1 if kt < FLIP else 2)) % RING
                        if kt == FLIP and ahead == 2:
                            pe_loaded(slot[0], turns)
                        share = [1, 1, len(todo)]
                        for part in range(3):
                            if part < 2:
                                pe_scores(h, r, kt, part)
                            elif kt:
                                pe_pv(h, r, kt - 1)
                            elif not first:
                                pe_pv(h - 1, (r - 1) % RING, NT - 1)
                            for e in todo[:share[part]]:
                                pe_entry(e, n0 + i, (bank0 + i) % RB)
                                i += 1
                            todo = todo[share[part]:]

                head(0, 0, 1, first=True)
                with pe.Fori(0, 4) as i:
                    for j in range(RING):
                        head(i * RING + (j + 1), (j + 1) % RING, i + ((j + 3) // RING + 1))
                head(NH - 3, (NH - 3) % RING, (NH - 1) // RING + 1)
                head(NH - 2, (NH - 2) % RING, 0, ahead=1)
                head(NH - 1, (NH - 1) % RING, 0, ahead=0)
                pe_pv(NH - 1, (NH - 1) % RING, NT - 1)
                last = entry_of_out(NH - 1)
                pe_entry(("out", NH - 1, 0), last, last % RB)

            @block.scalar
            def _(act):
                def copy_acc(h):
                    act.wait_ge(s.pv, (h + 1) * NT)
                    if not (isinstance(h, int) and h == 0):
                        act.wait_ge(s.ring_in, entry_of_out(h - 1) + 1)
                    nc.scalar.activation(b.o_t[:, :], b.acc[:, :], ACT.Copy).then_inc(s.acc_out, 1)

                def head(h, first=False):
                    for kt in range(NT):
                        rows = tiles[kt][1]
                        for half in range(2):
                            act.wait_ge(s.scores, h * (2 * NT) + (2 * kt + half + 1))
                            if kt >= 2:
                                act.wait_ge(s.pv, h * NT + (kt - 1))
                            elif not first:
                                act.wait_ge(s.pv, h * NT - (NT + kt + 1) % 2)
                            nc.scalar.activation(b.p[0:rows, kt % 2, half, :].rearrange("p (c n) -> p c n", c=2), b.s[0:rows, half, :, :],
                                                 ACT.Exp, scale=SCALE).then_inc(s.probs, 1)
                        if kt == 0 and not first:
                            copy_acc(h - 1)

                head(0, first=True)
                with act.Fori(0, 4) as i:
                    for j in range(RING):
                        head(i * RING + (j + 1))
                head(NH - 3)
                head(NH - 2)
                head(NH - 1)
                copy_acc(NH - 1)

            @block.vector
            def _(dve):
                def unit(n, bank, u):
                    t, (c0, cs) = u // CH, chunks[u % CH]
                    nc.vector.tensor_reduce(b.mx[:, u // HALF, t, u % CH:u % CH + 1], b.ring[:, bank, 0:cs], AX.X, ALU.max).then_inc(s.ring_out, 1)

                def split_max(h):
                    dve.wait_ge(s.ring_out, entry_of_last_unit(h))
                    for w in range(2):
                        nc.vector.tensor_reduce(b.nm[:, w * TT // 2:(w + 1) * TT // 2], b.mx[:, w, w * TT // 2:(w + 1) * TT // 2, :],
                                                AX.X, ALU.max, negate=True).then_inc(s.neg_max, 1)
                    dve.wait_ge(s.neg_max, 2 * (h + 1))
                    nc.vector.tensor_copy(b.mparts[:, 0, :], b.nm[:, :]).then_inc(s.split, 1)
                    dve.wait_ge(s.split, 5 * h + 1)
                    nc.vector.tensor_tensor(b.rest[:, 0, :], b.nm[:, :], b.mparts[:, 0, :], ALU.subtract).then_inc(s.split, 1)
                    dve.wait_ge(s.split, 5 * h + 2)
                    nc.vector.tensor_copy(b.mparts[:, 1, :], b.rest[:, 0, :]).then_inc(s.split, 1)
                    dve.wait_ge(s.split, 5 * h + 3)
                    nc.vector.tensor_tensor(b.rest[:, 1, :], b.rest[:, 0, :], b.mparts[:, 1, :], ALU.subtract).then_inc(s.split, 1)
                    dve.wait_ge(s.split, 5 * h + 4)
                    nc.vector.tensor_copy(b.mparts[:, 2, :], b.rest[:, 1, :]).then_inc(s.split, 1)

                def copy_max(h, bank):
                    if not (isinstance(h, int) and h == 0):
                        dve.wait_ge(s.m_in, h * 16)
                    nc.vector.tensor_copy(b.mt[:, :], b.ring[0:3 * TT, bank, 0:P // 2].bitcast(BF16)).then_inc(s.ring_out, 1)

                def normalise(h, bank):
                    tv = b.ring[:, bank, :].rearrange("p (c j d) -> p c j d", c=4, j=4)
                    rs = b.rs[:, :].rearrange("p (c j) -> p c j", c=4)
                    nc.vector.reciprocal(rs, tv[:, :, :, DH]).then_inc(s.rsum, 1)
                    dve.wait_ge(s.rsum, h + 1)
                    o = out[:, :, bass.ds(h * DH, DH)].rearrange("p (j c) d -> p c j d", j=4)
                    nc.vector.tensor_tensor(o, tv[:, :, :, 0:DH], rs.unsqueeze(3).broadcast_to([P, 4, 4, DH]), ALU.mult).then_inc(s.ring_out, 1)

                def entry(e, n, bank):
                    kind, h, u = e
                    dve.wait_ge(s.ring_in, n + 1)
                    if kind == "unit":
                        unit(n, bank, u)
                        if u == UNITS - 1:
                            split_max(h)
                    elif kind == "max":
                        copy_max(h, bank)
                    else:
                        if not (isinstance(h, int) and h == 0):
                            dve.wait_ge(s.ring_out, entry_of_out(h - 1) + 1)
                        normalise(h, bank)

                def head(h, first=False, ahead=2):
                    n0 = first_entry(h)
                    bank0 = n0 % RB if isinstance(n0, int) else 0
                    todo = [e for kt in range(NT) for e in entries(h, kt, ahead, first)]
                    for i, e in enumerate(todo):
                        entry(e, n0 + i, (bank0 + i) % RB)

                for n in range(UNITS):
                    entry(("unit", 0, n), n, n % RB)
                entry(("max", 0, 0), UNITS, UNITS % RB)
                for u in range(HALF):
                    entry(("unit", 1, u), UNITS + 1 + u, (UNITS + 1 + u) % RB)
                head(0, first=True)
                with dve.Fori(0, 4) as i:
                    for j in range(RING):
                        head(i * RING + (j + 1))
                head(NH - 3)
                head(NH - 2, ahead=1)
                head(NH - 1, ahead=0)
                last = entry_of_out(NH - 1)
                entry(("out", NH - 1, 0), last, last % RB)



def project_add(nc, g, name, srcT, wt, bias, gate=None):
    kc = wt.shape[0] // P
    NB = 8
    with stage(nc, name, ["w_in", "ready", "done", "gated"],
               [("w", [P, kc, D], F32), ("bias", [1, D], F32)], [("ps", [P, NB, BANK], F32)]) as (s, b):
        block = nc.Block()
        with block:
            @block.sync
            def _(sp):
                sp.dma_start(b.w[:, :, :], wt.rearrange("(k p) n -> p k n", p=P)).then_inc(s.w_in, 16)
                sp.dma_start(b.bias[:, :], bias.rearrange("(o n) -> o n", o=1)).then_inc(s.w_in, 16)

            @block.vector
            def _(dve):
                if gate is not None:
                    dve.wait_ge(s.w_in, 32)
                    for k in range(kc):
                        nc.vector.tensor_tensor(b.w[:, k, :], b.w[:, k, :], gate[:, :], ALU.mult).then_inc(s.gated, 1)
                    nc.vector.tensor_tensor(b.bias[:, :], b.bias[:, :], gate[0:1, :], ALU.mult).then_inc(s.gated, 1)
                for t in range(TT):
                    dve.wait_ge(s.ready, t + 1)
                    nc.vector.tensor_tensor(g.x[:, t, :], g.x[:, t, :], b.ps[:, t % NB, 0:D], ALU.add).then_inc(s.done, 1)

            @block.tensor
            def _(pe):
                pe.wait_ge(s.w_in, 32)
                if gate is not None:
                    pe.wait_ge(s.gated, kc + 1)
                for t in range(TT):
                    if t >= NB:
                        pe.wait_ge(s.done, t - NB + 1)
                    for k in range(kc):
                        nc.tensor.matmul(b.ps[:, t % NB, 0:D], srcT[:, k, t * P:(t + 1) * P], b.w[:, k, :], start=(k == 0), stop=False)
                    nc.tensor.matmul(b.ps[:, t % NB, 0:D], g.ones[0:1, :], b.bias[0:1, :], start=False, stop=True).then_inc(s.ready, 1)



def plain_projections(nc, g, name, jobs_in, tok_x, tok_n, tok_w, tok_dst):
    blocks = [(w, m, c0, cs) for w in range(len(jobs_in)) for m in range(KC) for c0, cs in cut(jobs_in[w][1], BANK)]
    NB, NW, first_tok = 8, len(jobs_in), len(blocks)
    tiles = cut(tok_n, P)
    with stage(nc, name, ["w_in", "ready", "out_act", "out_dve"], [("w", [P, NW + 1, KC, D], F32)],
               [("ps", [P, NB, BANK], F32)]) as (s, b):
        def bank_free(eng, j):
            if j >= NB:
                eng.wait_ge(s.out_act if j % 2 else s.out_dve, (j - NB) // 2 + 1)

        def job_out(j):
            if j < first_tok:
                w, m, c0, cs = blocks[j]
                return jobs_in[w][3][:, m, c0:c0 + cs], b.ps[:, j % NB, 0:cs]
            t = j - first_tok
            return tok_dst[0:tiles[t][1], t, :], b.ps[0:tiles[t][1], j % NB, 0:D]
        total = first_tok + len(tiles)

        block = nc.Block()
        with block:
            @block.sync
            def _(sp):
                for w, wt in enumerate([jb[2] for jb in jobs_in] + [tok_w]):
                    sp.dma_start(b.w[:, w], wt.rearrange("(k p) n -> p k n", p=P)).then_inc(s.w_in, 16)

            @block.tensor
            def _(pe):
                pe.wait_ge(s.w_in, 16 * (NW + 1))
                for j, (w, m, c0, cs) in enumerate(blocks):
                    bank_free(pe, j)
                    for k in range(KC):
                        mm = nc.tensor.matmul(b.ps[:, j % NB, 0:cs], b.w[:, w, k, m * P:(m + 1) * P], jobs_in[w][0][:, k, c0:c0 + cs],
                                              start=(k == 0), stop=(k == KC - 1))
                    mm.then_inc(s.ready, 1)
                for t, (c0, r) in enumerate(tiles):
                    j = first_tok + t
                    bank_free(pe, j)
                    for k in range(KC):
                        mm = nc.tensor.matmul(b.ps[0:r, j % NB, 0:D], tok_x[:, k, c0:c0 + r], b.w[:, NW, k, :], start=(k == 0), stop=(k == KC - 1))
                    mm.then_inc(s.ready, 1)

            @block.vector
            def _(dve):
                for j in range(0, total, 2):
                    dve.wait_ge(s.ready, j + 1)
                    nc.vector.tensor_copy(*job_out(j)).then_inc(s.out_dve, 1)

            @block.scalar
            def _(act):
                for j in range(1, total, 2):
                    act.wait_ge(s.ready, j + 1)
                    nc.scalar.activation(*job_out(j), ACT.Copy).then_inc(s.out_act, 1)


def prototype_attention(nc, g, name, qT, kT, v, evT):
    tiles = cut(CTX, P)
    CH = 4
    chunks = cut(CTX, -(-CTX // CH))
    groups = cut(CT, 4)
    NG = len(groups)
    QB = BANK // P
    NBLK = TT // QB
    SCALE = float(D) ** -0.5
    with stage(nc, name, ["scores", "maxed", "neg", "bias", "exped", "summed", "recip", "normed", "turned",
                          "pt_dve", "pt_act", "ev", "ev_out"],
               [("mx", [P, 2, CH], F32), ("nm", [P, 2], F32), ("nb", [P, 2], F32), ("sm", [P, 2, CH], F32), ("rs", [P, 2, 2], F32),
                ("p", [P, 2, CTX], F32), ("pt", [P, CT, BANK], F32)],
               [("s", [P, CH, BANK], F32), ("t", [P, 2, BANK], F32), ("e", [P, 2, BANK], F32)]) as (s, b):
        def copied(eng, n):
            if n > 0:
                eng.wait_ge(s.pt_dve, (n + 1) // 2)
            if n > 1:
                eng.wait_ge(s.pt_act, n // 2)

        def copy_turned(eng, t, i):
            n = t * NG + i
            k0, m = groups[i]
            eng.wait_ge(s.turned, n + 1)
            if t % QB == 0 and t:
                eng.wait_ge(s.ev, KC * (t // QB))
            q = (t % QB) * P
            full = sum(1 for _, r in tiles[k0:k0 + m] if r == P)
            outs = []
            if full:
                outs.append((b.pt[:, k0:k0 + full, q:q + P], b.t[:, n % 2, 0:full * P].rearrange("p (k c) -> p k c", k=full)))
            if full < m:
                r = tiles[k0 + full][1]
                outs.append((b.pt[0:r, k0 + full, q:q + P], b.t[0:r, n % 2, full * P:(full + 1) * P]))
            return outs

        block = nc.Block()
        with block:
            @block.tensor
            def _(pe):
                def scores(t):
                    for c, (c0, cs) in enumerate(chunks):
                        if t:
                            pe.wait_ge(s.exped, CH * (t - 1) + c + 1)
                        for k in range(KC):
                            mm = nc.tensor.matmul(b.s[:, c, 0:cs], qT[:, k, t * P:(t + 1) * P], kT[:, k, c0:c0 + cs],
                                                  start=(k == 0), stop=(k == KC - 1))
                        mm.then_inc(s.scores, 1)

                def turn(t):
                    pe.wait_ge(s.normed, t + 1)
                    for i, (k0, m) in enumerate(groups):
                        copied(pe, t * NG + i - 1)
                        for q in range(m):
                            c0, r = tiles[k0 + q]
                            mm = nc.tensor.transpose(b.t[0:r, (t * NG + i) % 2, q * P:(q + 1) * P], b.p[:, t % 2, c0:c0 + r], g.ident[:, :])
                        mm.then_inc(s.turned, 1)

                def evidence(blk):
                    copied(pe, (blk + 1) * QB * NG)
                    for m in range(KC):
                        if blk:
                            pe.wait_ge(s.ev_out, KC * (blk - 1) + m + 1)
                        for k, (_, r) in enumerate(tiles):
                            mm = nc.tensor.matmul(b.e[:, m, :], v[0:r, k, m * P:(m + 1) * P], b.pt[0:r, k, :], start=(k == 0), stop=(k == CT - 1))
                        mm.then_inc(s.ev, 1)

                for t in range(TT):
                    scores(t)
                    if t:
                        turn(t - 1)
                    if t and t % QB == 0:
                        evidence(t // QB - 1)
                turn(TT - 1)
                evidence(NBLK - 1)

            @block.vector
            def _(dve):
                for t in range(TT + 1):
                    if t < TT:
                        i = t % 2
                        for c, (c0, cs) in enumerate(chunks):
                            dve.wait_ge(s.scores, CH * t + c + 1)
                            nc.vector.tensor_reduce(b.mx[:, i, c:c + 1], b.s[:, c, 0:cs], AX.X, ALU.max).then_inc(s.maxed, 1)
                        dve.wait_ge(s.maxed, CH * (t + 1))
                        nc.vector.tensor_reduce(b.nm[:, i:i + 1], b.mx[:, i, :], AX.X, ALU.max, negate=True).then_inc(s.neg, 1)
                        dve.wait_ge(s.neg, t + 1)
                        nc.vector.tensor_scalar(b.nb[:, i:i + 1], b.nm[:, i:i + 1], SCALE, None, ALU.mult).then_inc(s.bias, 1)
                    if t:
                        for n in range(NG):
                            if ((t - 1) * NG + n) % 2 == 0:
                                for o, src in copy_turned(dve, t - 1, n):
                                    ins = nc.vector.tensor_copy(o, src)
                                ins.then_inc(s.pt_dve, 1)
                    if t < TT:
                        dve.wait_ge(s.exped, CH * (t + 1))
                        nc.vector.tensor_reduce(b.rs[:, i, 0:1], b.sm[:, i, :], AX.X, ALU.add).then_inc(s.summed, 1)
                        dve.wait_ge(s.summed, t + 1)
                        nc.vector.reciprocal(b.rs[:, i, 1:2], b.rs[:, i, 0:1]).then_inc(s.recip, 1)
                        dve.wait_ge(s.recip, t + 1)
                        nc.vector.tensor_scalar(b.p[:, i, :], b.p[:, i, :], b.rs[:, i, 1:2], None, ALU.mult).then_inc(s.normed, 1)
                    if (t - 1) % QB == 0 and t > 1 or t == TT:
                        blk = (t - 1) // QB - 1 if t < TT else NBLK - 1
                        for m in range(KC):
                            dve.wait_ge(s.ev, KC * blk + m + 1)
                            nc.vector.tensor_copy(evT[:, m, blk * BANK:(blk + 1) * BANK], b.e[:, m, :]).then_inc(s.ev_out, 1)

            @block.scalar
            def _(act):
                for t in range(TT + 1):
                    if t:
                        for n in range(NG):
                            if ((t - 1) * NG + n) % 2 == 1:
                                for o, src in copy_turned(act, t - 1, n):
                                    ins = nc.scalar.activation(o, src, ACT.Copy)
                                ins.then_inc(s.pt_act, 1)
                    if t < TT:
                        i = t % 2
                        act.wait_ge(s.bias, t + 1)
                        if t >= 2:
                            act.wait_ge(s.turned, NG * (t - 1))
                        for c, (c0, cs) in enumerate(chunks):
                            nc.scalar.activation(b.p[:, i, c0:c0 + cs], b.s[:, c, 0:cs], ACT.Exp, bias=b.nb[:, i:i + 1], scale=SCALE,
                                                 accum_out=b.sm[:, i, c:c + 1]).then_inc(s.exped, 1)


def experts(nc, g, name, a, nxT, evT, routed, g1T):
    E, RH = 3, 512
    CK = 3 * D // P
    XK = 2 * D // P
    MC = RH // P
    NBLK = TOK // BANK
    TB = BANK // P
    comb = [nxT[:, 0], nxT[:, 1], evT[:, 0], evT[:, 1]]
    NCOL = E * MC + KC
    units = [(nb, e) for nb in range(NBLK) for e in range(E + 1)]
    rows_of = lambda e: MC if e < E else KC
    hidden = [(u, m) for u in range(len(units)) for m in range(rows_of(units[u][1]))]
    outs = [(u, q) for u in range(len(units)) if units[u][1] < E for q in range(TB)]
    HB, OB = 4, 3
    hid_end = [sum(rows_of(e) for _, e in units[:u + 1]) for u in range(len(units))]
    out_end = [TB * sum(1 for _, e in units[:u + 1] if e < E) for u in range(len(units))]
    exp_units = [u for u in range(len(units)) if units[u][1] < E]
    with stage(nc, name, ["w_in", "cols", "bias_set", "anchor_b", "logits", "dve", "exped", "hid", "act_out", "ready", "done"],
               [("w1", [P, E, CK, RH], F32), ("w2", [P, E, MC, D], F32), ("gw", [P, CK, D], F32), ("rw", [P, CK, E], F32),
                ("b1", [P, NCOL], F32), ("b2", [1, E, D], F32), ("rb", [1, E], F32), ("bias", [P, NCOL], F32),
                ("anchor", [P, KC, P], F32), ("row", [P, E], F32), ("lg", [P, TT, E], F32), ("red", [P, 3, TT], F32),
                ("prob", [P, TT, E], F32), ("h", [P, 2, MC, BANK], F32)],
               [("hp", [P, HB, BANK], F32), ("op", [P, OB, BANK], F32), ("sp", [P, BANK], F32)]) as (s, b):
        NIN = E * 2 + 2 + 4
        LG = 64
        ROW = LG + TT * E
        block = nc.Block()
        with block:
            @block.sync
            def _(sp):
                for e in range(E):
                    sp.dma_start(b.w1[:, e], a.L1_xcond_e_w1[e].rearrange("(k p) n -> p k n", p=P)).then_inc(s.w_in, 16)
                    sp.dma_start(b.w2[:, e], a.L1_xcond_e_w2[e].rearrange("(k p) n -> p k n", p=P)).then_inc(s.w_in, 16)
                sp.dma_start(b.gw[:, :, :], a.L1_xcond_gate_w1.rearrange("(k p) n -> p k n", p=P)).then_inc(s.w_in, 16)
                with nc.allow_non_contiguous_dma("short rows of biases and router weights"):
                    sp.dma_start(b.rw[:, :, :], a.L1_xcond_router_W.rearrange("(k p) n -> p k n", p=P)).then_inc(s.w_in, 16)
                    sp.dma_start(b.b1[:, 0:E * MC], a.L1_xcond_e_b1.rearrange("e (k p) -> p (e k)", p=P)).then_inc(s.w_in, 16)
                    sp.dma_start(b.b1[:, E * MC:NCOL], a.L1_xcond_gate_b1.rearrange("(k p) -> p k", p=P)).then_inc(s.w_in, 16)
                sp.dma_start(b.b2[:, :, :], a.L1_xcond_e_b2.rearrange("(o e) n -> o e n", o=1)).then_inc(s.w_in, 16)
                sp.dma_start(b.rb[:, :], a.L1_xcond_router_b.rearrange("(o n) -> o n", o=1)).then_inc(s.w_in, 16)

            @block.tensor
            def _(pe):
                pe.wait_ge(s.w_in, 16 * NIN)
                for c in range(NCOL):
                    w = b.w1[:, c // MC, :, (c % MC) * P:(c % MC + 1) * P] if c < E * MC else b.gw[:, :, (c - E * MC) * P:(c - E * MC + 1) * P]
                    for k in range(XK, CK):
                        nc.tensor.matmul(b.sp[:, c:c + 1], w[:, k, :], g.cond[:, k - XK:k - XK + 1], start=(k == XK), stop=(k == CK - 1))
                pe.wait_ge(s.anchor_b, KC)
                for k in range(XK, CK):
                    nc.tensor.matmul(b.sp[:, ROW:ROW + E], b.anchor[:, k - XK, :], b.rw[:, k, :], start=(k == XK), stop=False)
                nc.tensor.matmul(b.sp[:, ROW:ROW + E], g.ones[0:1, :], b.rb[0:1, :], start=False, stop=True)
                for t in range(TT):
                    for k in range(XK):
                        mm = nc.tensor.matmul(b.sp[:, LG + t * E:LG + (t + 1) * E], comb[k][:, t * P:(t + 1) * P], b.rw[:, k, :],
                                              start=(k == 0), stop=(k == XK - 1))
                mm.then_inc(s.logits, 1)

                n_hid = 0
                n_out = 0

                def first_layer(u, n):
                    nb, e = units[u]
                    for m in range(rows_of(e)):
                        if n >= HB:
                            pe.wait_ge(s.act_out, n - HB + 1)
                        for k in range(XK):
                            w = b.w1[:, e, k, m * P:(m + 1) * P] if e < E else b.gw[:, k, m * P:(m + 1) * P]
                            mm = nc.tensor.matmul(b.hp[:, n % HB, :], w, comb[k][:, nb * BANK:(nb + 1) * BANK], start=(k == 0), stop=(k == XK - 1))
                        mm.then_inc(s.hid, 1)
                        n += 1
                    return n

                def second_layer(u, n):
                    e = units[u][1]
                    i = exp_units.index(u) % 2
                    pe.wait_ge(s.act_out, hid_end[u])
                    for q in range(TB):
                        if n >= OB:
                            pe.wait_ge(s.done, n - OB + 1)
                        for k in range(MC):
                            nc.tensor.matmul(b.op[:, n % OB, 0:D], b.h[:, i, k, q * P:(q + 1) * P], b.w2[:, e, k, :], start=(k == 0), stop=False)
                        nc.tensor.matmul(b.op[:, n % OB, 0:D], g.ones[0:1, :], b.b2[0:1, e, :], start=False, stop=True).then_inc(s.ready, 1)
                        n += 1
                    return n

                for u in range(len(units)):
                    n_hid = first_layer(u, n_hid)
                    if u and units[u - 1][1] < E:
                        n_out = second_layer(u - 1, n_out)

            @block.scalar
            def _(act):
                act.wait_ge(s.dve, 3)
                nc.scalar.activation(b.lg[:, :, :], b.lg[:, :, :], ACT.Exp).then_inc(s.exped, 1)
                act.wait_ge(s.bias_set, 1)
                for n, (u, m) in enumerate(hidden):
                    nb, e = units[u]
                    act.wait_ge(s.hid, n + 1)
                    if e < E:
                        i = exp_units.index(u)
                        if i >= 2:
                            act.wait_ge(s.ready, out_end[exp_units[i - 2]])
                        o = b.h[:, i % 2, m, :]
                    else:
                        o = g1T[:, m, nb * BANK:(nb + 1) * BANK]
                    c = e * MC + m
                    nc.scalar.activation(o, b.hp[:, n % HB, :], ACT.Silu, bias=b.bias[:, c:c + 1]).then_inc(s.act_out, 1)

            @block.vector
            def _(dve):
                for k in range(KC):
                    nc.vector.tensor_scalar(b.anchor[:, k, :], g.ones[:, :], g.cond[:, k:k + 1], None, ALU.mult).then_inc(s.anchor_b, 1)
                dve.wait_ge(s.w_in, 16 * NIN)
                dve.wait_ge(s.logits, 1)
                nc.vector.tensor_tensor(b.bias[:, :], b.b1[:, :], b.sp[:, 0:NCOL], ALU.add).then_inc(s.bias_set, 1)
                nc.vector.tensor_copy(b.row[:, :], b.sp[:, ROW:ROW + E]).then_inc(s.cols, 1)
                dve.wait_ge(s.cols, 1)
                nc.vector.tensor_tensor(b.lg[:, :, :], b.sp[:, LG:ROW].rearrange("p (t e) -> p t e", e=E),
                                        b.row[:, :].unsqueeze(1).broadcast_to([P, TT, E]), ALU.add).then_inc(s.dve, 1)
                dve.wait_ge(s.dve, 1)
                nc.vector.tensor_reduce(b.red[:, 0, :], b.lg[:, :, :], AX.X, ALU.max).then_inc(s.dve, 1)
                dve.wait_ge(s.dve, 2)
                nc.vector.tensor_tensor(b.lg[:, :, :], b.lg[:, :, :], b.red[:, 0, :].unsqueeze(2).broadcast_to([P, TT, E]), ALU.subtract).then_inc(s.dve, 1)
                dve.wait_ge(s.exped, 1)
                nc.vector.tensor_reduce(b.red[:, 1, :], b.lg[:, :, :], AX.X, ALU.add).then_inc(s.dve, 1)
                dve.wait_ge(s.dve, 4)
                nc.vector.reciprocal(b.red[:, 2, :], b.red[:, 1, :]).then_inc(s.dve, 1)
                dve.wait_ge(s.dve, 5)
                nc.vector.tensor_tensor(b.prob[:, :, :], b.lg[:, :, :], b.red[:, 2, :].unsqueeze(2).broadcast_to([P, TT, E]), ALU.mult).then_inc(s.dve, 1)
                dve.wait_ge(s.dve, 6)
                for n, (u, q) in enumerate(outs):
                    nb, e = units[u]
                    t = nb * TB + q
                    dve.wait_ge(s.ready, n + 1)
                    src, w = b.op[:, n % OB, 0:D], b.prob[:, t, e:e + 1]
                    if e == 0:
                        nc.vector.tensor_scalar(routed[:, t, :], src, w, None, ALU.mult).then_inc(s.done, 1)
                    else:
                        dve.wait_ge(s.done, n - TB + 1)
                        nc.vector.scalar_tensor_tensor(routed[:, t, :], src, w, routed[:, t, :], ALU.mult, ALU.add).then_inc(s.done, 1)


def gated_output(nc, g, name, routedT, g1T, ow, ob, gw, gb):
    NB = 4
    with stage(nc, name, ["w_in", "ready", "gate", "prod", "done"],
               [("w", [P, 2, KC, D], F32), ("bias", [1, 2, D], F32), ("sg", [P, 2, D], F32), ("pr", [P, 2, D], F32)],
               [("o", [P, NB, BANK], F32), ("z", [P, NB, BANK], F32)]) as (s, b):
        block = nc.Block()
        with block:
            @block.sync
            def _(sp):
                for i, (w, bias) in enumerate([(ow, ob), (gw, gb)]):
                    sp.dma_start(b.w[:, i], w.rearrange("(k p) n -> p k n", p=P)).then_inc(s.w_in, 16)
                    sp.dma_start(b.bias[:, i, :], bias.rearrange("(o n) -> o n", o=1)).then_inc(s.w_in, 16)

            @block.tensor
            def _(pe):
                pe.wait_ge(s.w_in, 64)
                for t in range(TT):
                    if t >= NB:
                        pe.wait_ge(s.prod, t - NB + 1)
                    for i, (src, ps) in enumerate([(g1T, b.z), (routedT, b.o)]):
                        w = 1 - i
                        for k in range(KC):
                            nc.tensor.matmul(ps[:, t % NB, 0:D], src[:, k, t * P:(t + 1) * P], b.w[:, w, k, :], start=(k == 0), stop=False)
                        mm = nc.tensor.matmul(ps[:, t % NB, 0:D], g.ones[0:1, :], b.bias[0:1, w, :], start=False, stop=True)
                    mm.then_inc(s.ready, 1)

            @block.scalar
            def _(act):
                for t in range(TT):
                    act.wait_ge(s.ready, t + 1)
                    if t >= 2:
                        act.wait_ge(s.prod, t - 1)
                    nc.scalar.activation(b.sg[:, t % 2, :], b.z[:, t % NB, 0:D], ACT.Sigmoid).then_inc(s.gate, 1)

            @block.vector
            def _(dve):
                for t in range(TT):
                    dve.wait_ge(s.gate, t + 1)
                    if t >= 2:
                        dve.wait_ge(s.done, t - 1)
                    nc.vector.tensor_tensor(b.pr[:, t % 2, :], b.sg[:, t % 2, :], b.o[:, t % NB, 0:D], ALU.mult).then_inc(s.prod, 1)
                    dve.wait_ge(s.prod, t + 1)
                    nc.vector.tensor_tensor(g.x[:, t, :], g.x[:, t, :], b.pr[:, t % 2, :], ALU.add).then_inc(s.done, 1)


def expert_block(nc, g, a, ctxT):
    with ExitStack() as ctx:
        nxT = ctx.enter_context(tile(nc, "L1_nxT", [P, KC, TOK]))
        evT = ctx.enter_context(tile(nc, "L1_evT", [P, KC, TOK]))
        gb = ctx.enter_context(tile(nc, "L1_gb", [P, 2, KC]))
        with stage(nc, "L1gb", ["loaded"]) as (s, b):
            block = nc.Block()
            with block:
                @block.sync
                def _(sp):
                    with nc.allow_non_contiguous_dma("vectors, one word per partition"):
                        sp.dma_start(gb[:, 0], a.L1_xcond_ln_gamma.rearrange("(k p) -> p k", p=P)).then_inc(s.loaded, 16)
                        sp.dma_start(gb[:, 1], a.L1_xcond_ln_beta.rearrange("(k p) -> p k", p=P)).then_inc(s.loaded, 16)
                    sp.wait_ge(s.loaded, 32)
        norm_transpose(nc, g, "L1nx", g.x, TOK, nxT, 1e-5, gb[:, 0], gb[:, 1])
        with ExitStack() as inner:
            qT = inner.enter_context(tile(nc, "L1_qT", [P, KC, TOK]))
            kT = inner.enter_context(tile(nc, "L1_kT", [P, KC, CTX]))
            v = inner.enter_context(tile(nc, "L1_v", [P, CT, D]))
            plain_projections(nc, g, "L1qkv", [(nxT, TOK, a.L1_xcond_Wq, qT), (ctxT, CTX, a.L1_xcond_Wk, kT)], ctxT, CTX, a.L1_xcond_Wv, v)
            prototype_attention(nc, g, "L1at", qT, kT, v, evT)
        routed = ctx.enter_context(tile(nc, "L1_routed", [P, TT, D]))
        g1T = ctx.enter_context(tile(nc, "L1_g1T", [P, KC, TOK]))
        experts(nc, g, "L1ex", a, nxT, evT, routed, g1T)
        routedT = nxT
        norm_transpose(nc, g, "L1rt", routed, TOK, routedT)
        gated_output(nc, g, "L1go", routedT, g1T, a.L1_xcond_out_w, a.L1_xcond_out_b, a.L1_xcond_gate_w2, a.L1_xcond_gate_b2)



def mlp(nc, g, name, xT, w1, b1, w2, b2, gate, func):
    F = w1.shape[1]
    FC = F // P
    NBLK, TB = TOK // BANK, BANK // P
    HB = OB = 4
    with stage(nc, name, ["w_in", "hid", "act_out", "ready", "done", "gated"],
               [("w1", [P, KC, F], F32), ("w2", [P, FC, D], F32), ("b1", [P, FC], F32), ("b2", [1, D], F32), ("h", [P, 2, FC, BANK], F32)],
               [("hp", [P, HB, BANK], F32), ("op", [P, OB, BANK], F32)]) as (s, b):
        block = nc.Block()
        with block:
            @block.sync
            def _(sp):
                sp.dma_start(b.w1[:, :, :], w1.rearrange("(k p) n -> p k n", p=P)).then_inc(s.w_in, 16)
                sp.dma_start(b.w2[:, :, :], w2.rearrange("(k p) n -> p k n", p=P)).then_inc(s.w_in, 16)
                with nc.allow_non_contiguous_dma("a bias vector, one word per partition"):
                    sp.dma_start(b.b1[:, :], b1.rearrange("(k p) -> p k", p=P)).then_inc(s.w_in, 16)
                sp.dma_start(b.b2[:, :], b2.rearrange("(o n) -> o n", o=1)).then_inc(s.w_in, 16)

            @block.tensor
            def _(pe):
                pe.wait_ge(s.w_in, 64)

                def first_layer(nb):
                    for m in range(FC):
                        n = nb * FC + m
                        if n >= HB:
                            pe.wait_ge(s.act_out, n - HB + 1)
                        for k in range(KC):
                            mm = nc.tensor.matmul(b.hp[:, n % HB, :], b.w1[:, k, m * P:(m + 1) * P], xT[:, k, nb * BANK:(nb + 1) * BANK],
                                                  start=(k == 0), stop=(k == KC - 1))
                        mm.then_inc(s.hid, 1)

                def second_layer(nb):
                    pe.wait_ge(s.act_out, (nb + 1) * FC)
                    for q in range(TB):
                        t = nb * TB + q
                        if t >= OB:
                            pe.wait_ge(s.done, t - OB + 1)
                        for k in range(FC):
                            nc.tensor.matmul(b.op[:, t % OB, 0:D], b.h[:, nb % 2, k, q * P:(q + 1) * P], b.w2[:, k, :], start=(k == 0), stop=False)
                        nc.tensor.matmul(b.op[:, t % OB, 0:D], g.ones[0:1, :], b.b2[0:1, :], start=False, stop=True).then_inc(s.ready, 1)

                for nb in range(NBLK):
                    first_layer(nb)
                    if nb == 0:
                        pe.wait_ge(s.gated, FC + 1)
                    if nb:
                        second_layer(nb - 1)
                second_layer(NBLK - 1)

            @block.scalar
            def _(act):
                act.wait_ge(s.w_in, 64)
                for n in range(NBLK * FC):
                    nb, m = n // FC, n % FC
                    act.wait_ge(s.hid, n + 1)
                    if nb >= 2:
                        act.wait_ge(s.ready, (nb - 1) * TB)
                    nc.scalar.activation(b.h[:, nb % 2, m, :], b.hp[:, n % HB, :], func, bias=b.b1[:, m:m + 1]).then_inc(s.act_out, 1)

            @block.vector
            def _(dve):
                dve.wait_ge(s.w_in, 64)
                for k in range(FC):
                    nc.vector.tensor_tensor(b.w2[:, k, :], b.w2[:, k, :], gate[:, :], ALU.mult).then_inc(s.gated, 1)
                nc.vector.tensor_tensor(b.b2[:, :], b.b2[:, :], gate[0:1, :], ALU.mult).then_inc(s.gated, 1)
                for t in range(TT):
                    dve.wait_ge(s.ready, t + 1)
                    nc.vector.tensor_tensor(g.x[:, t, :], g.x[:, t, :], b.op[:, t % OB, 0:D], ALU.add).then_inc(s.done, 1)


def modulated_mlp(nc, g, name, eps, mod, w1, b1, w2, b2, gate, func):
    with tile(nc, name + "_xT", [P, KC, TOK]) as xT:
        norm_transpose(nc, g, name + "nx", g.x, TOK, xT, eps, *mod)
        mlp(nc, g, name + "ml", xT, w1, b1, w2, b2, gate, func)


def load_mask(nc, g, mask, keep, row):
    full = CTX // P
    with stage(nc, "mask", ["loaded", "cast", "done", "stored"],
               [("col", [P, CT], mybir.dt.uint8), ("row", [1, CTX], mybir.dt.uint8), ("rowb", [1, CTX], BF16)]) as (s, b):
        block = nc.Block()
        with block:
            @block.sync
            def _(sp):
                sp.wait_ge(s.cast, 1)
                with nc.allow_non_contiguous_dma("the mask, one byte per partition"):
                    sp.dma_start(b.col[:, 0:full], mask[0, 0:full * P].rearrange("(t p) -> p t", p=P)).then_inc(s.loaded, 16)
                    sp.dma_start(b.col[0:CTX - full * P, full:full + 1], mask[0, full * P:CTX].rearrange("(p o) -> p o", o=1)).then_inc(s.loaded, 16)
                sp.dma_start(b.row[:, :], mask).then_inc(s.loaded, 16)
                sp.wait_ge(s.done, 2)
                sp.dma_start(row, b.rowb[:, :]).then_inc(s.stored, 16)
                sp.wait_ge(s.stored, 16)

            @block.vector
            def _(dve):
                nc.vector.memset(b.col[:, :], 0).then_inc(s.cast, 1)
                dve.wait_ge(s.loaded, 48)
                nc.vector.tensor_scalar(keep[:, :], b.col[:, :], -1.0, 1.0, ALU.mult, ALU.add).then_inc(s.done, 1)
                nc.vector.tensor_scalar(b.rowb[:, :], b.row[:, :], MASKED, None, ALU.mult).then_inc(s.done, 1)


def store(nc, g, out):
    with stage(nc, "out", ["stored"]) as (s, b):
        block = nc.Block()
        with block:
            @block.sync
            def _(sp):
                sp.dma_start(out[0].rearrange("(t p) d -> p t d", p=P), g.x[:, :, :]).then_inc(s.stored, 16)
                sp.wait_ge(s.stored, 16)


@contextmanager
def tile(nc, name, shape, dt=F32):
    with nc.sbuf_tensor(name, shape, dt) as t:
        yield t


def attend(nc, g, name, eps, kv, n, mod_q, mod_kv, wq, bq, wk, bk, wv, bv, wp, bp, gate=None, keep=None, mask_row=None, kv_eps=None, kvT=None):
    with ExitStack() as ctx:
        proj = ctx.enter_context(ExitStack())
        xT = proj.enter_context(tile(nc, name + "_xT", [P, KC, TOK]))
        norm_transpose(nc, g, name + "nx", g.x, TOK, xT, eps, *mod_q)
        if kvT is None and kv is not None:
            kvT = proj.enter_context(tile(nc, name + "_cT", [P, KC, CTX]))
            norm_transpose(nc, g, name + "nc", kv, n, kvT, kv_eps, *mod_kv)
        if kvT is None:
            kvT = xT
        split_projections(nc, g, name + "qk", [(xT, TOK, wq, bq, g.q_scr), (kvT, n, wk, bk, g.k_scr)])
        value_projection(nc, g, name + "v", kvT, n, wv, bv, keep)
        proj.close()
        o = ctx.enter_context(tile(nc, name + "_o", [P, TT, D]))
        attention(nc, g, name + "at", n, o, keep, mask_row)
        oT = ctx.enter_context(tile(nc, name + "_oT", [P, KC, TOK]))
        norm_transpose(nc, g, name + "ot", o, TOK, oT)
        project_add(nc, g, name + "pr", oT, wp, bp, gate)


def program(nc, a, out):
    with ExitStack() as ctx:
        lasting = [("x", [P, TT, D], F32), ("ctx", [P, CT, D], F32), ("ident", [P, P], F32), ("ident_b", [P, P], BF16),
                   ("ones", [P, P], F32), ("cond", [P, KC], F32), ("mod", [P, 32], F32), ("gate", [P, 4, D], F32),
                   ("v", [P, NH, TT, DH], F32)]
        g = named([n for n, _, _ in lasting] + ["q_scr", "k_scr"],
                  [ctx.enter_context(nc.sbuf_tensor("g_" + n, shape, dt)) for n, shape, dt in lasting]
                  + [nc.dram_tensor(n, [3, D, TOK], BF16, kind="Internal").ap() for n in ("q_parts", "k_parts")])
        ctxT = ctx.enter_context(tile(nc, "ctxT", [P, KC, CTX]))
        keep = ctx.enter_context(tile(nc, "keep", [P, CT]))
        mask_row = nc.dram_tensor("mask_scores", [1, CTX], BF16, kind="Internal").ap()
        base = load_and_modulate(nc, g, a)

        def vec(block, i):
            at = base[block] + i * KC
            return g.mod[:, at:at + KC]

        attend(nc, g, "L0", 1e-5, g.ctx, CTX, (vec("L0q", 0), vec("L0q", 1)), (vec("L0kv", 0), vec("L0kv", 1)),
               a.L0_xcond_Wq, a.L0_xcond_bq, a.L0_xcond_Wkv[:, 0:D], a.L0_xcond_bkv[0:D],
               a.L0_xcond_Wkv[:, D:2 * D], a.L0_xcond_bkv[D:2 * D], a.L0_xcond_Wp, a.L0_xcond_bp, kv_eps=1e-5)
        norm_transpose(nc, g, "ctxT", g.ctx, CTX, ctxT)
        expert_block(nc, g, a, ctxT)

        attend(nc, g, "L2s", 1e-6, None, TOK, (vec("L2", 1), vec("L2", 0)), None,
               a.L2_xcond_W_qkv[:, 0:D], a.L2_xcond_b_qkv[0:D], a.L2_xcond_W_qkv[:, D:2 * D], a.L2_xcond_b_qkv[D:2 * D],
               a.L2_xcond_W_qkv[:, 2 * D:3 * D], a.L2_xcond_b_qkv[2 * D:3 * D], a.L2_xcond_W_proj, a.L2_xcond_b_proj, gate=g.gate[:, 0])
        attend(nc, g, "L2c", 1e-6, g.ctx, CTX, (), (), a.L2_xcond_W_qc, a.L2_xcond_b_qc,
               a.L2_xcond_W_kvc[:, 0:D], a.L2_xcond_b_kvc[0:D], a.L2_xcond_W_kvc[:, D:2 * D], a.L2_xcond_b_kvc[D:2 * D],
               a.L2_xcond_W_cproj, a.L2_xcond_b_cproj, kv_eps=1e-6)
        modulated_mlp(nc, g, "L2m", 1e-6, (vec("L2", 4), vec("L2", 3)), a.L2_xcond_W_mlp1, a.L2_xcond_b_mlp1,
                      a.L2_xcond_W_mlp2, a.L2_xcond_b_mlp2, g.gate[:, 1], ACT.Gelu_apprx_tanh)

        attend(nc, g, "L3s", 1e-6, None, TOK, (vec("L3", 1), vec("L3", 0)), None,
               a.L3_xcond_qkv_w[:, 0:D], a.L3_xcond_qkv_b[0:D], a.L3_xcond_qkv_w[:, D:2 * D], a.L3_xcond_qkv_b[D:2 * D],
               a.L3_xcond_qkv_w[:, 2 * D:3 * D], a.L3_xcond_qkv_b[2 * D:3 * D], a.L3_xcond_sa_proj_w, a.L3_xcond_sa_proj_b, gate=g.gate[:, 2])
        load_mask(nc, g, a.mask_BxS2_bf0, keep, mask_row)
        attend(nc, g, "L3c", 1e-6, None, CTX, (), (), a.L3_xcond_q_w, a.L3_xcond_q_b,
               a.L3_xcond_kv_w[:, 0:D], a.L3_xcond_kv_b[0:D], a.L3_xcond_kv_w[:, D:2 * D], a.L3_xcond_kv_b[D:2 * D],
               a.L3_xcond_ca_proj_w, a.L3_xcond_ca_proj_b, keep=keep, mask_row=mask_row, kvT=ctxT)
        modulated_mlp(nc, g, "L3m", 1e-6, (vec("L3", 4), vec("L3", 3)), a.L3_xcond_fc1_w, a.L3_xcond_fc1_b,
                      a.L3_xcond_fc2_w, a.L3_xcond_fc2_b, g.gate[:, 3], ACT.Gelu)
        store(nc, g, out)



def kernel(**inputs):
    import numpy as _np
    import concourse.bacc as _bacc
    from concourse import mybir as _mybir
    from concourse.bass_utils import run_bass_kernel_spmd as _run

    nc = _bacc.Bacc("TRN2", target_bir_lowering=False, num_devices=1)
    arrays, args = {}, {}
    for name, value in inputs.items():
        a = _np.ascontiguousarray(value)
        arrays[f"in_{name}"] = a
        args[name] = nc.dram_tensor(f"in_{name}", a.shape, _mybir.dt.from_np(a.dtype), kind="ExternalInput").ap()
    out = nc.dram_tensor("out_0", (1, 2048, 256), _mybir.dt.float32, kind="ExternalOutput").ap()
    program(nc, named(list(args), list(args.values())), out)
    r = _run(nc, [arrays], core_ids=[0])
    return r.results[0]["out_0"]
```

```python
from collections import namedtuple
from contextlib import ExitStack, contextmanager

import concourse.bass as bass
from concourse import mybir

ALU = mybir.AluOpType
ACT = mybir.ActivationFunctionType
AX = mybir.AxisListType
F32 = mybir.dt.float32
BF16 = mybir.dt.bfloat16

P = 128
D = 256
KC = D // P
NH = 16
DH = D // NH
TOK = 2048
TT = TOK // P
CTX = 1601
CT = -(-CTX // P)
BANK = 512
MASKED = -3.0e38


def cut(n, step):
    return [(i, min(step, n - i)) for i in range(0, n, step)]


def named(names, values):
    return namedtuple("Named", names)(*values)


RETIRED = []


def semaphores(nc, names):
    held = ExitStack()
    handles = [held.enter_context(nc.semaphore(n)) for n in names]

    def retire():
        RETIRED.append((handles, held))
    return handles, retire


@contextmanager
def stage(nc, name, sems, tiles=(), psum=()):
    with ExitStack() as ctx:
        handles, retire = semaphores(nc, [f"{name}_{n}" for n in sems])
        s = named(sems, handles)
        b = named([t[0] for t in (*tiles, *psum)],
                  [ctx.enter_context(nc.sbuf_tensor(f"{name}_{n}", shape, dt)) for n, shape, dt in tiles]
                  + [ctx.enter_context(nc.psum_tensor(f"{name}_{n}", shape, dt)) for n, shape, dt in psum])
        old = RETIRED[:]
        RETIRED.clear()
        with nc.Block() as block:
            if old:
                @block.gpsimd
                def _(pool):
                    for found, _ in old:
                        for h in found:
                            pool.sem_clear(h)
            yield s, b, block
        for _, held in old:
            held.close()
        retire()


def loads(ctx, nc, name, copies):
    (sem,), retire = semaphores(nc, [name])
    ctx.callback(retire)
    return sem, copies


def start_loads(nc, sp, group):
    sem, copies = group
    with nc.allow_non_contiguous_dma("bias vectors, one word per partition"):
        for dst, src in copies:
            sp.dma_start(dst, src).then_inc(sem, 16)


def loaded(eng, group):
    eng.wait_ge(group[0], 16 * len(group[1]))


def by_rows(w):
    return w.rearrange("(k p) n -> p k n", p=P)


def as_columns(v):
    return v.rearrange("(k p) -> p k", p=P)


def as_row(v):
    return v.rearrange("(o n) -> o n", o=1)



def tile_statistics(nc, g, dve, s, t):
    if 1 <= t <= TT:
        dve.wait_ge(s.done, t)
        nc.vector.bn_stats(g.st[:, t - 1, :], g.x[:, t - 1, :]).then_inc(s.stats, 1)
    if t >= 2:
        dve.wait_ge(s.stats, t - 1)
        nc.vector.bn_aggr(g.mv[:, t - 2, :], g.st[:, t - 2, :]).then_inc(s.aggr, 1)


def finish_statistics_dve(nc, g, dve, s, eps):
    dve.wait_ge(s.aggr, TT)
    nc.vector.tensor_scalar(g.sd[:, :], g.mv[:, :, 1], eps, None, ALU.add).then_inc(s.eps_added, 1)
    dve.wait_ge(s.std, 1)
    nc.vector.reciprocal(g.rs[:, :], g.sd[:, :]).then_inc(s.rstd, 1)


def finish_statistics_act(nc, g, act, s):
    act.wait_ge(s.eps_added, 1)
    nc.scalar.activation(g.sd[:, :], g.sd[:, :], ACT.Sqrt).then_inc(s.std, 1)


STAT_SEMS = ["stats", "aggr", "eps_added", "std", "rstd"]



def start(nc, g, a, also):
    full = CTX // P
    rest = CTX - full * P
    with stage(nc, "start", ["cond_in", "x_in", "ctx_in", "mask_set", "mask_in", "small_in", "const", "silu_done", "bcast",
                             "done", "ctx_stats", "ctx_aggr", "mask_done", "mask_out"] + STAT_SEMS,
               [("cst", [P, CT, 6], F32), ("mcol", [P, CT], mybir.dt.uint8), ("mrow", [1, CTX], mybir.dt.uint8), ("mrowb", [1, CTX], BF16)]) as (s, b, block):
        @block.sync
        def _(sp):
            with nc.allow_non_contiguous_dma("a condition vector, one word per partition"):
                sp.dma_start(g.cond[:, :], a.cond_1024.rearrange("o (k p) -> p (o k)", p=P)).then_inc(s.cond_in, 16)
            sp.dma_start(g.x[:, :, :], a.x[0].rearrange("(t p) d -> p t d", p=P)).then_inc(s.x_in, 16)
            for group in also:
                start_loads(nc, sp, group)
            sp.dma_start(g.ctx[:, 0:full, :], a.ctx_1024[0, 0:full * P].rearrange("(t p) d -> p t d", p=P)).then_inc(s.ctx_in, 16)
            sp.dma_start(g.ctx[0:rest, full, :], a.ctx_1024[0, full * P:CTX]).then_inc(s.ctx_in, 16)
            sp.wait_ge(s.mask_set, 1)
            with nc.allow_non_contiguous_dma("the mask, one byte per partition; norm vectors, one word"):
                sp.dma_start(b.mcol[:, 0:full], a.mask_BxS2_bf0[0, 0:full * P].rearrange("(t p) -> p t", p=P)).then_inc(s.mask_in, 16)
                sp.dma_start(b.mcol[0:rest, full:full + 1], a.mask_BxS2_bf0[0, full * P:CTX].rearrange("(p o) -> p o", o=1)).then_inc(s.mask_in, 16)
                sp.dma_start(g.affine[:, 0], as_columns(a.L1_xcond_ln_gamma)).then_inc(s.small_in, 16)
                sp.dma_start(g.affine[:, 1], as_columns(a.L1_xcond_ln_beta)).then_inc(s.small_in, 16)
            sp.dma_start(b.mrow[:, :], a.mask_BxS2_bf0).then_inc(s.mask_in, 16)
            sp.wait_ge(s.mask_done, 2)
            sp.dma_start(g.mask_row, b.mrowb[:, :]).then_inc(s.mask_out, 16)
            sp.wait_ge(s.mask_out, 16)
            sp.wait_ge(s.small_in, 32)

        @block.gpsimd
        def _(pool):
            nc.gpsimd.memset(g.ones[:, :], 1.0).then_inc(s.const, 1)
            nc.gpsimd.memset(g.ident[:, :], 0.0).then_inc(s.const, 1)
            pool.wait_ge(s.const, 2)
            nc.gpsimd.affine_select(out=g.ident[:, :], in_=g.ident[:, :], compare_op=ALU.not_equal, fill=1.0,
                                    base=0, pattern=[[-1, P]], channel_multiplier=1).then_inc(s.const, 1)
            pool.wait_ge(s.const, 3)
            nc.gpsimd.tensor_copy(g.ident_b[:, :], g.ident[:, :]).then_inc(s.const, 1)

        @block.scalar
        def _(act):
            act.wait_ge(s.cond_in, 16)
            nc.scalar.activation(g.silu[:, :], g.cond[:, :], ACT.Silu).then_inc(s.silu_done, 1)
            finish_statistics_act(nc, g, act, s)

        @block.vector
        def _(dve):
            nc.vector.memset(b.mcol[:, :], 0).then_inc(s.mask_set, 1)
            nc.vector.memset(g.mv_ctx[:, :, :], 1.0).then_inc(s.mask_set, 1)
            dve.wait_ge(s.silu_done, 1)
            dve.wait_ge(s.const, 1)
            for k in range(KC):
                nc.vector.tensor_scalar(g.silu_b[:, k, :], g.ones[:, :], g.silu[:, k:k + 1], None, ALU.mult).then_inc(s.bcast, 1)
            dve.wait_ge(s.x_in, 16)
            for t in range(TT):
                nc.vector.bn_stats(g.st[:, t, :], g.x[:, t, :]).then_inc(s.stats, 1)
            for t in range(TT):
                dve.wait_ge(s.stats, t + 1)
                nc.vector.bn_aggr(g.mv[:, t, :], g.st[:, t, :]).then_inc(s.aggr, 1)
            finish_statistics_dve(nc, g, dve, s, 1e-5)
            dve.wait_ge(s.ctx_in, 32)
            dve.wait_ge(s.mask_set, 2)
            rows = [r for _, r in cut(CTX, P)]
            for t, r in enumerate(rows):
                nc.vector.bn_stats(b.cst[0:r, t, :], g.ctx[0:r, t, :]).then_inc(s.ctx_stats, 1)
            for t, r in enumerate(rows):
                dve.wait_ge(s.ctx_stats, t + 1)
                nc.vector.bn_aggr(g.mv_ctx[0:r, t, :], b.cst[0:r, t, :]).then_inc(s.ctx_aggr, 1)
            dve.wait_ge(s.mask_in, 48)
            nc.vector.tensor_scalar(g.keep[:, :], b.mcol[:, :], -1.0, 1.0, ALU.mult, ALU.add).then_inc(s.mask_done, 1)
            nc.vector.tensor_scalar(b.mrowb[:, :], b.mrow[:, :], MASKED, None, ALU.mult).then_inc(s.mask_done, 1)


def modulation(nc, g, name, w, bcol, group, ncol, mod0, scales, gates=(), brow=None, gate0=0):
    with stage(nc, name, ["cols_ready", "gates_ready", "dve_done"], [],
               [("cols", [P, BANK], F32), ("gate", [P, max(1, len(gates)), BANK], F32)]) as (s, b, block):
        @block.tensor
        def _(pe):
            loaded(pe, group)
            for c in range(ncol):
                for k in range(KC):
                    mm = nc.tensor.matmul(b.cols[:, c:c + 1], w[:, k, c * P:(c + 1) * P], g.silu[:, k:k + 1],
                                          start=(k == 0), stop=(k == KC - 1))
            mm.then_inc(s.cols_ready, 1)
            for i, c in enumerate(gates):
                for k in range(KC):
                    nc.tensor.matmul(b.gate[:, i, 0:D], g.silu_b[:, k, :], w[:, k, c * P:c * P + D], start=(k == 0), stop=False)
                nc.tensor.matmul(b.gate[:, i, 0:D], g.ones[0:1, :], brow[0:1, i, :], start=False, stop=True).then_inc(s.gates_ready, 1)

        @block.vector
        def _(dve):
            loaded(dve, group)
            dve.wait_ge(s.cols_ready, 1)
            nc.vector.tensor_tensor(g.mod[:, mod0:mod0 + ncol], b.cols[:, 0:ncol], bcol[:, :], ALU.add).then_inc(s.dve_done, 1)
            dve.wait_ge(s.dve_done, 1)
            for c in scales:
                v = g.mod[:, mod0 + c:mod0 + c + KC]
                nc.vector.tensor_scalar(v, v, 1.0, None, ALU.add).then_inc(s.dve_done, 1)
            if gates:
                dve.wait_ge(s.gates_ready, len(gates))
                nc.vector.tensor_copy(g.gate[:, gate0:gate0 + len(gates), :], b.gate[:, :, 0:D]).then_inc(s.dve_done, 1)



def norm_transpose(nc, g, name, sources, also=()):
    jobs, first_row, rows = [], [], []
    for i, (src, n, dst, norm, scale, shift) in enumerate(sources):
        tiles = cut(n, P)
        first_row.append(len(rows))
        rows += [(i, t, r) for t, (_, r) in enumerate(tiles)]
        jobs += [(i, k, t0, m, sum(r for _, r in tiles[t0:t0 + m])) for t0, m in cut(len(tiles), 4) for k in range(KC)]
    NB = 8
    eps = [(i, norm) for i, (_, _, _, norm, _, _) in enumerate(sources) if norm is not None and norm[2] is not None]
    with stage(nc, name, ["eps_added", "std", "rstd", "normed", "turned", "out_dve", "out_act"],
               [("y", [P, len(rows), D], F32), ("sd", [P, CT], F32), ("rs", [P, CT], F32)],
               [("ps", [P, NB, BANK], F32)]) as (s, b, block):
        def copy(j):
            i, k, t0, m, w = jobs[j]
            _, _, dst, _, scale, shift = sources[i]
            return (dst[:, k, t0 * P:t0 * P + w], b.ps[:, j % NB, 0:w],
                    None if scale is None else scale[:, k:k + 1], None if scale is None else shift[:, k:k + 1])

        @block.sync
        def _(sp):
            for group in also:
                start_loads(nc, sp, group)

        @block.vector
        def _(dve):
            for i, (mv, _, e) in eps:
                nc.vector.tensor_scalar(b.sd[:, :], mv[:, :, 1], e, None, ALU.add).then_inc(s.eps_added, 1)
            count = 0
            for i, t, r in rows:
                src, _, _, norm, _, _ = sources[i]
                if norm is None:
                    continue
                mv, rs, e = norm
                if e is not None:
                    rs = b.rs
                    if t == 0:
                        dve.wait_ge(s.std, 1)
                        nc.vector.reciprocal(b.rs[:, :], b.sd[:, :]).then_inc(s.rstd, 1)
                        dve.wait_ge(s.rstd, 1)
                nc.vector.tensor_scalar(b.y[0:r, first_row[i] + t, :], src[0:r, t, :], mv[0:r, t, 0:1], rs[0:r, t:t + 1],
                                        ALU.subtract, ALU.mult).then_inc(s.normed, 1)
            for j in range(0, len(jobs), 2):
                o, i, scale, shift = copy(j)
                dve.wait_ge(s.turned, j + 1)
                if scale is None:
                    nc.vector.tensor_copy(o, i).then_inc(s.out_dve, 1)
                else:
                    nc.vector.tensor_scalar(o, i, scale, shift, ALU.mult, ALU.add).then_inc(s.out_dve, 1)

        @block.scalar
        def _(act):
            for _ in eps:
                act.wait_ge(s.eps_added, 1)
                nc.scalar.activation(b.sd[:, :], b.sd[:, :], ACT.Sqrt).then_inc(s.std, 1)
            for j in range(1, len(jobs), 2):
                o, i, scale, shift = copy(j)
                act.wait_ge(s.turned, j + 1)
                if scale is None:
                    nc.scalar.activation(o, i, ACT.Copy).then_inc(s.out_act, 1)
                else:
                    nc.scalar.activation(o, i, ACT.Identity, bias=shift, scale=scale).then_inc(s.out_act, 1)

        @block.tensor
        def _(pe):
            normed = 0
            for j, (i, k, t0, m, _) in enumerate(jobs):
                src, n, _, norm, _, _ = sources[i]
                if norm is not None and k == 0:
                    normed += m
                    pe.wait_ge(s.normed, normed)
                if j >= NB:
                    pe.wait_ge(s.out_act if j % 2 else s.out_dve, (j - NB) // 2 + 1)
                for q in range(m):
                    r = min(P, n - (t0 + q) * P)
                    y = src[0:r, t0 + q, k * P:(k + 1) * P] if norm is None else b.y[0:r, first_row[i] + t0 + q, k * P:(k + 1) * P]
                    mm = nc.tensor.transpose(b.ps[:, j % NB, q * P:q * P + r], y, g.ident[0:r, 0:r])
                mm.then_inc(s.turned, 1)



def split_projections(nc, g, name, jobs_in, w, bias, group, part, stored):
    NB, NW = 8, len(jobs_in)
    groups = [(j, m) for m in range(KC) for j in range(NW)]
    blocks = [(j, m, c0, cs) for j, m in groups for c0, cs in cut(jobs_in[j][1], BANK)]
    ends = [max(i for i, bl in enumerate(blocks) if bl[0:2] == gr) + 1 for gr in groups]
    with stage(nc, name, ["ready", "evac", "hi", "rest", "mid", "low"],
               [("full", [P, 2, TOK], F32), ("rest", [P, 2, TOK], F32)], [("ps", [P, NB, BANK], F32)]) as (s, b, block):
        @block.sync
        def _(sp):
            for i, (j, m) in enumerate(groups):
                _, n, scr = jobs_in[j]
                sp.wait_ge(s.mid, ends[i])
                sp.wait_ge(s.low, ends[i])
                sp.dma_start(scr[:, m * P:(m + 1) * P, 0:n].rearrange("i p n -> p i n"), part[:, i % 2, :, 0:n]).then_inc(stored[i], 16)

        @block.tensor
        def _(pe):
            loaded(pe, group)
            for i, (j, m, c0, cs) in enumerate(blocks):
                x = jobs_in[j][0]
                if i >= NB:
                    pe.wait_ge(s.hi, i - NB + 1)
                for k in range(KC):
                    mm = nc.tensor.matmul(b.ps[:, i % NB, 0:cs], w[:, j, k, m * P:(m + 1) * P], x[:, k, c0:c0 + cs],
                                          start=(k == 0), stop=(k == KC - 1))
                mm.then_inc(s.ready, 1)

        @block.scalar
        def _(act):
            def middle(i):
                j, m, c0, cs = blocks[i]
                at = groups.index((j, m)) % 2
                act.wait_ge(s.rest, i + 1)
                nc.scalar.activation(part[:, at, 1, c0:c0 + cs], b.rest[:, at, c0:c0 + cs], ACT.Copy).then_inc(s.mid, 1)

            for i, (j, m, c0, cs) in enumerate(blocks):
                gi = groups.index((j, m))
                act.wait_ge(s.ready, i + 1)
                if gi >= 2 and i == ends[gi - 1]:
                    act.wait_ge(stored[gi - 2], 16)
                    act.wait_ge(s.low, ends[gi - 2])
                col = bias[:, j, m:m + 1]
                nc.scalar.activation(b.full[:, gi % 2, c0:c0 + cs], b.ps[:, i % NB, 0:cs], ACT.Identity, bias=col).then_inc(s.evac, 1)
                nc.scalar.activation(part[:, gi % 2, 0, c0:c0 + cs], b.ps[:, i % NB, 0:cs], ACT.Identity, bias=col).then_inc(s.hi, 1)
                if i:
                    middle(i - 1)
            middle(len(blocks) - 1)

        @block.vector
        def _(dve):
            def low(i):
                j, m, c0, cs = blocks[i]
                at = groups.index((j, m)) % 2
                dve.wait_ge(s.mid, i + 1)
                nc.vector.tensor_tensor(part[:, at, 2, c0:c0 + cs], b.rest[:, at, c0:c0 + cs], part[:, at, 1, c0:c0 + cs], ALU.subtract).then_inc(s.low, 1)

            for i, (j, m, c0, cs) in enumerate(blocks):
                at = groups.index((j, m)) % 2
                dve.wait_ge(s.evac, i + 1)
                dve.wait_ge(s.hi, i + 1)
                nc.vector.tensor_tensor(b.rest[:, at, c0:c0 + cs], b.full[:, at, c0:c0 + cs], part[:, at, 0, c0:c0 + cs], ALU.subtract).then_inc(s.rest, 1)
                if i:
                    low(i - 1)
            low(len(blocks) - 1)



def attention(nc, g, name, n, out, kvT, w, vbias, group, v_all, stored, keep=None, mask_row=None, also=()):
    tiles = cut(n, P)
    NT = len(tiles)
    PARTS = 96
    MASKROW, ONEROWS = 96, 97
    ROWS = ONEROWS + 3
    RING = 3
    CH = 4
    step = -(-n // CH)
    chunks = cut(n, step)
    UNITS = TT * CH
    SCALE = float(DH) ** -0.5
    HALF = UNITS // 2
    FLIP = NT // 2

    RB = 3

    def entries(h, kt, ahead=2, first=False):
        if kt < FLIP:
            lo, hi = HALF + HALF * kt // FLIP, HALF + HALF * (kt + 1) // FLIP
            found = [("unit", 1, u) for u in range(lo, hi)]
        else:
            m = NT - FLIP
            lo, hi = HALF * (kt - FLIP) // m, HALF * (kt - FLIP + 1) // m
            found = [("unit", 2, u) for u in range(lo, hi)]
        found = [f for f in found if f[1] <= ahead]
        if kt == FLIP and ahead >= 1:
            found.append(("max", 1, 0))
        if kt == 2 and not first:
            found.insert(1 if found else 0, ("out", -1, 0))
        return [(kind, h + d, u) for kind, d, u in found]

    PER = UNITS + 2
    LEAD = UNITS + 1 + HALF

    def first_entry(h):
        if isinstance(h, int) and h == 0:
            return LEAD
        if isinstance(h, int) and h == NH - 1:
            return LEAD - 1 + PER * (NH - 2) + HALF + 2
        return PER * h + (LEAD - 1)

    assert PER % RB == 0 and (LEAD - 1) % RB == 0

    def entry_of_last_unit(h):
        if isinstance(h, int) and h == 0:
            return UNITS
        if isinstance(h, int) and h == 1:
            return LEAD + HALF
        return first_entry_inner(h - 1) + (HALF + 1)

    def first_entry_inner(h):
        return PER * h + (LEAD - 1)

    before_max = sum(len(entries(0, kt)) for kt in range(FLIP + 1)) - 1

    def entry_of_max(h):
        if isinstance(h, int) and h == 0:
            return UNITS
        if isinstance(h, int) and h == 1:
            return LEAD + before_max - 1
        if isinstance(h, int) and h == NH - 1:
            return first_entry_inner(h - 1) + HALF + 1
        return first_entry_inner(h - 1) + before_max

    out_at = len(entries(0, 0)) + len(entries(0, 1)) + 1
    def entry_of_out(h):
        if isinstance(h, int) and h == NH - 1:
            return first_entry(NH - 1) + 1
        if isinstance(h, int) and h == NH - 2:
            return first_entry(NH - 1)
        return first_entry_inner(h + 1) + out_at

    with stage(nc, name, ["q_in0", "q_in1", "q_in2", "v_in", "consts", "scores", "probs", "pv",
                          "ring_in", "ring_out", "neg_max", "split", "m_in", "acc_out", "rsum", "mask_in", "v_ready", "v_out", "v_set"],
               [("q", [P, RING, TOK], BF16), ("k", [P, RING, NT * P], BF16), ("v", [P, RING, NT, 2 * DH], F32),
                ("p", [P, 2, 2, 2 * BANK], F32), ("mx", [P, 2, TT, CH], F32), ("nm", [P, TT], F32),
                ("rest", [P, 2, TT], F32), ("mparts", [P, P // TT, TT], BF16), ("mt", [3 * TT, P], BF16),
                ("o_t", [P, BANK], F32), ("rs", [P, TT], F32)],
               [("s", [P, 2, 2, BANK], F32), ("ring", [P, RB, BANK], F32), ("acc", [P, BANK], F32)]) as (s, b, block):
        q_in = [s.q_in0, s.q_in1, s.q_in2]
        LOAD = 6 * 16
        CONSTS = 5 + (NT if keep is not None else 0)

        def load_head(sp, h, r):
            qs = g.q_scr[:, bass.ds(h * DH, DH), :]
            ks = g.k_scr[:, bass.ds(h * DH, DH), 0:n]
            sp.dma_start(b.q[0:48, r, :], qs[0:1].broadcast_to([3, DH, TOK])).then_inc(q_in[r], 16)
            sp.dma_start(b.q[48:80, r, :], qs[1:2].broadcast_to([2, DH, TOK])).then_inc(q_in[r], 16)
            sp.dma_start(b.q[80:96, r, :], qs[2:3]).then_inc(q_in[r], 16)
            sp.dma_start(b.k[0:48, r, 0:n], ks).then_inc(q_in[r], 16)
            sp.dma_start(b.k[48:80, r, 0:n], ks[0:2]).then_inc(q_in[r], 16)
            sp.dma_start(b.k[80:96, r, 0:n], ks[0:1]).then_inc(q_in[r], 16)

        def max_rows(sp, h, r):
            sp.wait_ge(s.ring_out, entry_of_max(h) + 1)
            sp.dma_start(b.q[ONEROWS:ROWS, r, :].rearrange("i (t c) -> i t c", t=TT), b.mt[:, :]).then_inc(s.m_in, 16)

        @block.sync
        def _(sp):
            sp.wait_ge(s.consts, 4)
            if mask_row is not None:
                for r in range(RING):
                    sp.dma_start(b.k[MASKROW:MASKROW + 1, r, 0:n], mask_row).then_inc(s.mask_in, 16)
            for sem in stored[0:2]:
                sp.wait_ge(sem, 16)
            for h in range(RING):
                load_head(sp, h, h)
            for sem in stored[2:4]:
                sp.wait_ge(sem, 16)
            for group in also:
                start_loads(nc, sp, group)
            max_rows(sp, 0, 0)
            def body(h, r):
                max_rows(sp, h + 1, (r + 1) % RING)
                sp.wait_ge(s.pv, NT * (h + 1))
                load_head(sp, h + RING, r)
            with sp.Fori(0, 4) as i:
                for r in range(RING):
                    body(i * RING + r, r)
            body(NH - 4, (NH - 4) % RING)
            for h in range(NH - 3, NH - 1):
                max_rows(sp, h + 1, (h + 1) % RING)
            sp.wait_ge(s.m_in, 16 * NH)

        @block.gpsimd
        def _(pool):
            if n % P:
                nc.gpsimd.memset(v_all[:, :, NT - 1, :], 0.0).then_inc(s.v_set, 1)
                pool.wait_ge(s.v_set, 1)
            nc.gpsimd.memset(b.q[PARTS:ROWS, :, :], 1.0).then_inc(s.consts, 1)
            pool.wait_ge(s.consts, 1)
            nc.gpsimd.memset(b.k[PARTS:ROWS, :, :], 1.0).then_inc(s.consts, 1)
            pool.wait_ge(s.consts, 2)
            nc.gpsimd.memset(b.k[MASKROW:MASKROW + 1, :, :], 0.0).then_inc(s.consts, 1)
            pool.wait_ge(s.consts, 3)
            nc.gpsimd.memset(b.mparts[:, 3:, :], 0.0).then_inc(s.consts, 1)
            pool.wait_ge(s.consts, 4)
            nc.gpsimd.memset(b.v[:, :, :, DH:2 * DH], 1.0).then_inc(s.consts, 1)
            pool.wait_ge(s.consts, 5)
            if keep is not None:
                for t, (_, rows) in enumerate(tiles):
                    nc.gpsimd.tensor_scalar(b.v[0:rows, :, t, DH:2 * DH], b.v[0:rows, :, t, DH:2 * DH],
                                            keep[0:rows, t:t + 1], None, ALU.mult).then_inc(s.consts, 1)
                    pool.wait_ge(s.consts, 5 + t + 1)

            def values(h, r):
                nc.gpsimd.tensor_copy(b.v[:, r, :, 0:DH], v_all[:, bass.ds(h, 1), 0:NT, :].rearrange("p o t d -> p (o t) d")).then_inc(s.v_in, 1)
                pool.wait_ge(s.v_in, h + 1)
            pool.wait_ge(s.v_out, NT)
            for h in range(RING):
                values(h, h)
            with pool.Fori(0, 4) as i:
                for r in range(RING):
                    pool.wait_ge(s.pv, (i * RING + r + 1) * NT)
                    values(i * RING + r + RING, r)
            pool.wait_ge(s.pv, (NH - RING) * NT)
            values(NH - 1, (NH - 1) % RING)

        def pe_scores(h, r, kt, half):
            rows = tiles[kt][1]
            if kt == 0 and half == 0:
                nc.tensor.wait_ge(s.m_in, (h + 1) * 16)
                if isinstance(h, int) and h == 0:
                    nc.tensor.wait_ge(s.v_out, NT)
            if not (isinstance(h, int) and h == 0 and kt == 0):
                nc.tensor.wait_ge(s.probs, h * (2 * NT) + (2 * kt - 1 + half))
            for c in range(2):
                mm = nc.tensor.matmul(b.s[0:rows, half, c, :], b.k[0:ROWS, r, kt * P:kt * P + rows],
                                      b.q[0:ROWS, r, (2 * half + c) * BANK:(2 * half + c + 1) * BANK],
                                      start=True, stop=True)
            mm.then_inc(s.scores, 1)

        def pe_pv(h, r, kt):
            rows = tiles[kt][1]
            nc.tensor.wait_ge(s.probs, h * (2 * NT) + (2 * kt + 2))
            if kt == 0:
                nc.tensor.wait_ge(s.v_in, h + 1)
                if not (isinstance(h, int) and h == 0):
                    nc.tensor.wait_ge(s.acc_out, h)
            for j in range(4):
                mm = nc.tensor.matmul(b.acc[32 * j:32 * j + 2 * DH, :], b.v[0:rows, r, kt, :], b.p[0:rows, kt % 2, j // 2, (j % 2) * BANK:(j % 2 + 1) * BANK],
                                      start=(kt == 0), stop=(kt == NT - 1))
            mm.then_inc(s.pv, 1)

        def pe_entry(e, n, bank):
            kind, h, u = e
            if not (isinstance(n, int) and n < RB):
                nc.tensor.wait_ge(s.ring_out, n - (RB - 1))
            if kind == "unit":
                t, (c0, cs) = u // CH, chunks[u % CH]
                r = slot[0]
                nc.tensor.matmul(b.ring[:, bank, 0:cs], b.q[0:ONEROWS, r, t * P:(t + 1) * P], b.k[0:ONEROWS, r, c0:c0 + cs],
                                 start=True, stop=True).then_inc(s.ring_in, 1)
            elif kind == "max":
                nc.tensor.wait_ge(s.split, 5 * (h + 1))
                nc.tensor.transpose(b.ring[:, bank, 0:P // 2].bitcast(BF16), b.mparts[:, :, :].rearrange("p i t -> p (i t)"),
                                    g.ident_b[:, :]).then_inc(s.ring_in, 1)
            else:
                nc.tensor.wait_ge(s.acc_out, h + 1)
                for c in range(4):
                    mm = nc.tensor.transpose(b.ring[:, bank, c * P:(c + 1) * P], b.o_t[:, c * P:(c + 1) * P], g.ident[:, :])
                mm.then_inc(s.ring_in, 1)

        def pe_loaded(r, turn):
            nc.tensor.wait_ge(q_in[r], turn * LOAD)

        slot = [0]

        @block.tensor
        def _(pe):
            pe.wait_ge(s.consts, CONSTS)
            if mask_row is not None:
                pe.wait_ge(s.mask_in, 16 * RING)
            loaded(pe, group)

            def project_values(t):
                c0, rows = tiles[t]
                o = b.s[0:rows, (t // 2) % 2, t % 2, 0:D]
                if t >= 4:
                    pe.wait_ge(s.v_out, t - 3)
                for k in range(KC):
                    nc.tensor.matmul(o, kvT[:, k, c0:c0 + rows], w[:, k, :], start=(k == 0), stop=False)
                nc.tensor.matmul(o, g.ones[0:1, 0:rows], vbias[0:1, :], start=False, stop=True).then_inc(s.v_ready, 1)

            EARLY = 4
            for t in range(EARLY):
                project_values(t)
            pe_loaded(0, 1)
            for u in range(UNITS):
                pe_entry(("unit", 0, u), u, u % RB)
                if u % 4 == 3 and EARLY + u // 4 < NT:
                    project_values(EARLY + u // 4)
            pe_entry(("max", 0, 0), UNITS, UNITS % RB)
            pe_loaded(1, 1)
            slot[0] = 1
            for u in range(HALF):
                pe_entry(("unit", 1, u), UNITS + 1 + u, (UNITS + 1 + u) % RB)

            def head(h, r, turns, first=False, ahead=2):
                n0 = first_entry(h)
                bank0 = n0 % RB if isinstance(n0, int) else 0
                i = 0
                for kt in range(NT):
                    todo = entries(h, kt, ahead, first)
                    slot[0] = (r + (1 if kt < FLIP else 2)) % RING
                    if kt == FLIP and ahead == 2:
                        pe_loaded(slot[0], turns)
                    share = [1, 1, len(todo)]
                    for part in range(3):
                        if part < 2:
                            pe_scores(h, r, kt, part)
                        elif kt:
                            pe_pv(h, r, kt - 1)
                        elif not first:
                            pe_pv(h - 1, (r - 1) % RING, NT - 1)
                        for e in todo[:share[part]]:
                            pe_entry(e, n0 + i, (bank0 + i) % RB)
                            i += 1
                        todo = todo[share[part]:]

            head(0, 0, 1, first=True)
            with pe.Fori(0, 4) as i:
                for j in range(RING):
                    head(i * RING + (j + 1), (j + 1) % RING, i + ((j + 3) // RING + 1))
            head(NH - 3, (NH - 3) % RING, (NH - 1) // RING + 1)
            head(NH - 2, (NH - 2) % RING, 0, ahead=1)
            head(NH - 1, (NH - 1) % RING, 0, ahead=0)
            pe_pv(NH - 1, (NH - 1) % RING, NT - 1)
            last = entry_of_out(NH - 1)
            pe_entry(("out", NH - 1, 0), last, last % RB)

        @block.scalar
        def _(act):
            def copy_acc(h):
                act.wait_ge(s.pv, (h + 1) * NT)
                if not (isinstance(h, int) and h == 0):
                    act.wait_ge(s.ring_in, entry_of_out(h - 1) + 1)
                nc.scalar.activation(b.o_t[:, :], b.acc[:, :], ACT.Copy).then_inc(s.acc_out, 1)

            def head(h, first=False):
                for kt in range(NT):
                    rows = tiles[kt][1]
                    for half in range(2):
                        act.wait_ge(s.scores, h * (2 * NT) + (2 * kt + half + 1))
                        if kt >= 2:
                            act.wait_ge(s.pv, h * NT + (kt - 1))
                        elif not first:
                            act.wait_ge(s.pv, h * NT - (NT + kt + 1) % 2)
                        nc.scalar.activation(b.p[0:rows, kt % 2, half, :].rearrange("p (c n) -> p c n", c=2), b.s[0:rows, half, :, :],
                                             ACT.Exp, scale=SCALE).then_inc(s.probs, 1)
                    if kt == 0 and not first:
                        copy_acc(h - 1)

            if n % P:
                act.wait_ge(s.v_set, 1)
            for t, (_, rows) in enumerate(tiles):
                act.wait_ge(s.v_ready, t + 1)
                o = v_all[0:rows, :, t, :]
                ps = b.s[0:rows, (t // 2) % 2, t % 2, 0:D].rearrange("p (h d) -> p h d", h=NH)
                if keep is None:
                    nc.scalar.activation(o, ps, ACT.Copy).then_inc(s.v_out, 1)
                else:
                    nc.scalar.activation(o, ps, ACT.Identity, scale=keep[0:rows, t:t + 1]).then_inc(s.v_out, 1)
            head(0, first=True)
            with act.Fori(0, 4) as i:
                for j in range(RING):
                    head(i * RING + (j + 1))
            head(NH - 3)
            head(NH - 2)
            head(NH - 1)
            copy_acc(NH - 1)

        @block.vector
        def _(dve):
            def unit(n, bank, u):
                t, (c0, cs) = u // CH, chunks[u % CH]
                nc.vector.tensor_reduce(b.mx[:, u // HALF, t, u % CH:u % CH + 1], b.ring[:, bank, 0:cs], AX.X, ALU.max).then_inc(s.ring_out, 1)

            def split_max(h):
                dve.wait_ge(s.ring_out, entry_of_last_unit(h))
                for w in range(2):
                    nc.vector.tensor_reduce(b.nm[:, w * TT // 2:(w + 1) * TT // 2], b.mx[:, w, w * TT // 2:(w + 1) * TT // 2, :],
                                            AX.X, ALU.max, negate=True).then_inc(s.neg_max, 1)
                dve.wait_ge(s.neg_max, 2 * (h + 1))
                nc.vector.tensor_copy(b.mparts[:, 0, :], b.nm[:, :]).then_inc(s.split, 1)
                dve.wait_ge(s.split, 5 * h + 1)
                nc.vector.tensor_tensor(b.rest[:, 0, :], b.nm[:, :], b.mparts[:, 0, :], ALU.subtract).then_inc(s.split, 1)
                dve.wait_ge(s.split, 5 * h + 2)
                nc.vector.tensor_copy(b.mparts[:, 1, :], b.rest[:, 0, :]).then_inc(s.split, 1)
                dve.wait_ge(s.split, 5 * h + 3)
                nc.vector.tensor_tensor(b.rest[:, 1, :], b.rest[:, 0, :], b.mparts[:, 1, :], ALU.subtract).then_inc(s.split, 1)
                dve.wait_ge(s.split, 5 * h + 4)
                nc.vector.tensor_copy(b.mparts[:, 2, :], b.rest[:, 1, :]).then_inc(s.split, 1)

            def copy_max(h, bank):
                if not (isinstance(h, int) and h == 0):
                    dve.wait_ge(s.m_in, h * 16)
                nc.vector.tensor_copy(b.mt[:, :], b.ring[0:3 * TT, bank, 0:P // 2].bitcast(BF16)).then_inc(s.ring_out, 1)

            def normalise(h, bank):
                tv = b.ring[:, bank, :].rearrange("p (c j d) -> p c j d", c=4, j=4)
                rs = b.rs[:, :].rearrange("p (c j) -> p c j", c=4)
                nc.vector.reciprocal(rs, tv[:, :, :, DH]).then_inc(s.rsum, 1)
                dve.wait_ge(s.rsum, h + 1)
                o = out[:, :, bass.ds(h * DH, DH)].rearrange("p (j c) d -> p c j d", j=4)
                nc.vector.tensor_tensor(o, tv[:, :, :, 0:DH], rs.unsqueeze(3).broadcast_to([P, 4, 4, DH]), ALU.mult).then_inc(s.ring_out, 1)

            def entry(e, n, bank):
                kind, h, u = e
                dve.wait_ge(s.ring_in, n + 1)
                if kind == "unit":
                    unit(n, bank, u)
                    if u == UNITS - 1:
                        split_max(h)
                elif kind == "max":
                    copy_max(h, bank)
                else:
                    if not (isinstance(h, int) and h == 0):
                        dve.wait_ge(s.ring_out, entry_of_out(h - 1) + 1)
                    normalise(h, bank)

            def head(h, first=False, ahead=2):
                n0 = first_entry(h)
                bank0 = n0 % RB if isinstance(n0, int) else 0
                todo = [e for kt in range(NT) for e in entries(h, kt, ahead, first)]
                for i, e in enumerate(todo):
                    entry(e, n0 + i, (bank0 + i) % RB)

            for n in range(UNITS):
                entry(("unit", 0, n), n, n % RB)
            entry(("max", 0, 0), UNITS, UNITS % RB)
            for u in range(HALF):
                entry(("unit", 1, u), UNITS + 1 + u, (UNITS + 1 + u) % RB)
            head(0, first=True)
            with dve.Fori(0, 4) as i:
                for j in range(RING):
                    head(i * RING + (j + 1))
            head(NH - 3)
            head(NH - 2, ahead=1)
            head(NH - 1, ahead=0)
            last = entry_of_out(NH - 1)
            entry(("out", NH - 1, 0), last, last % RB)



def project_heads(nc, g, name, src, w, biasb, group, next_eps, gate=None, also=()):
    NB, TB = 4, 4
    jobs = [(q, k) for q in range(TT // 4) for k in range(KC)]
    with stage(nc, name, ["turned", "out_dve", "out_act", "ready", "gated", "biased", "done"] + STAT_SEMS,
               [("t", [P, KC, TOK], F32)], [("ps", [P, NB, BANK], F32), ("tp", [P, TB, BANK], F32)]) as (s, b, block):
        @block.sync
        def _(sp):
            for other in also:
                start_loads(nc, sp, other)

        @block.vector
        def _(dve):
            loaded(dve, group)
            if gate is not None:
                for k in range(KC):
                    nc.vector.tensor_tensor(w[:, k, :], w[:, k, :], gate[:, :], ALU.mult).then_inc(s.gated, 1)
                nc.vector.tensor_tensor(biasb[:, :], biasb[:, :], gate[:, :], ALU.mult).then_inc(s.gated, 1)
                dve.wait_ge(s.gated, KC + 1)
            for j in range(0, len(jobs), 2):
                q, k = jobs[j]
                dve.wait_ge(s.turned, j + 1)
                nc.vector.tensor_copy(b.t[:, k, q * BANK:(q + 1) * BANK], b.tp[:, j % TB, :]).then_inc(s.out_dve, 1)
            nc.vector.tensor_tensor(g.x[:, :, :], g.x[:, :, :], biasb[:, :].unsqueeze(1).broadcast_to([P, TT, D]), ALU.add).then_inc(s.biased, 1)
            dve.wait_ge(s.biased, 1)
            for t in range(TT + 2):
                if t < TT:
                    dve.wait_ge(s.ready, t + 1)
                    nc.vector.tensor_tensor(g.x[:, t, :], g.x[:, t, :], b.ps[:, t % NB, 0:D], ALU.add).then_inc(s.done, 1)
                tile_statistics(nc, g, dve, s, t)
            finish_statistics_dve(nc, g, dve, s, next_eps)

        @block.scalar
        def _(act):
            for j in range(1, len(jobs), 2):
                q, k = jobs[j]
                act.wait_ge(s.turned, j + 1)
                nc.scalar.activation(b.t[:, k, q * BANK:(q + 1) * BANK], b.tp[:, j % TB, :], ACT.Copy).then_inc(s.out_act, 1)
            finish_statistics_act(nc, g, act, s)

        @block.tensor
        def _(pe):
            loaded(pe, group)

            def turn(j):
                q, k = jobs[j]
                if j >= TB:
                    pe.wait_ge(s.out_act if j % 2 else s.out_dve, (j - TB) // 2 + 1)
                for t in range(4):
                    mm = nc.tensor.transpose(b.tp[:, j % TB, t * P:(t + 1) * P], src[:, 4 * q + t, k * P:(k + 1) * P], g.ident[:, :])
                mm.then_inc(s.turned, 1)

            for j in range(len(jobs)):
                turn(j)
            if gate is not None:
                pe.wait_ge(s.gated, KC + 1)
            for t in range(TT):
                pe.wait_ge(s.out_dve, t // 4 + 1)
                pe.wait_ge(s.out_act, t // 4 + 1)
                if t >= NB:
                    pe.wait_ge(s.done, t - NB + 1)
                for k in range(KC):
                    mm = nc.tensor.matmul(b.ps[:, t % NB, 0:D], b.t[:, k, t * P:(t + 1) * P], w[:, k, :], start=(k == 0), stop=(k == KC - 1))
                mm.then_inc(s.ready, 1)



def plain_projections(nc, g, name, jobs_in, tok_x, tok_n, tok_dst, w_all, group):
    blocks = [(w, m, c0, cs) for w in range(len(jobs_in)) for m in range(KC) for c0, cs in cut(jobs_in[w][1], BANK)]
    NB, NW, first_tok = 8, len(jobs_in), len(blocks)
    tiles = cut(tok_n, P)
    with stage(nc, name, ["ready", "out_act", "out_dve"], [],
               [("ps", [P, NB, BANK], F32)]) as (s, b, block):
        def bank_free(eng, j):
            if j >= NB:
                eng.wait_ge(s.out_act if j % 2 else s.out_dve, (j - NB) // 2 + 1)

        def job_out(j):
            if j < first_tok:
                w, m, c0, cs = blocks[j]
                return jobs_in[w][2][:, m, c0:c0 + cs], b.ps[:, j % NB, 0:cs]
            t = j - first_tok
            return tok_dst[0:tiles[t][1], t, :], b.ps[0:tiles[t][1], j % NB, 0:D]
        total = first_tok + len(tiles)

        @block.tensor
        def _(pe):
            loaded(pe, group)
            for j, (w, m, c0, cs) in enumerate(blocks):
                bank_free(pe, j)
                for k in range(KC):
                    mm = nc.tensor.matmul(b.ps[:, j % NB, 0:cs], w_all[:, w, k, m * P:(m + 1) * P], jobs_in[w][0][:, k, c0:c0 + cs],
                                          start=(k == 0), stop=(k == KC - 1))
                mm.then_inc(s.ready, 1)
            for t, (c0, r) in enumerate(tiles):
                j = first_tok + t
                bank_free(pe, j)
                for k in range(KC):
                    mm = nc.tensor.matmul(b.ps[0:r, j % NB, 0:D], tok_x[:, k, c0:c0 + r], w_all[:, NW, k, :], start=(k == 0), stop=(k == KC - 1))
                mm.then_inc(s.ready, 1)

        @block.vector
        def _(dve):
            for j in range(0, total, 2):
                dve.wait_ge(s.ready, j + 1)
                nc.vector.tensor_copy(*job_out(j)).then_inc(s.out_dve, 1)

        @block.scalar
        def _(act):
            for j in range(1, total, 2):
                act.wait_ge(s.ready, j + 1)
                nc.scalar.activation(*job_out(j), ACT.Copy).then_inc(s.out_act, 1)


def prototype_attention(nc, g, name, qT, kT, v, evT, also=()):
    tiles = cut(CTX, P)
    CH = 4
    chunks = cut(CTX, -(-CTX // CH))
    groups = cut(CT, 4)
    NG = len(groups)
    QB = BANK // P
    NBLK = TT // QB
    SCALE = float(D) ** -0.5
    with stage(nc, name, ["scores", "maxed", "neg", "bias", "exped", "summed", "recip", "normed", "turned",
                          "pt_dve", "pt_act", "ev", "ev_out"],
               [("mx", [P, 2, CH], F32), ("nm", [P, 2], F32), ("nb", [P, 2], F32), ("sm", [P, 2, CH], F32), ("rs", [P, 2, 2], F32),
                ("p", [P, 2, CTX], F32), ("pt", [P, CT, BANK], F32)],
               [("s", [P, CH, BANK], F32), ("t", [P, 2, BANK], F32), ("e", [P, 2, BANK], F32)]) as (s, b, block):
        def copied(eng, n):
            if n > 0:
                eng.wait_ge(s.pt_dve, (n + 1) // 2)
            if n > 1:
                eng.wait_ge(s.pt_act, n // 2)

        def copy_turned(eng, t, i):
            n = t * NG + i
            k0, m = groups[i]
            eng.wait_ge(s.turned, n + 1)
            if t % QB == 0 and t:
                eng.wait_ge(s.ev, KC * (t // QB))
            q = (t % QB) * P
            full = sum(1 for _, r in tiles[k0:k0 + m] if r == P)
            outs = []
            if full:
                outs.append((b.pt[:, k0:k0 + full, q:q + P], b.t[:, n % 2, 0:full * P].rearrange("p (k c) -> p k c", k=full)))
            if full < m:
                r = tiles[k0 + full][1]
                outs.append((b.pt[0:r, k0 + full, q:q + P], b.t[0:r, n % 2, full * P:(full + 1) * P]))
            return outs

        @block.sync
        def _(sp):
            for group in also:
                start_loads(nc, sp, group)

        @block.tensor
        def _(pe):
            def scores(t):
                for c, (c0, cs) in enumerate(chunks):
                    if t:
                        pe.wait_ge(s.exped, CH * (t - 1) + c + 1)
                    for k in range(KC):
                        mm = nc.tensor.matmul(b.s[:, c, 0:cs], qT[:, k, t * P:(t + 1) * P], kT[:, k, c0:c0 + cs],
                                              start=(k == 0), stop=(k == KC - 1))
                    mm.then_inc(s.scores, 1)

            def turn(t):
                pe.wait_ge(s.normed, t + 1)
                for i, (k0, m) in enumerate(groups):
                    copied(pe, t * NG + i - 1)
                    for q in range(m):
                        c0, r = tiles[k0 + q]
                        mm = nc.tensor.transpose(b.t[0:r, (t * NG + i) % 2, q * P:(q + 1) * P], b.p[:, t % 2, c0:c0 + r], g.ident[:, :])
                    mm.then_inc(s.turned, 1)

            def evidence(blk):
                copied(pe, (blk + 1) * QB * NG)
                for m in range(KC):
                    if blk:
                        pe.wait_ge(s.ev_out, KC * (blk - 1) + m + 1)
                    for k, (_, r) in enumerate(tiles):
                        mm = nc.tensor.matmul(b.e[:, m, :], v[0:r, k, m * P:(m + 1) * P], b.pt[0:r, k, :], start=(k == 0), stop=(k == CT - 1))
                    mm.then_inc(s.ev, 1)

            for t in range(TT):
                scores(t)
                if t:
                    turn(t - 1)
                if t and t % QB == 0:
                    evidence(t // QB - 1)
            turn(TT - 1)
            evidence(NBLK - 1)

        @block.vector
        def _(dve):
            for t in range(TT + 1):
                if t < TT:
                    i = t % 2
                    for c, (c0, cs) in enumerate(chunks):
                        dve.wait_ge(s.scores, CH * t + c + 1)
                        nc.vector.tensor_reduce(b.mx[:, i, c:c + 1], b.s[:, c, 0:cs], AX.X, ALU.max).then_inc(s.maxed, 1)
                    dve.wait_ge(s.maxed, CH * (t + 1))
                    nc.vector.tensor_reduce(b.nm[:, i:i + 1], b.mx[:, i, :], AX.X, ALU.max, negate=True).then_inc(s.neg, 1)
                    dve.wait_ge(s.neg, t + 1)
                    nc.vector.tensor_scalar(b.nb[:, i:i + 1], b.nm[:, i:i + 1], SCALE, None, ALU.mult).then_inc(s.bias, 1)
                if t:
                    for n in range(NG):
                        if ((t - 1) * NG + n) % 2 == 0:
                            for o, src in copy_turned(dve, t - 1, n):
                                ins = nc.vector.tensor_copy(o, src)
                            ins.then_inc(s.pt_dve, 1)
                if t < TT:
                    dve.wait_ge(s.exped, CH * (t + 1))
                    nc.vector.tensor_reduce(b.rs[:, i, 0:1], b.sm[:, i, :], AX.X, ALU.add).then_inc(s.summed, 1)
                    dve.wait_ge(s.summed, t + 1)
                    nc.vector.reciprocal(b.rs[:, i, 1:2], b.rs[:, i, 0:1]).then_inc(s.recip, 1)
                    dve.wait_ge(s.recip, t + 1)
                    nc.vector.tensor_scalar(b.p[:, i, :], b.p[:, i, :], b.rs[:, i, 1:2], None, ALU.mult).then_inc(s.normed, 1)
                if (t - 1) % QB == 0 and t > 1 or t == TT:
                    blk = (t - 1) // QB - 1 if t < TT else NBLK - 1
                    for m in range(KC):
                        dve.wait_ge(s.ev, KC * blk + m + 1)
                        nc.vector.tensor_copy(evT[:, m, blk * BANK:(blk + 1) * BANK], b.e[:, m, :]).then_inc(s.ev_out, 1)

        @block.scalar
        def _(act):
            for t in range(TT + 1):
                if t:
                    for n in range(NG):
                        if ((t - 1) * NG + n) % 2 == 1:
                            for o, src in copy_turned(act, t - 1, n):
                                ins = nc.scalar.activation(o, src, ACT.Copy)
                            ins.then_inc(s.pt_act, 1)
                if t < TT:
                    i = t % 2
                    act.wait_ge(s.bias, t + 1)
                    if t >= 2:
                        act.wait_ge(s.turned, NG * (t - 1))
                    for c, (c0, cs) in enumerate(chunks):
                        nc.scalar.activation(b.p[:, i, c0:c0 + cs], b.s[:, c, 0:cs], ACT.Exp, bias=b.nb[:, i:i + 1], scale=SCALE,
                                             accum_out=b.sm[:, i, c:c + 1]).then_inc(s.exped, 1)


def experts(nc, g, name, nxT, evT, routed, g1T, w1, w2, gw, rw, b1, b2, rb, early, w2_in, late, also):
    E, RH = 3, 512
    CK = 3 * D // P
    XK = 2 * D // P
    MC = RH // P
    NBLK = TOK // BANK
    TB = BANK // P
    comb = [nxT[:, 0], nxT[:, 1], evT[:, 0], evT[:, 1]]
    NCOL = E * MC + KC
    units = [(nb, e) for nb in range(NBLK) for e in range(E + 1)]
    rows_of = lambda e: MC if e < E else KC
    hidden = [(u, m) for u in range(len(units)) for m in range(rows_of(units[u][1]))]
    outs = [(u, q) for u in range(len(units)) if units[u][1] < E for q in range(TB)]
    HB, OB = 3, 3
    hid_end = [sum(rows_of(e) for _, e in units[:u + 1]) for u in range(len(units))]
    out_end = [TB * sum(1 for _, e in units[:u + 1] if e < E) for u in range(len(units))]
    exp_units = [u for u in range(len(units)) if units[u][1] < E]
    with stage(nc, name, ["cols", "bias_set", "init", "row_set", "anchor_b", "logits", "dve", "exped", "hid", "act_out", "ready", "done"],
               [("bias", [P, NCOL], F32), ("anchor", [P, KC, P], F32), ("row", [P, E], F32), ("lg", [P, TT, E], F32), ("red", [P, 3, TT], F32),
                ("prob", [P, TT, E], F32), ("h", [P, 2, MC, BANK], F32)],
               [("hp", [P, HB, BANK], F32), ("op", [P, OB, BANK], F32), ("sp", [P, BANK], F32), ("cp", [P, BANK], F32)]) as (s, b, block):
        LG = 64
        ROW = LG + TT * E
        @block.sync
        def _(sp):
            for group in (w2_in, *late, *also):
                start_loads(nc, sp, group)

        @block.tensor
        def _(pe):
            def anchor_columns(e):
                for m in range(rows_of(e)):
                    c = e * MC + m
                    w = (w1[e] if e < E else gw)[:, :, m * P:(m + 1) * P]
                    for k in range(XK, CK):
                        mm = nc.tensor.matmul(b.cp[:, c:c + 1], w[:, k, :], g.cond[:, k - XK:k - XK + 1], start=(k == XK), stop=(k == CK - 1))
                mm.then_inc(s.cols, 1)

            loaded(pe, early)
            pe.wait_ge(s.anchor_b, KC)
            for k in range(XK, CK):
                nc.tensor.matmul(b.sp[:, ROW:ROW + E], b.anchor[:, k - XK, :], rw[:, k, :], start=(k == XK), stop=False)
            nc.tensor.matmul(b.sp[:, ROW:ROW + E], g.ones[0:1, :], rb[0:1, :], start=False, stop=True)
            for t in range(TT):
                for k in range(XK):
                    mm = nc.tensor.matmul(b.sp[:, LG + t * E:LG + (t + 1) * E], comb[k][:, t * P:(t + 1) * P], rw[:, k, :],
                                          start=(k == 0), stop=(k == XK - 1))
            mm.then_inc(s.logits, 1)

            n_hid = 0
            n_out = 0

            def first_layer(u, n):
                nb, e = units[u]
                if nb == 0:
                    if e > 0:
                        loaded(pe, late[e - 1])
                    if e:
                        pe.wait_ge(s.bias_set, e)
                    anchor_columns(e)
                for m in range(rows_of(e)):
                    if n >= HB:
                        pe.wait_ge(s.act_out, n - HB + 1)
                    for k in range(XK):
                        w = (w1[e] if e < E else gw)[:, k, m * P:(m + 1) * P]
                        mm = nc.tensor.matmul(b.hp[:, n % HB, :], w, comb[k][:, nb * BANK:(nb + 1) * BANK], start=(k == 0), stop=(k == XK - 1))
                    mm.then_inc(s.hid, 1)
                    n += 1
                return n

            def second_layer(u, n):
                e = units[u][1]
                i = exp_units.index(u) % 2
                pe.wait_ge(s.act_out, hid_end[u])
                if n == 0:
                    loaded(pe, w2_in)
                for q in range(TB):
                    if n >= OB:
                        pe.wait_ge(s.done, n - OB + 1)
                    for k in range(MC):
                        mm = nc.tensor.matmul(b.op[:, n % OB, 0:D], b.h[:, i, k, q * P:(q + 1) * P], w2[:, e, k, :], start=(k == 0), stop=(k == MC - 1))
                    mm.then_inc(s.ready, 1)
                    n += 1
                return n

            for u in range(len(units)):
                n_hid = first_layer(u, n_hid)
                if u and units[u - 1][1] < E:
                    n_out = second_layer(u - 1, n_out)

        @block.scalar
        def _(act):
            act.wait_ge(s.dve, 3)
            nc.scalar.activation(b.lg[:, :, :], b.lg[:, :, :], ACT.Exp).then_inc(s.exped, 1)
            for n, (u, m) in enumerate(hidden):
                nb, e = units[u]
                if nb == 0 and m == 0:
                    act.wait_ge(s.bias_set, e + 1)
                act.wait_ge(s.hid, n + 1)
                if e < E:
                    i = exp_units.index(u)
                    if i >= 2:
                        act.wait_ge(s.ready, out_end[exp_units[i - 2]])
                    o = b.h[:, i % 2, m, :]
                else:
                    o = g1T[:, m, nb * BANK:(nb + 1) * BANK]
                c = e * MC + m
                nc.scalar.activation(o, b.hp[:, n % HB, :], ACT.Silu, bias=b.bias[:, c:c + 1]).then_inc(s.act_out, 1)

        @block.vector
        def _(dve):
            for k in range(KC):
                nc.vector.tensor_scalar(b.anchor[:, k, :], g.ones[:, :], g.cond[:, k:k + 1], None, ALU.mult).then_inc(s.anchor_b, 1)
            loaded(dve, early)
            dve.wait_ge(s.logits, 1)
            def bias_columns(e):
                c0, c1 = e * MC, e * MC + rows_of(e)
                dve.wait_ge(s.cols, e + 1)
                nc.vector.tensor_tensor(b.bias[:, c0:c1], b1[:, c0:c1], b.cp[:, c0:c1], ALU.add).then_inc(s.bias_set, 1)

            nc.vector.tensor_copy(b.row[:, :], b.sp[:, ROW:ROW + E]).then_inc(s.row_set, 1)
            dve.wait_ge(s.row_set, 1)
            nc.vector.tensor_tensor(b.lg[:, :, :], b.sp[:, LG:ROW].rearrange("p (t e) -> p t e", e=E),
                                    b.row[:, :].unsqueeze(1).broadcast_to([P, TT, E]), ALU.add).then_inc(s.dve, 1)
            dve.wait_ge(s.dve, 1)
            nc.vector.tensor_reduce(b.red[:, 0, :], b.lg[:, :, :], AX.X, ALU.max).then_inc(s.dve, 1)
            dve.wait_ge(s.dve, 2)
            nc.vector.tensor_tensor(b.lg[:, :, :], b.lg[:, :, :], b.red[:, 0, :].unsqueeze(2).broadcast_to([P, TT, E]), ALU.subtract).then_inc(s.dve, 1)
            dve.wait_ge(s.exped, 1)
            nc.vector.tensor_reduce(b.red[:, 1, :], b.lg[:, :, :], AX.X, ALU.add).then_inc(s.dve, 1)
            dve.wait_ge(s.dve, 4)
            nc.vector.reciprocal(b.red[:, 2, :], b.red[:, 1, :]).then_inc(s.dve, 1)
            dve.wait_ge(s.dve, 5)
            nc.vector.tensor_tensor(b.prob[:, :, :], b.lg[:, :, :], b.red[:, 2, :].unsqueeze(2).broadcast_to([P, TT, E]), ALU.mult).then_inc(s.dve, 1)
            dve.wait_ge(s.dve, 6)
            bias_columns(0)
            for e in range(E):
                for t in range(TT):
                    w = b.prob[:, t, e:e + 1]
                    if e == 0:
                        nc.vector.tensor_scalar(routed[:, t, :], b2[:, e, :], w, None, ALU.mult).then_inc(s.init, 1)
                    else:
                        dve.wait_ge(s.init, (e - 1) * TT + t + 1)
                        nc.vector.scalar_tensor_tensor(routed[:, t, :], b2[:, e, :], w, routed[:, t, :], ALU.mult, ALU.add).then_inc(s.init, 1)
            dve.wait_ge(s.init, E * TT)
            for n, (u, q) in enumerate(outs):
                nb, e = units[u]
                if nb == 0 and q == 0:
                    bias_columns(e + 1)
                t = nb * TB + q
                dve.wait_ge(s.ready, n + 1)
                src, w = b.op[:, n % OB, 0:D], b.prob[:, t, e:e + 1]
                if e:
                    dve.wait_ge(s.done, n - TB + 1)
                nc.vector.scalar_tensor_tensor(routed[:, t, :], src, w, routed[:, t, :], ALU.mult, ALU.add).then_inc(s.done, 1)


def gated_output(nc, g, name, routedT, g1T, w, ob, gb, group, next_eps, also=()):
    NB = 4
    with stage(nc, name, ["ready", "gate", "biased", "prod", "done"] + STAT_SEMS,
               [("sg", [P, 2, D], F32), ("ro", [P, 2, D], F32), ("pr", [P, 2, D], F32)],
               [("o", [P, NB, BANK], F32), ("z", [P, NB, BANK], F32)]) as (s, b, block):
        @block.sync
        def _(sp):
            for other in also:
                start_loads(nc, sp, other)

        @block.tensor
        def _(pe):
            loaded(pe, group)
            for t in range(TT):
                if t >= NB:
                    pe.wait_ge(s.prod, t - NB + 1)
                for k in range(KC):
                    nc.tensor.matmul(b.z[:, t % NB, 0:D], g1T[:, k, t * P:(t + 1) * P], w[:, 1, k, :], start=(k == 0), stop=False)
                nc.tensor.matmul(b.z[:, t % NB, 0:D], g.ones[0:1, :], gb[0:1, :], start=False, stop=True)
                for k in range(KC):
                    mm = nc.tensor.matmul(b.o[:, t % NB, 0:D], routedT[:, k, t * P:(t + 1) * P], w[:, 0, k, :], start=(k == 0), stop=(k == KC - 1))
                mm.then_inc(s.ready, 1)

        @block.scalar
        def _(act):
            for t in range(TT):
                act.wait_ge(s.ready, t + 1)
                if t >= 2:
                    act.wait_ge(s.prod, t - 1)
                nc.scalar.activation(b.sg[:, t % 2, :], b.z[:, t % NB, 0:D], ACT.Sigmoid).then_inc(s.gate, 1)
            finish_statistics_act(nc, g, act, s)

        @block.vector
        def _(dve):
            loaded(dve, group)
            for t in range(TT + 2):
                if t < TT:
                    dve.wait_ge(s.ready, t + 1)
                    if t >= 2:
                        dve.wait_ge(s.done, t - 1)
                    nc.vector.tensor_tensor(b.ro[:, t % 2, :], b.o[:, t % NB, 0:D], ob[:, :], ALU.add).then_inc(s.biased, 1)
                    dve.wait_ge(s.biased, t + 1)
                    dve.wait_ge(s.gate, t + 1)
                    nc.vector.tensor_tensor(b.pr[:, t % 2, :], b.sg[:, t % 2, :], b.ro[:, t % 2, :], ALU.mult).then_inc(s.prod, 1)
                    dve.wait_ge(s.prod, t + 1)
                    nc.vector.tensor_tensor(g.x[:, t, :], g.x[:, t, :], b.pr[:, t % 2, :], ALU.add).then_inc(s.done, 1)
                tile_statistics(nc, g, dve, s, t)
            finish_statistics_dve(nc, g, dve, s, next_eps)


def expert_block(nc, g, a, ctxT, next_eps):
    E, RH = 3, 512
    CK, MC = 3 * D // P, RH // P
    with ExitStack() as ctx:
        def t(name, shape, where=ctx):
            return where.enter_context(tile(nc, "L1_" + name, shape))
        nxT, evT, qT, keys = t("nxT", [P, KC, TOK]), t("evT", [P, KC, TOK]), t("qT", [P, KC, TOK]), t("keys", [P, KC * TOK])
        kT = keys[:, 0:KC * CTX].rearrange("p (k n) -> p k n", k=KC)
        routed, g1T = keys[:, :].rearrange("p (t d) -> p t d", d=D), qT
        wo, ob, gb = t("wo", [P, 2, KC, D]), t("ob", [P, D]), t("gb2", [1, D])
        w_out = loads(ctx, nc, "L1_out_in", [(wo[:, 0], by_rows(a.L1_xcond_out_w)), (wo[:, 1], by_rows(a.L1_xcond_gate_w2)),
                                             (ob[:, :], a.L1_xcond_out_b.partition_broadcast(P)), (gb[:, :], as_row(a.L1_xcond_gate_b2))])
        with ExitStack() as ex:
            w1_0, gw = t("w1_0", [P, CK, RH], ex), t("gw", [P, CK, D], ex)
            rw, b1, b2, rb = t("rw", [P, CK, E], ex), t("b1", [P, E * MC + KC], ex), t("b2", [P, E, D], ex), t("rb", [1, E], ex)
            w_in = loads(ex, nc, "L1_qkv_in", [(gw[:, KC * i:KC * (i + 1)], by_rows(m)) for i, m in enumerate([a.L1_xcond_Wq, a.L1_xcond_Wk, a.L1_xcond_Wv])])
            early = loads(ex, nc, "L1_early", [(w1_0[:, :, :], by_rows(a.L1_xcond_e_w1[0]))]
                          + [(rw[:, :, :], by_rows(a.L1_xcond_router_W)), (b1[:, 0:E * MC], a.L1_xcond_e_b1.rearrange("e (k p) -> p (e k)", p=P)),
                             (b1[:, E * MC:], as_columns(a.L1_xcond_gate_b1)), (rb[:, :], as_row(a.L1_xcond_router_b))]
                          + [(b2[:, e, :], a.L1_xcond_e_b2[e].partition_broadcast(P)) for e in range(E)])
            norm_transpose(nc, g, "L1nx", [(g.x, TOK, nxT, (g.mv, g.rs, None), g.affine[:, 0], g.affine[:, 1]),
                                           (g.ctx, CTX, ctxT, None, None, None)], also=[w_in])
            with ExitStack() as inner:
                v = t("v", [P, CT, D], inner)
                plain_projections(nc, g, "L1qkv", [(nxT, TOK, qT), (ctxT, CTX, kT)], ctxT, CTX, v,
                                  gw[:, :, :].rearrange("p (i k) d -> p i k d", k=KC), w_in)
                prototype_attention(nc, g, "L1at", qT, kT, v, evT, also=[early])
            w2, w1_1, w1_2 = t("w2", [P, E, MC, D], ex), t("w1_1", [P, CK, RH], ex), t("w1_2", [P, CK, RH], ex)
            w2_in = loads(ex, nc, "L1_w2_in", [(w2[:, e], by_rows(a.L1_xcond_e_w2[e])) for e in range(E)])
            late = [loads(ex, nc, f"L1_late{i}", [(dst[:, :, :], by_rows(src))])
                    for i, (dst, src) in enumerate([(w1_1, a.L1_xcond_e_w1[1]), (w1_2, a.L1_xcond_e_w1[2]), (gw, a.L1_xcond_gate_w1)])]
            experts(nc, g, "L1ex", nxT, evT, routed, g1T, [w1_0, w1_1, w1_2], w2, gw, rw, b1, b2, rb, early, w2_in, late, [w_out])
        norm_transpose(nc, g, "L1rt", [(routed, TOK, nxT, None, None, None)])
        gated_output(nc, g, "L1go", nxT, g1T, wo, ob, gb, w_out, next_eps)



def mlp(nc, g, name, xT, w1, b1, w2, b2, group, gate, func, next_eps=None):
    FC = w2.shape[1]
    NBLK, TB = TOK // BANK, BANK // P
    HB = OB = 4
    with stage(nc, name, ["hid", "act_out", "ready", "done", "gated", "biased"] + STAT_SEMS,
               [("h", [P, 2, FC, BANK], F32)],
               [("hp", [P, HB, BANK], F32), ("op", [P, OB, BANK], F32)]) as (s, b, block):
        @block.tensor
        def _(pe):
            loaded(pe, group)

            def first_layer(nb):
                for m in range(FC):
                    n = nb * FC + m
                    if n >= HB:
                        pe.wait_ge(s.act_out, n - HB + 1)
                    for k in range(KC):
                        mm = nc.tensor.matmul(b.hp[:, n % HB, :], w1[:, k, m * P:(m + 1) * P], xT[:, k, nb * BANK:(nb + 1) * BANK],
                                              start=(k == 0), stop=(k == KC - 1))
                    mm.then_inc(s.hid, 1)

            def second_layer(nb):
                pe.wait_ge(s.act_out, (nb + 1) * FC)
                for q in range(TB):
                    t = nb * TB + q
                    if t >= OB:
                        pe.wait_ge(s.done, t - OB + 1)
                    for k in range(FC):
                        mm = nc.tensor.matmul(b.op[:, t % OB, 0:D], b.h[:, nb % 2, k, q * P:(q + 1) * P], w2[:, k, :], start=(k == 0), stop=(k == FC - 1))
                    mm.then_inc(s.ready, 1)

            for nb in range(NBLK):
                first_layer(nb)
                if nb == 0:
                    pe.wait_ge(s.gated, FC + 1)
                if nb:
                    second_layer(nb - 1)
            second_layer(NBLK - 1)

        @block.scalar
        def _(act):
            loaded(act, group)
            for n in range(NBLK * FC):
                nb, m = n // FC, n % FC
                act.wait_ge(s.hid, n + 1)
                if nb >= 2:
                    act.wait_ge(s.ready, (nb - 1) * TB)
                nc.scalar.activation(b.h[:, nb % 2, m, :], b.hp[:, n % HB, :], func, bias=b1[:, m:m + 1]).then_inc(s.act_out, 1)
            if next_eps is not None:
                finish_statistics_act(nc, g, act, s)

        @block.vector
        def _(dve):
            loaded(dve, group)
            for k in range(FC):
                nc.vector.tensor_tensor(w2[:, k, :], w2[:, k, :], gate[:, :], ALU.mult).then_inc(s.gated, 1)
            nc.vector.tensor_tensor(b2[:, :], b2[:, :], gate[:, :], ALU.mult).then_inc(s.gated, 1)
            dve.wait_ge(s.gated, FC + 1)
            nc.vector.tensor_tensor(g.x[:, :, :], g.x[:, :, :], b2[:, :].unsqueeze(1).broadcast_to([P, TT, D]), ALU.add).then_inc(s.biased, 1)
            dve.wait_ge(s.biased, 1)
            for t in range(TT + 2):
                if t < TT:
                    dve.wait_ge(s.ready, t + 1)
                    nc.vector.tensor_tensor(g.x[:, t, :], g.x[:, t, :], b.op[:, t % OB, 0:D], ALU.add).then_inc(s.done, 1)
                if next_eps is not None:
                    tile_statistics(nc, g, dve, s, t)
            if next_eps is not None:
                finish_statistics_dve(nc, g, dve, s, next_eps)


def modulated_mlp(nc, g, name, mod, w1, b1, w2, b2, gate, func, next_eps=None, also=()):
    F = w1.shape[1]
    with ExitStack() as ctx:
        xT = ctx.enter_context(tile(nc, name + "_xT", [P, KC, TOK]))
        w1s, w2s = ctx.enter_context(tile(nc, name + "_w1", [P, KC, F])), ctx.enter_context(tile(nc, name + "_w2", [P, F // P, D]))
        b1s, b2s = ctx.enter_context(tile(nc, name + "_b1", [P, F // P])), ctx.enter_context(tile(nc, name + "_b2", [P, D]))
        w_in = loads(ctx, nc, name + "_in", [(w1s[:, :, :], by_rows(w1)), (b1s[:, :], as_columns(b1)),
                                             (w2s[:, :, :], by_rows(w2)), (b2s[:, :], b2.partition_broadcast(P))])
        norm_transpose(nc, g, name + "nx", [(g.x, TOK, xT, (g.mv, g.rs, None), *mod)], also=[w_in, *also])
        mlp(nc, g, name + "ml", xT, w1s, b1s, w2s, b2s, w_in, gate, func, next_eps)


def store(nc, g, out):
    with stage(nc, "out", ["stored"]) as (s, b, block):
        @block.sync
        def _(sp):
            sp.dma_start(out[0].rearrange("(t p) d -> p t d", p=P), g.x[:, :, :]).then_inc(s.stored, 16)
            sp.wait_ge(s.stored, 16)


@contextmanager
def tile(nc, name, shape, dt=F32):
    with nc.sbuf_tensor(name, shape, dt) as t:
        yield t


def attend(nc, g, name, mod_q, kv, n, wq, bq, wk, bk, wv, bv, wp, bp, next_eps, gate=None, keep=None, mask_row=None, also=()):
    with ExitStack() as ctx:
        def t(name_, shape, dt=F32, where=ctx):
            return where.enter_context(tile(nc, name + name_, shape, dt))
        stored, retire = semaphores(nc, [f"{name}_stored_{n}" for n in ("k0", "q0", "k1", "q1")])
        ctx.callback(retire)
        w, bias, vbias = t("_w", [P, 4, KC, D]), t("_bias", [P, 2, KC]), t("_vb", [1, D])
        pbias = t("_pb", [P, D])
        xT = t("_xT", [P, KC, TOK])
        w_in = loads(ctx, nc, name + "_w_in", [(w[:, 0], by_rows(wk)), (w[:, 1], by_rows(wq)), (bias[:, 0], as_columns(bk)), (bias[:, 1], as_columns(bq)),
                                               (w[:, 2], by_rows(wv)), (vbias[:, :], as_row(bv))])
        p_in = loads(ctx, nc, name + "_p_in", [(w[:, 3], by_rows(wp)), (pbias[:, :], bp.partition_broadcast(P))])
        sources = [(g.x, TOK, xT, (g.mv, g.rs, None), *mod_q)]
        kvT = xT if kv is None else kv
        inner = ctx.enter_context(ExitStack())
        if isinstance(kv, tuple):
            src, mv, eps, *mod_kv = kv
            kvT = t("_cT", [P, KC, CTX], F32, inner)
            sources.append((src, n, kvT, (mv, None, eps), *mod_kv))
        norm_transpose(nc, g, name + "nx", sources, also=[w_in])
        part = t("_part", [P, 2, 3, TOK], BF16, inner)
        split_projections(nc, g, name + "qk", [(kvT, n, g.k_scr), (xT, TOK, g.q_scr)], w, bias, w_in, part, stored)
        v_all = t("_v", [P, NH, -(-n // P), DH], F32, inner)
        o = xT[:, :, :].rearrange("p k n -> p (k n)").rearrange("p (t d) -> p t d", d=D)
        attention(nc, g, name + "at", n, o, kvT, w[:, 2], vbias, w_in, v_all, stored, keep, mask_row, also=[p_in])
        inner.close()
        project_heads(nc, g, name + "pr", o, w[:, 3], pbias, p_in, next_eps, gate, also)


def program(nc, a, out):
    RETIRED.clear()
    with ExitStack() as ctx:
        lasting = [("x", [P, TT, D], F32), ("ctx", [P, CT, D], F32), ("ident", [P, P], F32), ("ident_b", [P, P], BF16),
                   ("ones", [P, P], F32), ("cond", [P, KC], F32), ("silu", [P, KC], F32), ("silu_b", [P, KC, P], F32), ("mod", [P, 32], F32),
                   ("gate", [P, 4, D], F32), ("affine", [P, 2, KC], F32), ("keep", [P, CT], F32), ("mv_ctx", [P, CT, 2], F32),
                   ("st", [P, TT, 6], F32), ("mv", [P, TT, 2], F32), ("sd", [P, TT], F32), ("rs", [P, TT], F32)]
        scratch = [("q_scr", [3, D, TOK]), ("k_scr", [3, D, TOK]), ("mask_row", [1, CTX])]
        g = named([n for n, _, _ in lasting] + [n for n, _ in scratch],
                  [ctx.enter_context(nc.sbuf_tensor("g_" + n, shape, dt)) for n, shape, dt in lasting]
                  + [nc.dram_tensor(n, shape, BF16, kind="Internal").ap() for n, shape in scratch])

        def vec(i):
            return g.mod[:, i * KC:(i + 1) * KC]

        with ExitStack() as mods:
            w, bcol = mods.enter_context(tile(nc, "m0_w", [P, KC, 4 * D])), mods.enter_context(tile(nc, "m0_b", [P, 8]))
            m_in = loads(mods, nc, "m0_in", [(w[:, :, 0:2 * D], by_rows(a.L0_xcond_Wss_q)), (w[:, :, 2 * D:], by_rows(a.L0_xcond_Wss_kv)),
                                             (bcol[:, 0:4], as_columns(a.L0_xcond_bss_q)), (bcol[:, 4:8], as_columns(a.L0_xcond_bss_kv))])
            start(nc, g, a, [m_in])
            modulation(nc, g, "m0", w, bcol, m_in, 8, 0, [0, 4])

        with ExitStack() as mods:
            w, bcol = mods.enter_context(tile(nc, "m2_w", [P, KC, 6 * D])), mods.enter_context(tile(nc, "m2_b", [P, 12]))
            brow = mods.enter_context(tile(nc, "m2_r", [1, 2, D]))
            m2_in = loads(mods, nc, "m2_in", [(w[:, :, :], by_rows(a.L2_xcond_W_mod)), (bcol[:, :], as_columns(a.L2_xcond_b_mod))]
                          + [(brow[:, i, :], as_row(a.L2_xcond_b_mod[v * D:(v + 1) * D])) for i, v in ((0, 2), (1, 5))])
            attend(nc, g, "L0", (vec(0), vec(1)), (g.ctx, g.mv_ctx, 1e-5, vec(2), vec(3)), CTX, a.L0_xcond_Wq, a.L0_xcond_bq,
                   a.L0_xcond_Wkv[:, 0:D], a.L0_xcond_bkv[0:D], a.L0_xcond_Wkv[:, D:2 * D], a.L0_xcond_bkv[D:2 * D],
                   a.L0_xcond_Wp, a.L0_xcond_bp, next_eps=1e-5, also=[m2_in])
            modulation(nc, g, "m2", w, bcol, m2_in, 12, 8, [2, 8], [4, 10], brow, 0)

        ctxT = ctx.enter_context(tile(nc, "ctxT", [P, KC, CTX]))
        expert_block(nc, g, a, ctxT, next_eps=1e-6)

        def vec2(i):
            return vec(4 + i)

        attend(nc, g, "L2s", (vec2(1), vec2(0)), None, TOK, a.L2_xcond_W_qkv[:, 0:D], a.L2_xcond_b_qkv[0:D],
               a.L2_xcond_W_qkv[:, D:2 * D], a.L2_xcond_b_qkv[D:2 * D], a.L2_xcond_W_qkv[:, 2 * D:3 * D], a.L2_xcond_b_qkv[2 * D:3 * D],
               a.L2_xcond_W_proj, a.L2_xcond_b_proj, next_eps=1e-6, gate=g.gate[:, 0])
        attend(nc, g, "L2c", (None, None), (g.ctx, g.mv_ctx, 1e-6, None, None), CTX, a.L2_xcond_W_qc, a.L2_xcond_b_qc,
               a.L2_xcond_W_kvc[:, 0:D], a.L2_xcond_b_kvc[0:D], a.L2_xcond_W_kvc[:, D:2 * D], a.L2_xcond_b_kvc[D:2 * D],
               a.L2_xcond_W_cproj, a.L2_xcond_b_cproj, next_eps=1e-6)
        with ExitStack() as mods:
            w, bcol = mods.enter_context(tile(nc, "m3_w", [P, KC, 6 * D])), mods.enter_context(tile(nc, "m3_b", [P, 12]))
            brow = mods.enter_context(tile(nc, "m3_r", [1, 2, D]))
            m3_in = loads(mods, nc, "m3_in", [(w[:, :, :], by_rows(a.L3_xcond_ada_w)), (bcol[:, :], as_columns(a.L3_xcond_ada_b))]
                          + [(brow[:, i, :], as_row(a.L3_xcond_ada_b[v * D:(v + 1) * D])) for i, v in ((0, 2), (1, 5))])
            modulated_mlp(nc, g, "L2m", (vec2(4), vec2(3)), a.L2_xcond_W_mlp1, a.L2_xcond_b_mlp1,
                          a.L2_xcond_W_mlp2, a.L2_xcond_b_mlp2, g.gate[:, 1], ACT.Gelu_apprx_tanh, next_eps=1e-6, also=[m3_in])
            modulation(nc, g, "m3", w, bcol, m3_in, 12, 20, [2, 8], [4, 10], brow, 2)

        def vec3(i):
            return vec(10 + i)

        attend(nc, g, "L3s", (vec3(1), vec3(0)), None, TOK, a.L3_xcond_qkv_w[:, 0:D], a.L3_xcond_qkv_b[0:D],
               a.L3_xcond_qkv_w[:, D:2 * D], a.L3_xcond_qkv_b[D:2 * D], a.L3_xcond_qkv_w[:, 2 * D:3 * D], a.L3_xcond_qkv_b[2 * D:3 * D],
               a.L3_xcond_sa_proj_w, a.L3_xcond_sa_proj_b, next_eps=1e-6, gate=g.gate[:, 2])
        attend(nc, g, "L3c", (None, None), ctxT, CTX, a.L3_xcond_q_w, a.L3_xcond_q_b,
               a.L3_xcond_kv_w[:, 0:D], a.L3_xcond_kv_b[0:D], a.L3_xcond_kv_w[:, D:2 * D], a.L3_xcond_kv_b[D:2 * D],
               a.L3_xcond_ca_proj_w, a.L3_xcond_ca_proj_b, next_eps=1e-6, keep=g.keep, mask_row=g.mask_row)
        modulated_mlp(nc, g, "L3m", (vec3(4), vec3(3)), a.L3_xcond_fc1_w, a.L3_xcond_fc1_b,
                      a.L3_xcond_fc2_w, a.L3_xcond_fc2_b, g.gate[:, 3], ACT.Gelu)
        store(nc, g, out)



def kernel(**inputs):
    import numpy as _np
    import concourse.bacc as _bacc
    from concourse import mybir as _mybir
    from concourse.bass_utils import run_bass_kernel_spmd as _run

    nc = _bacc.Bacc("TRN2", target_bir_lowering=False, num_devices=1)
    arrays, args = {}, {}
    for name, value in inputs.items():
        a = _np.ascontiguousarray(value)
        arrays[f"in_{name}"] = a
        args[name] = nc.dram_tensor(f"in_{name}", a.shape, _mybir.dt.from_np(a.dtype), kind="ExternalInput").ap()
    out = nc.dram_tensor("out_0", (1, 2048, 256), _mybir.dt.float32, kind="ExternalOutput").ap()
    program(nc, named(list(args), list(args.values())), out)
    r = _run(nc, [arrays], core_ids=[0])
    return r.results[0]["out_0"]
```

```python
import struct
from collections import namedtuple
from contextlib import ExitStack, contextmanager

import concourse.bass as bass
from concourse import mybir

ALU = mybir.AluOpType
ACT = mybir.ActivationFunctionType
AX = mybir.AxisListType
F32 = mybir.dt.float32
BF16 = mybir.dt.bfloat16

P = 128
D = 256
KC = D // P
NH = 16
DH = D // NH
TOK = 2048
TT = TOK // P
CTX = 1601
CT = -(-CTX // P)
BANK = 512
MASKED = -3.0e38
TWO_ONES = struct.unpack("<f", struct.pack("<I", 0x3F803F80))[0]


def cut(n, step):
    return [(i, min(step, n - i)) for i in range(0, n, step)]


def named(names, values):
    return namedtuple("Named", names)(*values)


RETIRED = []


def semaphores(nc, names):
    held = ExitStack()
    handles = [held.enter_context(nc.semaphore(n)) for n in names]

    def retire():
        RETIRED.append((handles, held))
    return handles, retire


@contextmanager
def stage(nc, name, sems, tiles=(), psum=()):
    with ExitStack() as ctx:
        handles, retire = semaphores(nc, [f"{name}_{n}" for n in sems])
        s = named(sems, handles)
        b = named([t[0] for t in (*tiles, *psum)],
                  [ctx.enter_context(nc.sbuf_tensor(f"{name}_{n}", shape, dt)) for n, shape, dt in tiles]
                  + [ctx.enter_context(nc.psum_tensor(f"{name}_{n}", shape, dt)) for n, shape, dt in psum])
        old = RETIRED[:]
        RETIRED.clear()
        with nc.Block() as block:
            if old:
                @block.gpsimd
                def _(pool):
                    for found, _ in old:
                        for h in found:
                            pool.sem_clear(h)
            yield s, b, block
        for _, held in old:
            held.close()
        retire()


def loads(ctx, nc, name, copies):
    (sem,), retire = semaphores(nc, [name])
    ctx.callback(retire)
    return sem, copies


def start_loads(nc, sp, group):
    sem, copies = group
    with nc.allow_non_contiguous_dma("bias vectors, one word per partition"):
        for dst, src in copies:
            sp.dma_start(dst, src).then_inc(sem, 16)


def loaded(eng, group):
    eng.wait_ge(group[0], 16 * len(group[1]))


def by_rows(w):
    return w.rearrange("(k p) n -> p k n", p=P)


def as_columns(v):
    return v.rearrange("(k p) -> p k", p=P)


def as_row(v):
    return v.rearrange("(o n) -> o n", o=1)



def tile_statistics(nc, g, dve, s, t):
    if 1 <= t <= TT:
        dve.wait_ge(s.done, t)
        nc.vector.bn_stats(g.st[:, t - 1, :], g.x[:, t - 1, :]).then_inc(s.stats, 1)
    if t >= 2:
        dve.wait_ge(s.stats, t - 1)
        nc.vector.bn_aggr(g.mv[:, t - 2, :], g.st[:, t - 2, :]).then_inc(s.aggr, 1)


def finish_statistics_dve(nc, g, dve, s, eps):
    dve.wait_ge(s.aggr, TT)
    nc.vector.tensor_scalar(g.sd[:, :], g.mv[:, :, 1], eps, None, ALU.add).then_inc(s.eps_added, 1)
    dve.wait_ge(s.std, 1)
    nc.vector.reciprocal(g.rs[:, :], g.sd[:, :]).then_inc(s.rstd, 1)


def finish_statistics_act(nc, g, act, s):
    act.wait_ge(s.eps_added, 1)
    nc.scalar.activation(g.sd[:, :], g.sd[:, :], ACT.Sqrt).then_inc(s.std, 1)


STAT_SEMS = ["stats", "aggr", "eps_added", "std", "rstd"]



def start(nc, g, a, also):
    full = CTX // P
    rest = CTX - full * P
    with stage(nc, "start", ["cond_in", "x_in", "ctx_in", "mask_set", "mask_in", "small_in", "const", "silu_done", "bcast",
                             "done", "ctx_stats", "ctx_aggr", "mask_done", "mask_out"] + STAT_SEMS,
               [("cst", [P, CT, 6], F32), ("mcol", [P, CT], mybir.dt.uint8), ("mrow", [1, CTX], mybir.dt.uint8), ("mrowb", [1, CTX], BF16)]) as (s, b, block):
        @block.sync
        def _(sp):
            with nc.allow_non_contiguous_dma("a condition vector, one word per partition"):
                sp.dma_start(g.cond[:, :], a.cond_1024.rearrange("o (k p) -> p (o k)", p=P)).then_inc(s.cond_in, 16)
            sp.dma_start(g.x[:, :, :], a.x[0].rearrange("(t p) d -> p t d", p=P)).then_inc(s.x_in, 16)
            sp.wait_ge(s.mask_set, 1)
            with nc.allow_non_contiguous_dma("the mask, one byte per partition; norm vectors, one word"):
                sp.dma_start(b.mcol[:, 0:full], a.mask_BxS2_bf0[0, 0:full * P].rearrange("(t p) -> p t", p=P)).then_inc(s.mask_in, 16)
                sp.dma_start(b.mcol[0:rest, full:full + 1], a.mask_BxS2_bf0[0, full * P:CTX].rearrange("(p o) -> p o", o=1)).then_inc(s.mask_in, 16)
                sp.dma_start(g.affine[:, 0], as_columns(a.L1_xcond_ln_gamma)).then_inc(s.small_in, 16)
                sp.dma_start(g.affine[:, 1], as_columns(a.L1_xcond_ln_beta)).then_inc(s.small_in, 16)
            sp.dma_start(b.mrow[:, :], a.mask_BxS2_bf0).then_inc(s.mask_in, 16)
            for group in also:
                start_loads(nc, sp, group)
            sp.dma_start(g.ctx[:, 0:full, :], a.ctx_1024[0, 0:full * P].rearrange("(t p) d -> p t d", p=P)).then_inc(s.ctx_in, 16)
            sp.dma_start(g.ctx[0:rest, full, :], a.ctx_1024[0, full * P:CTX]).then_inc(s.ctx_in, 16)
            sp.wait_ge(s.mask_done, 2)
            sp.dma_start(g.mask_row, b.mrowb[:, :]).then_inc(s.mask_out, 16)
            sp.wait_ge(s.mask_out, 16)
            sp.wait_ge(s.small_in, 32)

        @block.gpsimd
        def _(pool):
            nc.gpsimd.memset(g.ones[:, :], 1.0).then_inc(s.const, 1)
            nc.gpsimd.memset(g.ident[:, :], 0.0).then_inc(s.const, 1)
            pool.wait_ge(s.const, 2)
            nc.gpsimd.affine_select(out=g.ident[:, :], in_=g.ident[:, :], compare_op=ALU.not_equal, fill=1.0,
                                    base=0, pattern=[[-1, P]], channel_multiplier=1).then_inc(s.const, 1)
            pool.wait_ge(s.const, 3)
            nc.gpsimd.tensor_copy(g.ident_b[:, :], g.ident[:, :]).then_inc(s.const, 1)

        @block.scalar
        def _(act):
            act.wait_ge(s.cond_in, 16)
            nc.scalar.activation(g.silu[:, :], g.cond[:, :], ACT.Silu).then_inc(s.silu_done, 1)
            finish_statistics_act(nc, g, act, s)

        @block.vector
        def _(dve):
            nc.vector.memset(b.mcol[:, :], 0).then_inc(s.mask_set, 1)
            nc.vector.memset(g.mv_ctx[:, :, :], 1.0).then_inc(s.mask_set, 1)
            dve.wait_ge(s.silu_done, 1)
            dve.wait_ge(s.const, 1)
            for k in range(KC):
                nc.vector.tensor_scalar(g.silu_b[:, k, :], g.ones[:, :], g.silu[:, k:k + 1], None, ALU.mult).then_inc(s.bcast, 1)
            dve.wait_ge(s.x_in, 16)
            for t in range(TT):
                nc.vector.bn_stats(g.st[:, t, :], g.x[:, t, :]).then_inc(s.stats, 1)
            for t in range(TT):
                dve.wait_ge(s.stats, t + 1)
                nc.vector.bn_aggr(g.mv[:, t, :], g.st[:, t, :]).then_inc(s.aggr, 1)
            finish_statistics_dve(nc, g, dve, s, 1e-5)
            dve.wait_ge(s.mask_in, 48)
            nc.vector.tensor_scalar(g.keep[:, :], b.mcol[:, :], -1.0, 1.0, ALU.mult, ALU.add).then_inc(s.mask_done, 1)
            nc.vector.tensor_scalar(b.mrowb[:, :], b.mrow[:, :], MASKED, None, ALU.mult).then_inc(s.mask_done, 1)
            dve.wait_ge(s.ctx_in, 32)
            dve.wait_ge(s.mask_set, 2)
            rows = [r for _, r in cut(CTX, P)]
            for t, r in enumerate(rows):
                nc.vector.bn_stats(b.cst[0:r, t, :], g.ctx[0:r, t, :]).then_inc(s.ctx_stats, 1)
            for t, r in enumerate(rows):
                dve.wait_ge(s.ctx_stats, t + 1)
                nc.vector.bn_aggr(g.mv_ctx[0:r, t, :], b.cst[0:r, t, :]).then_inc(s.ctx_aggr, 1)


def modulation(nc, g, name, w, bcol, group, ncol, mod0, scales, gates=(), brow=None, gate0=0):
    with stage(nc, name, ["cols_ready", "gates_ready", "dve_done"], [],
               [("cols", [P, BANK], F32), ("gate", [P, max(1, len(gates)), BANK], F32)]) as (s, b, block):
        @block.tensor
        def _(pe):
            loaded(pe, group)
            for c in range(ncol):
                for k in range(KC):
                    mm = nc.tensor.matmul(b.cols[:, c:c + 1], w[:, k, c * P:(c + 1) * P], g.silu[:, k:k + 1],
                                          start=(k == 0), stop=(k == KC - 1))
            mm.then_inc(s.cols_ready, 1)
            for i, c in enumerate(gates):
                for k in range(KC):
                    nc.tensor.matmul(b.gate[:, i, 0:D], g.silu_b[:, k, :], w[:, k, c * P:c * P + D], start=(k == 0), stop=False)
                nc.tensor.matmul(b.gate[:, i, 0:D], g.ones[0:1, :], brow[0:1, i, :], start=False, stop=True).then_inc(s.gates_ready, 1)

        @block.vector
        def _(dve):
            loaded(dve, group)
            dve.wait_ge(s.cols_ready, 1)
            nc.vector.tensor_tensor(g.mod[:, mod0:mod0 + ncol], b.cols[:, 0:ncol], bcol[:, :], ALU.add).then_inc(s.dve_done, 1)
            dve.wait_ge(s.dve_done, 1)
            for c in scales:
                v = g.mod[:, mod0 + c:mod0 + c + KC]
                nc.vector.tensor_scalar(v, v, 1.0, None, ALU.add).then_inc(s.dve_done, 1)
            if gates:
                dve.wait_ge(s.gates_ready, len(gates))
                nc.vector.tensor_copy(g.gate[:, gate0:gate0 + len(gates), :], b.gate[:, :, 0:D]).then_inc(s.dve_done, 1)



def norm_transpose(nc, g, name, sources, also=(), zeroed=None):
    jobs, first_row, rows = [], [], []
    for i, (src, n, dst, norm, scale, shift) in enumerate(sources):
        tiles = cut(n, P)
        first_row.append(len(rows))
        rows += [(i, t, r) for t, (_, r) in enumerate(tiles)]
        jobs += [(i, k, t0, m, sum(r for _, r in tiles[t0:t0 + m])) for t0, m in cut(len(tiles), 4) for k in range(KC)]
    NB = 8
    eps = [(i, norm) for i, (_, _, _, norm, _, _) in enumerate(sources) if norm is not None and norm[2] is not None]
    with stage(nc, name, ["zeroed", "eps_added", "std", "rstd", "normed", "turned", "out_dve", "out_act"],
               [("y", [P, len(rows), D], F32), ("sd", [P, CT], F32), ("rs", [P, CT], F32)],
               [("ps", [P, NB, BANK], F32)]) as (s, b, block):
        def copy(j):
            i, k, t0, m, w = jobs[j]
            _, _, dst, _, scale, shift = sources[i]
            return (dst[:, k, t0 * P:t0 * P + w], b.ps[:, j % NB, 0:w],
                    None if scale is None else scale[:, k:k + 1], None if scale is None else shift[:, k:k + 1])

        @block.sync
        def _(sp):
            for group in also:
                start_loads(nc, sp, group)

        if zeroed is not None:
            @block.gpsimd
            def _(pool):
                nc.gpsimd.memset(zeroed[:, :, :], 0.0).then_inc(s.zeroed, 1)
                pool.wait_ge(s.zeroed, 1)

        @block.vector
        def _(dve):
            for i, (mv, _, e) in eps:
                nc.vector.tensor_scalar(b.sd[:, :], mv[:, :, 1], e, None, ALU.add).then_inc(s.eps_added, 1)
            for i, t, r in rows:
                src, _, _, norm, _, _ = sources[i]
                if norm is None:
                    continue
                mv, rs, e = norm
                if e is not None:
                    rs = b.rs
                    if t == 0:
                        dve.wait_ge(s.std, 1)
                        nc.vector.reciprocal(b.rs[:, :], b.sd[:, :]).then_inc(s.rstd, 1)
                        dve.wait_ge(s.rstd, 1)
                nc.vector.tensor_scalar(b.y[0:r, first_row[i] + t, :], src[0:r, t, :], mv[0:r, t, 0:1], rs[0:r, t:t + 1],
                                        ALU.subtract, ALU.mult).then_inc(s.normed, 1)
            for j in range(0, len(jobs), 2):
                o, i, scale, shift = copy(j)
                dve.wait_ge(s.turned, j + 1)
                if scale is None:
                    nc.vector.tensor_copy(o, i).then_inc(s.out_dve, 1)
                else:
                    nc.vector.tensor_scalar(o, i, scale, shift, ALU.mult, ALU.add).then_inc(s.out_dve, 1)

        @block.scalar
        def _(act):
            for _ in eps:
                act.wait_ge(s.eps_added, 1)
                nc.scalar.activation(b.sd[:, :], b.sd[:, :], ACT.Sqrt).then_inc(s.std, 1)
            for j in range(1, len(jobs), 2):
                o, i, scale, shift = copy(j)
                act.wait_ge(s.turned, j + 1)
                if scale is None:
                    nc.scalar.activation(o, i, ACT.Copy).then_inc(s.out_act, 1)
                else:
                    nc.scalar.activation(o, i, ACT.Identity, bias=shift, scale=scale).then_inc(s.out_act, 1)

        @block.tensor
        def _(pe):
            normed = 0
            for j, (i, k, t0, m, _) in enumerate(jobs):
                src, n, _, norm, _, _ = sources[i]
                if norm is not None and k == 0:
                    normed += m
                    pe.wait_ge(s.normed, normed)
                if j >= NB:
                    pe.wait_ge(s.out_act if j % 2 else s.out_dve, (j - NB) // 2 + 1)
                for q in range(m):
                    r = min(P, n - (t0 + q) * P)
                    y = src[0:r, t0 + q, k * P:(k + 1) * P] if norm is None else b.y[0:r, first_row[i] + t0 + q, k * P:(k + 1) * P]
                    mm = nc.tensor.transpose(b.ps[:, j % NB, q * P:q * P + r], y, g.ident[0:r, 0:r])
                mm.then_inc(s.turned, 1)



def split_projections(nc, g, name, jobs_in, w, bias, group, part, stored):
    NB, NW = 8, len(jobs_in)
    groups = [(j, 0) for j in range(NW)]
    blocks = [(j, m, c0, cs) for j, m in groups for c0, cs in cut(jobs_in[j][1], BANK)]
    ends = [max(i for i, bl in enumerate(blocks) if bl[0:2] == gr) + 1 for gr in groups]
    with stage(nc, name, ["ready", "evac", "hi", "rest", "mid", "low"],
               [("full", [P, 2, TOK], F32), ("rest", [P, 2, TOK], F32)], [("ps", [P, NB, BANK], F32)]) as (s, b, block):
        @block.sync
        def _(sp):
            for i, (j, m) in enumerate(groups):
                _, n, scr = jobs_in[j]
                sp.wait_ge(s.mid, ends[i])
                sp.wait_ge(s.low, ends[i])
                sp.dma_start(scr[:, m * P:(m + 1) * P, 0:n].rearrange("i p n -> p i n"), part[:, i % 2, :, 0:n]).then_inc(stored[i], 16)

        @block.tensor
        def _(pe):
            loaded(pe, group)
            for i, (j, m, c0, cs) in enumerate(blocks):
                x = jobs_in[j][0]
                if i >= NB:
                    pe.wait_ge(s.hi, i - NB + 1)
                for k in range(KC):
                    mm = nc.tensor.matmul(b.ps[:, i % NB, 0:cs], w[:, j, k, m * P:(m + 1) * P], x[:, k, c0:c0 + cs],
                                          start=(k == 0), stop=(k == KC - 1))
                mm.then_inc(s.ready, 1)

        @block.scalar
        def _(act):
            def middle(i):
                j, m, c0, cs = blocks[i]
                at = groups.index((j, m)) % 2
                act.wait_ge(s.rest, i + 1)
                nc.scalar.activation(part[:, at, 1, c0:c0 + cs], b.rest[:, at, c0:c0 + cs], ACT.Copy).then_inc(s.mid, 1)

            for i, (j, m, c0, cs) in enumerate(blocks):
                gi = groups.index((j, m))
                act.wait_ge(s.ready, i + 1)
                col = bias[:, j, m:m + 1]
                nc.scalar.activation(b.full[:, gi % 2, c0:c0 + cs], b.ps[:, i % NB, 0:cs], ACT.Identity, bias=col).then_inc(s.evac, 1)
                nc.scalar.activation(part[:, gi % 2, 0, c0:c0 + cs], b.ps[:, i % NB, 0:cs], ACT.Identity, bias=col).then_inc(s.hi, 1)
                if i:
                    middle(i - 1)
            middle(len(blocks) - 1)

        @block.vector
        def _(dve):
            def low(i):
                j, m, c0, cs = blocks[i]
                at = groups.index((j, m)) % 2
                dve.wait_ge(s.mid, i + 1)
                nc.vector.tensor_tensor(part[:, at, 2, c0:c0 + cs], b.rest[:, at, c0:c0 + cs], part[:, at, 1, c0:c0 + cs], ALU.subtract).then_inc(s.low, 1)

            for i, (j, m, c0, cs) in enumerate(blocks):
                at = groups.index((j, m)) % 2
                dve.wait_ge(s.evac, i + 1)
                dve.wait_ge(s.hi, i + 1)
                nc.vector.tensor_tensor(b.rest[:, at, c0:c0 + cs], b.full[:, at, c0:c0 + cs], part[:, at, 0, c0:c0 + cs], ALU.subtract).then_inc(s.rest, 1)
                if i:
                    low(i - 1)
            low(len(blocks) - 1)



def attention(nc, g, name, n, out, jobs_in, w, bias, vbias, group, part, v_all, stored, keep=None, mask_row=None, also=()):
    kvT = jobs_in[0][0]
    blocks = [(j, c0, cs) for j in range(2) for c0, cs in cut(jobs_in[j][1], BANK)]
    NBL = len(blocks)
    EARLY = 2
    ends = [sum(1 for bl in blocks if bl[0] <= j) for j in range(2)]
    tiles = cut(n, P)
    NT = len(tiles)
    PARTS = 96
    MASKROW, ONEROWS = 96, 97
    ROWS = ONEROWS + 3
    RING = 3
    CH = 4
    step = -(-n // CH)
    chunks = cut(n, step)
    UNITS = TT * CH
    SCALE = float(DH) ** -0.5
    AHEAD = 5 * CH
    REST = UNITS - AHEAD
    PB = 2 + NT % 2
    FLIP = round(NT * REST / UNITS)

    RB = 3

    def entries(h, kt, ahead=2, first=False):
        if kt < FLIP:
            lo, hi = AHEAD + REST * kt // FLIP, AHEAD + REST * (kt + 1) // FLIP
            found = [("unit", 1, u) for u in range(lo, hi)]
        else:
            m = NT - FLIP
            lo, hi = AHEAD * (kt - FLIP) // m, AHEAD * (kt - FLIP + 1) // m
            found = [("unit", 2, u) for u in range(lo, hi)]
        found = [f for f in found if f[1] <= ahead]
        if kt == FLIP + 1 and ahead >= 1:
            found.append(("max", 1, 0))
        if kt == 2 and not first:
            found.insert(1 if found else 0, ("out", -1, 0))
        return [(kind, h + d, u) for kind, d, u in found]

    PER = UNITS + 2
    LEAD = UNITS + 1 + AHEAD

    lead = ([("unit", 0, u) for u in range(UNITS)] + [("unit", 1, u) for u in range(6)] + [("max", 0, 0)]
            + [("unit", 1, u) for u in range(6, AHEAD)])

    def first_entry(h):
        if isinstance(h, int) and h == 0:
            return LEAD
        if isinstance(h, int) and h == NH - 1:
            return LEAD - 1 + PER * (NH - 2) + REST + 2
        return PER * h + (LEAD - 1)

    assert PER % RB == 0 and (LEAD - 1) % RB == 0

    def entry_of_last_unit(h):
        if isinstance(h, int) and h == 0:
            return UNITS
        if isinstance(h, int) and h == 1:
            return LEAD + REST
        return steady_entry(h - 1) + (REST + 1)

    def steady_entry(h):
        return PER * h + (LEAD - 1)

    before_max = sum(len(entries(0, kt)) for kt in range(FLIP + 2)) - 1

    def entry_of_max(h):
        if isinstance(h, int) and h == 0:
            return lead.index(("max", 0, 0))
        if isinstance(h, int) and h == 1:
            return LEAD + before_max - 1
        if isinstance(h, int) and h == NH - 1:
            return steady_entry(h - 1) + REST + 1
        return steady_entry(h - 1) + before_max

    out_at = len(entries(0, 0)) + len(entries(0, 1)) + 1
    def entry_of_out(h):
        if isinstance(h, int) and h == NH - 1:
            return first_entry(NH - 1) + 1
        if isinstance(h, int) and h == NH - 2:
            return first_entry(NH - 1)
        return steady_entry(h + 1) + out_at

    with stage(nc, name, ["q_in0", "q_in1", "q_in2", "v_in", "q_rows", "k_rows", "consts", "scores", "probs", "pv",
                          "ring_in", "ring_out", "neg_max", "split", "m_in", "acc_out", "rsum", "mask_in", "v_ready", "v_out", "v_set",
                          "c_ready", "c_full", "c_hi", "c_rest", "c_mid", "c_low"],
               [("q", [P, RING, TOK], BF16), ("k", [P, RING, NT * P], BF16), ("v", [P, RING, NT, 2 * DH], F32),
                ("p", [P, PB, 2, 2 * BANK], F32), ("mx", [P, 2, TT, CH], F32), ("nm", [P, TT], F32),
                ("rest", [P, 2, TT], F32), ("mparts", [P, P // TT, TT], BF16), ("mt", [3 * TT, P], BF16),
                ("o_t", [P, BANK], F32), ("rs", [P, TT], F32)],
               [("s", [P, 2, 2, BANK], F32), ("ring", [P, RB, BANK], F32), ("acc", [P, BANK], F32)]) as (s, b, block):
        q_in = [s.q_in0, s.q_in1, s.q_in2]

        def split_chunk(eng, ops, of):
            def low_part(i):
                j, c0, cs = blocks[i]
                eng.wait_ge(s.c_mid, i + 1)
                eng.wait_ge(s.c_rest, min(i + 1, of[-1]) + 1)
                ops.tensor_tensor(part[:, j, 2, c0:c0 + cs], remains(i)[:, 0:cs], part[:, j, 1, c0:c0 + cs], ALU.subtract).then_inc(s.c_low, 1)

            for i in of:
                j, c0, cs = blocks[i]
                eng.wait_ge(s.c_full, i + 1)
                eng.wait_ge(s.c_hi, i + 1)
                if i >= 2:
                    eng.wait_ge(s.c_low, i - 1 if i > of[0] else i)
                ops.tensor_tensor(remains(i)[:, 0:cs], full(i)[:, 0:cs], part[:, j, 0, c0:c0 + cs], ALU.subtract).then_inc(s.c_rest, 1)
                if i > of[0]:
                    low_part(i - 1)
            low_part(of[-1])

        def full(i):
            return b.p[:, 0, i % 4 // 2, i % 2 * BANK:(i % 2 + 1) * BANK]

        def remains(i):
            return b.p[:, 1, i % 4 // 2, i % 2 * BANK:(i % 2 + 1) * BANK]
        LOAD = 6 * 16
        CONSTS = 2 + (NT if keep is not None else 0)

        def load_head(sp, h, r):
            qs = g.q_scr[:, bass.ds(h * DH, DH), :]
            ks = g.k_scr[:, bass.ds(h * DH, DH), 0:n]
            sp.dma_start(b.q[0:48, r, :], qs[0:1].broadcast_to([3, DH, TOK])).then_inc(q_in[r], 16)
            sp.dma_start(b.q[48:80, r, :], qs[1:2].broadcast_to([2, DH, TOK])).then_inc(q_in[r], 16)
            sp.dma_start(b.q[80:96, r, :], qs[2:3]).then_inc(q_in[r], 16)
            sp.dma_start(b.k[0:48, r, 0:n], ks).then_inc(q_in[r], 16)
            sp.dma_start(b.k[48:80, r, 0:n], ks[0:2]).then_inc(q_in[r], 16)
            sp.dma_start(b.k[80:96, r, 0:n], ks[0:1]).then_inc(q_in[r], 16)

        def max_rows(sp, h, r):
            sp.wait_ge(s.ring_out, entry_of_max(h) + 1)
            sp.dma_start(b.q[ONEROWS:ROWS, r, :].rearrange("i (t c) -> i t c", t=TT), b.mt[:, :]).then_inc(s.m_in, 16)

        @block.sync
        def _(sp):
            for sem in stored[0:2]:
                sp.wait_ge(sem, 16)
            load_head(sp, 0, 0)
            sp.wait_ge(s.q_rows, 1)
            sp.wait_ge(s.k_rows, 2)
            if mask_row is not None:
                for r in range(RING):
                    sp.dma_start(b.k[MASKROW:MASKROW + 1, r, 0:n], mask_row).then_inc(s.mask_in, 16)
            for h in range(1, RING):
                load_head(sp, h, h)
            for group in also:
                start_loads(nc, sp, group)
            for j, (_, width, scr) in enumerate(jobs_in):
                sp.wait_ge(s.c_mid, ends[j])
                sp.wait_ge(s.c_low, ends[j])
                sp.dma_start(scr[:, P:2 * P, 0:width].rearrange("i p n -> p i n"), part[:, j, :, 0:width]).then_inc(stored[2 + j], 16)
            for sem in stored[2:4]:
                sp.wait_ge(sem, 16)
            max_rows(sp, 0, 0)
            def body(h, r):
                max_rows(sp, h + 1, (r + 1) % RING)
                sp.wait_ge(s.pv, NT * (h + 1))
                load_head(sp, h + RING, r)
            with sp.Fori(0, 4) as i:
                for r in range(RING):
                    body(i * RING + r, r)
            body(NH - 4, (NH - 4) % RING)
            for h in range(NH - 3, NH - 1):
                max_rows(sp, h + 1, (h + 1) % RING)
            sp.wait_ge(s.m_in, 16 * NH)

        @block.gpsimd
        def _(pool):
            nc.gpsimd.memset(b.k[PARTS:ROWS, :, :].bitcast(F32), TWO_ONES).then_inc(s.k_rows, 1)
            pool.wait_ge(s.k_rows, 1)
            nc.gpsimd.memset(b.k[MASKROW:MASKROW + 1, :, :].bitcast(F32), 0.0).then_inc(s.k_rows, 1)
            pool.wait_ge(s.k_rows, 2)
            if n % P:
                nc.gpsimd.memset(v_all[:, :, NT - 1, :], 0.0).then_inc(s.v_set, 1)
                pool.wait_ge(s.v_set, 1)
            nc.gpsimd.memset(b.mparts[:, 3:, :], 0.0).then_inc(s.consts, 1)
            pool.wait_ge(s.consts, 1)
            nc.gpsimd.memset(b.v[:, :, :, DH:2 * DH], 1.0).then_inc(s.consts, 1)
            pool.wait_ge(s.consts, 2)
            if keep is not None:
                for t, (_, rows) in enumerate(tiles):
                    nc.gpsimd.tensor_scalar(b.v[0:rows, :, t, DH:2 * DH], b.v[0:rows, :, t, DH:2 * DH],
                                            keep[0:rows, t:t + 1], None, ALU.mult).then_inc(s.consts, 1)
                    pool.wait_ge(s.consts, 2 + t + 1)

            split_chunk(pool, nc.gpsimd, range(ends[0], NBL))
            pool.wait_ge(s.c_low, NBL)

            def values(h, r):
                nc.gpsimd.tensor_copy(b.v[:, r, :, 0:DH], v_all[:, bass.ds(h, 1), 0:NT, :].rearrange("p o t d -> p (o t) d")).then_inc(s.v_in, 1)
                pool.wait_ge(s.v_in, h + 1)
            pool.wait_ge(s.v_out, NT)
            for h in range(RING):
                values(h, h)
            with pool.Fori(0, 4) as i:
                for r in range(RING):
                    pool.wait_ge(s.pv, (i * RING + r + 1) * NT)
                    values(i * RING + r + RING, r)
            pool.wait_ge(s.pv, (NH - RING) * NT)
            values(NH - 1, (NH - 1) % RING)

        def pe_scores(h, r, kt, half):
            rows = tiles[kt][1]
            if kt == 0 and half == 0:
                nc.tensor.wait_ge(s.m_in, (h + 1) * 16)
                if isinstance(h, int) and h == 0:
                    nc.tensor.wait_ge(s.v_out, NT)
            if not (isinstance(h, int) and h == 0 and kt == 0):
                nc.tensor.wait_ge(s.probs, h * (2 * NT) + (2 * kt - 1 + half))
            for c in range(2):
                mm = nc.tensor.matmul(b.s[0:rows, half, c, :], b.k[0:ROWS, r, kt * P:kt * P + rows],
                                      b.q[0:ROWS, r, (2 * half + c) * BANK:(2 * half + c + 1) * BANK],
                                      start=True, stop=True)
            mm.then_inc(s.scores, 1)

        def buffer(r, kt):
            return (r * NT + kt) % PB

        def pe_pv(h, r, kt):
            rows = tiles[kt][1]
            nc.tensor.wait_ge(s.probs, h * (2 * NT) + (2 * kt + 2))
            if kt == 0:
                nc.tensor.wait_ge(s.v_in, h + 1)
                if not (isinstance(h, int) and h == 0):
                    nc.tensor.wait_ge(s.acc_out, h)
            for j in range(4):
                mm = nc.tensor.matmul(b.acc[32 * j:32 * j + 2 * DH, :], b.v[0:rows, r, kt, :], b.p[0:rows, buffer(r, kt), j // 2, (j % 2) * BANK:(j % 2 + 1) * BANK],
                                      start=(kt == 0), stop=(kt == NT - 1))
            mm.then_inc(s.pv, 1)

        def pe_entry(e, n, bank):
            kind, h, u = e
            if not (isinstance(n, int) and n < RB):
                nc.tensor.wait_ge(s.ring_out, n - (RB - 1))
            if kind == "unit":
                t, (c0, cs) = u // CH, chunks[u % CH]
                r = slot[0]
                nc.tensor.matmul(b.ring[:, bank, 0:cs], b.q[0:ONEROWS, r, t * P:(t + 1) * P], b.k[0:ONEROWS, r, c0:c0 + cs],
                                 start=True, stop=True).then_inc(s.ring_in, 1)
            elif kind == "max":
                nc.tensor.wait_ge(s.split, 5 * (h + 1))
                nc.tensor.transpose(b.ring[:, bank, 0:P // 2].bitcast(BF16), b.mparts[:, :, :].rearrange("p i t -> p (i t)"),
                                    g.ident_b[:, :]).then_inc(s.ring_in, 1)
            else:
                nc.tensor.wait_ge(s.acc_out, h + 1)
                for c in range(4):
                    mm = nc.tensor.transpose(b.ring[:, bank, c * P:(c + 1) * P], b.o_t[:, c * P:(c + 1) * P], g.ident[:, :])
                mm.then_inc(s.ring_in, 1)

        def pe_loaded(r, turn):
            nc.tensor.wait_ge(q_in[r], turn * LOAD)

        slot = [0]

        @block.tensor
        def _(pe):
            loaded(pe, group)

            def project_values(t, k):
                c0, rows = tiles[t]
                o = b.s[0:rows, 0, t % 2, 0:D]
                if t >= 2 and k == 0:
                    pe.wait_ge(s.v_out, t - 1)
                nc.tensor.matmul(o, kvT[:, k, c0:c0 + rows], w[:, 2, k, :], start=(k == 0), stop=False)
                if k == KC - 1:
                    nc.tensor.matmul(o, g.ones[0:1, 0:rows], vbias[0:1, :], start=False, stop=True).then_inc(s.v_ready, 1)

            def project_chunk(i, k):
                j, c0, cs = blocks[i]
                if i >= 2 and k == 0:
                    pe.wait_ge(s.c_hi, i - 1)
                mm = nc.tensor.matmul(b.s[:, 1, i % 2, 0:cs], w[:, j, k, P:2 * P], jobs_in[j][0][:, k, c0:c0 + cs],
                                      start=(k == 0), stop=(k == KC - 1))
                if k == KC - 1:
                    mm.then_inc(s.c_ready, 1)

            for i in range(ends[0]):
                for k in range(KC):
                    project_chunk(i, k)
            for t in range(EARLY):
                for k in range(KC):
                    project_values(t, k)
            pe.wait_ge(s.q_rows, 1)
            pe.wait_ge(s.k_rows, 2)
            if mask_row is not None:
                pe.wait_ge(s.mask_in, 16 * RING)
            pe_loaded(0, 1)
            pieces = ([(project_chunk, i, k) for i in range(ends[0], NBL) for k in range(KC)]
                      + [(project_values, t, k) for t in range(EARLY, NT) for k in range(KC)])
            for i, e in enumerate(lead):
                if e == ("unit", 1, 0):
                    pe_loaded(1, 1)
                if e[0] == "max":
                    pe.wait_ge(s.consts, CONSTS)
                slot[0] = e[1]
                pe_entry(e, i, i % RB)
                if i % 2 and i // 2 < len(pieces):
                    project, at, k = pieces[i // 2]
                    project(at, k)

            def head(h, r, turns, first=False, ahead=2):
                n0 = first_entry(h)
                bank0 = n0 % RB if isinstance(n0, int) else 0
                i = 0
                for kt in range(NT):
                    todo = entries(h, kt, ahead, first)
                    slot[0] = (r + (1 if kt < FLIP else 2)) % RING
                    if kt == FLIP and ahead == 2:
                        pe_loaded(slot[0], turns)
                    share = [(len(todo) - 1) // 2, len(todo) // 2, len(todo)]
                    for part in range(3):
                        if part < 2:
                            pe_scores(h, r, kt, part)
                        elif kt:
                            pe_pv(h, r, kt - 1)
                        elif not first:
                            pe_pv(h - 1, (r - 1) % RING, NT - 1)
                        for e in todo[:share[part]]:
                            pe_entry(e, n0 + i, (bank0 + i) % RB)
                            i += 1
                        todo = todo[share[part]:]

            head(0, 0, 1, first=True)
            with pe.Fori(0, 4) as i:
                for j in range(RING):
                    head(i * RING + (j + 1), (j + 1) % RING, i + ((j + 3) // RING + 1))
            head(NH - 3, (NH - 3) % RING, (NH - 1) // RING + 1)
            head(NH - 2, (NH - 2) % RING, 0, ahead=1)
            head(NH - 1, (NH - 1) % RING, 0, ahead=0)
            pe_pv(NH - 1, (NH - 1) % RING, NT - 1)
            last = entry_of_out(NH - 1)
            pe_entry(("out", NH - 1, 0), last, last % RB)

        @block.scalar
        def _(act):
            def copy_acc(h):
                act.wait_ge(s.pv, (h + 1) * NT)
                if not (isinstance(h, int) and h == 0):
                    act.wait_ge(s.ring_in, entry_of_out(h - 1) + 1)
                nc.scalar.activation(b.o_t[:, :], b.acc[:, :], ACT.Copy).then_inc(s.acc_out, 1)

            def head(h, r, first=False):
                for kt in range(NT):
                    rows = tiles[kt][1]
                    for half in range(2):
                        act.wait_ge(s.scores, h * (2 * NT) + (2 * kt + half + 1))
                        if kt >= PB or not first:
                            act.wait_ge(s.pv, h * NT + (kt - PB + 1))
                        nc.scalar.activation(b.p[0:rows, buffer(r, kt), half, :].rearrange("p (c n) -> p c n", c=2), b.s[0:rows, half, :, :],
                                             ACT.Exp, scale=SCALE).then_inc(s.probs, 1)
                    if kt == 0 and not first:
                        copy_acc(h - 1)

            def middle_part(i):
                j, c0, cs = blocks[i]
                act.wait_ge(s.c_rest, i + 1)
                nc.scalar.activation(part[:, j, 1, c0:c0 + cs], remains(i)[:, 0:cs], ACT.Copy).then_inc(s.c_mid, 1)

            def chunk_out(i):
                j, c0, cs = blocks[i]
                act.wait_ge(s.c_ready, i + 1)
                if i >= 4:
                    act.wait_ge(s.c_rest, i - 3)
                if i == 0 or i == ends[0]:
                    act.wait_ge(stored[j], 16)
                ps, col = b.s[:, 1, i % 2, 0:cs], bias[:, j, 1:2]
                nc.scalar.activation(full(i)[:, 0:cs], ps, ACT.Identity, bias=col).then_inc(s.c_full, 1)
                nc.scalar.activation(part[:, j, 0, c0:c0 + cs], ps, ACT.Identity, bias=col).then_inc(s.c_hi, 1)

            def values_out(t):
                rows = tiles[t][1]
                act.wait_ge(s.v_ready, t + 1)
                o = v_all[0:rows, :, t, :]
                ps = b.s[0:rows, 0, t % 2, 0:D].rearrange("p (h d) -> p h d", h=NH)
                if keep is None:
                    nc.scalar.activation(o, ps, ACT.Copy).then_inc(s.v_out, 1)
                else:
                    nc.scalar.activation(o, ps, ACT.Identity, scale=keep[0:rows, t:t + 1]).then_inc(s.v_out, 1)

            for i in range(ends[0]):
                chunk_out(i)
                if i:
                    middle_part(i - 1)
            middle_part(ends[0] - 1)
            if n % P:
                act.wait_ge(s.v_set, 1)
            for t in range(EARLY):
                values_out(t)
            for i in range(ends[0], NBL):
                chunk_out(i)
                if i > ends[0]:
                    middle_part(i - 1)
            middle_part(NBL - 1)
            for t in range(EARLY, NT):
                values_out(t)
            act.wait_ge(s.c_low, NBL)
            head(0, 0, first=True)
            with act.Fori(0, 4) as i:
                for j in range(RING):
                    head(i * RING + (j + 1), (j + 1) % RING)
            for h in range(NH - 3, NH):
                head(h, h % RING)
            copy_acc(NH - 1)

        @block.vector
        def _(dve):
            def unit(n, bank, u):
                t, (c0, cs) = u // CH, chunks[u % CH]
                nc.vector.tensor_reduce(b.mx[:, 0 if u < AHEAD else 1, t, u % CH:u % CH + 1], b.ring[:, bank, 0:cs], AX.X, ALU.max).then_inc(s.ring_out, 1)

            def first_units_max(h, n):
                dve.wait_ge(s.ring_out, n - 1)
                nc.vector.tensor_reduce(b.nm[:, 0:AHEAD // CH], b.mx[:, 0, 0:AHEAD // CH, :], AX.X, ALU.max, negate=True).then_inc(s.neg_max, 1)

            def split_max(h, step):
                if step == 0:
                    dve.wait_ge(s.ring_out, entry_of_last_unit(h))
                    nc.vector.tensor_reduce(b.nm[:, AHEAD // CH:], b.mx[:, 1, AHEAD // CH:, :], AX.X, ALU.max, negate=True).then_inc(s.neg_max, 1)
                elif step == 1:
                    dve.wait_ge(s.neg_max, 2 * (h + 1))
                    nc.vector.tensor_copy(b.mparts[:, 0, :], b.nm[:, :]).then_inc(s.split, 1)
                elif step == 2:
                    dve.wait_ge(s.split, 5 * h + 1)
                    nc.vector.tensor_tensor(b.rest[:, 0, :], b.nm[:, :], b.mparts[:, 0, :], ALU.subtract).then_inc(s.split, 1)
                elif step == 3:
                    dve.wait_ge(s.split, 5 * h + 2)
                    nc.vector.tensor_copy(b.mparts[:, 1, :], b.rest[:, 0, :]).then_inc(s.split, 1)
                elif step == 4:
                    dve.wait_ge(s.split, 5 * h + 3)
                    nc.vector.tensor_tensor(b.rest[:, 1, :], b.rest[:, 0, :], b.mparts[:, 1, :], ALU.subtract).then_inc(s.split, 1)
                elif step == 5:
                    dve.wait_ge(s.split, 5 * h + 4)
                    nc.vector.tensor_copy(b.mparts[:, 2, :], b.rest[:, 1, :]).then_inc(s.split, 1)
            STEPS = 6

            def copy_max(h, bank):
                if not (isinstance(h, int) and h == 0):
                    dve.wait_ge(s.m_in, h * 16)
                nc.vector.tensor_copy(b.mt[:, :], b.ring[0:3 * TT, bank, 0:P // 2].bitcast(BF16)).then_inc(s.ring_out, 1)

            def normalise(h, bank):
                tv = b.ring[:, bank, :].rearrange("p (c j d) -> p c j d", c=4, j=4)
                rs = b.rs[:, :].rearrange("p (c j) -> p c j", c=4)
                nc.vector.reciprocal(rs, tv[:, :, :, DH]).then_inc(s.rsum, 1)
                dve.wait_ge(s.rsum, h + 1)
                o = out[:, :, bass.ds(h * DH, DH)].rearrange("p (j c) d -> p c j d", j=4)
                nc.vector.tensor_tensor(o, tv[:, :, :, 0:DH], rs.unsqueeze(3).broadcast_to([P, 4, 4, DH]), ALU.mult).then_inc(s.ring_out, 1)

            def entry(e, n, bank):
                kind, h, u = e
                dve.wait_ge(s.ring_in, n + 1)
                if kind == "unit":
                    unit(n, bank, u)
                    if u == AHEAD + 1:
                        first_units_max(h, n)
                elif kind == "max":
                    copy_max(h, bank)
                else:
                    if not (isinstance(h, int) and h == 0):
                        dve.wait_ge(s.ring_out, entry_of_out(h - 1) + 1)
                    normalise(h, bank)

            def run(todo, n0, bank0):
                step, of = STEPS, None
                for i, e in enumerate(todo):
                    if e[0] == "max":
                        while step < STEPS:
                            split_max(of, step)
                            step += 1
                    entry(e, n0 + i, (bank0 + i) % RB)
                    if step < STEPS:
                        split_max(of, step)
                        step += 1
                    if e[0] == "unit" and e[2] == UNITS - 1:
                        step, of = 0, e[1]

            def head(h, first=False, ahead=2):
                n0 = first_entry(h)
                run([e for kt in range(NT) for e in entries(h, kt, ahead, first)], n0, n0 % RB if isinstance(n0, int) else 0)

            nc.vector.memset(b.q[PARTS:ROWS, :, :].bitcast(F32), TWO_ONES).then_inc(s.q_rows, 1)
            split_chunk(dve, nc.vector, range(ends[0]))
            run(lead, 0, 0)
            head(0, first=True)
            with dve.Fori(0, 4) as i:
                for j in range(RING):
                    head(i * RING + (j + 1))
            head(NH - 3)
            head(NH - 2, ahead=1)
            head(NH - 1, ahead=0)
            last = entry_of_out(NH - 1)
            entry(("out", NH - 1, 0), last, last % RB)



def project_heads(nc, g, name, src, w, biasb, group, next_eps, gate=None, also=()):
    NB, TB = 4, 4
    jobs = [(q, k) for q in range(TT // 4) for k in range(KC)]
    with stage(nc, name, ["turned", "out_dve", "out_act", "ready", "gated", "biased", "done"] + STAT_SEMS,
               [("t", [P, KC, TOK], F32)], [("ps", [P, NB, BANK], F32), ("tp", [P, TB, BANK], F32)]) as (s, b, block):
        @block.sync
        def _(sp):
            for other in also:
                start_loads(nc, sp, other)

        @block.vector
        def _(dve):
            loaded(dve, group)
            if gate is not None:
                for k in range(KC):
                    nc.vector.tensor_tensor(w[:, k, :], w[:, k, :], gate[:, :], ALU.mult).then_inc(s.gated, 1)
                nc.vector.tensor_tensor(biasb[:, :], biasb[:, :], gate[:, :], ALU.mult).then_inc(s.gated, 1)
                dve.wait_ge(s.gated, KC + 1)
            for j in range(0, len(jobs), 2):
                q, k = jobs[j]
                dve.wait_ge(s.turned, j + 1)
                nc.vector.tensor_copy(b.t[:, k, q * BANK:(q + 1) * BANK], b.tp[:, j % TB, :]).then_inc(s.out_dve, 1)
            nc.vector.tensor_tensor(g.x[:, :, :], g.x[:, :, :], biasb[:, :].unsqueeze(1).broadcast_to([P, TT, D]), ALU.add).then_inc(s.biased, 1)
            dve.wait_ge(s.biased, 1)
            for t in range(TT + 2):
                if t < TT:
                    dve.wait_ge(s.ready, t + 1)
                    nc.vector.tensor_tensor(g.x[:, t, :], g.x[:, t, :], b.ps[:, t % NB, 0:D], ALU.add).then_inc(s.done, 1)
                tile_statistics(nc, g, dve, s, t)
            finish_statistics_dve(nc, g, dve, s, next_eps)

        @block.scalar
        def _(act):
            for j in range(1, len(jobs), 2):
                q, k = jobs[j]
                act.wait_ge(s.turned, j + 1)
                nc.scalar.activation(b.t[:, k, q * BANK:(q + 1) * BANK], b.tp[:, j % TB, :], ACT.Copy).then_inc(s.out_act, 1)
            finish_statistics_act(nc, g, act, s)

        @block.tensor
        def _(pe):
            loaded(pe, group)

            def turn(j):
                q, k = jobs[j]
                if j >= TB:
                    pe.wait_ge(s.out_act if j % 2 else s.out_dve, (j - TB) // 2 + 1)
                for t in range(4):
                    mm = nc.tensor.transpose(b.tp[:, j % TB, t * P:(t + 1) * P], src[:, 4 * q + t, k * P:(k + 1) * P], g.ident[:, :])
                mm.then_inc(s.turned, 1)

            for j in range(len(jobs)):
                turn(j)
            if gate is not None:
                pe.wait_ge(s.gated, KC + 1)
            for t in range(TT):
                pe.wait_ge(s.out_dve, t // 4 + 1)
                pe.wait_ge(s.out_act, t // 4 + 1)
                if t >= NB:
                    pe.wait_ge(s.done, t - NB + 1)
                for k in range(KC):
                    mm = nc.tensor.matmul(b.ps[:, t % NB, 0:D], b.t[:, k, t * P:(t + 1) * P], w[:, k, :], start=(k == 0), stop=(k == KC - 1))
                mm.then_inc(s.ready, 1)



def plain_projections(nc, g, name, jobs_in, tok_x, tok_n, tok_dst, w_all, group):
    blocks = [(w, m, c0, cs) for w in range(len(jobs_in)) for m in range(KC) for c0, cs in cut(jobs_in[w][1], BANK)]
    NB, NW, first_tok = 8, len(jobs_in), len(blocks)
    tiles = cut(tok_n, P)
    with stage(nc, name, ["ready", "out_act", "out_dve"], [],
               [("ps", [P, NB, BANK], F32)]) as (s, b, block):
        def bank_free(eng, j):
            if j >= NB:
                eng.wait_ge(s.out_act if j % 2 else s.out_dve, (j - NB) // 2 + 1)

        def job_out(j):
            if j < first_tok:
                w, m, c0, cs = blocks[j]
                return jobs_in[w][2][:, m, c0:c0 + cs], b.ps[:, j % NB, 0:cs]
            t = j - first_tok
            return tok_dst[0:tiles[t][1], t, :], b.ps[0:tiles[t][1], j % NB, 0:D]
        total = first_tok + len(tiles)

        @block.tensor
        def _(pe):
            loaded(pe, group)
            for j, (w, m, c0, cs) in enumerate(blocks):
                bank_free(pe, j)
                for k in range(KC):
                    mm = nc.tensor.matmul(b.ps[:, j % NB, 0:cs], w_all[:, w, k, m * P:(m + 1) * P], jobs_in[w][0][:, k, c0:c0 + cs],
                                          start=(k == 0), stop=(k == KC - 1))
                mm.then_inc(s.ready, 1)
            for t, (c0, r) in enumerate(tiles):
                j = first_tok + t
                bank_free(pe, j)
                for k in range(KC):
                    mm = nc.tensor.matmul(b.ps[0:r, j % NB, 0:D], tok_x[:, k, c0:c0 + r], w_all[:, NW, k, :], start=(k == 0), stop=(k == KC - 1))
                mm.then_inc(s.ready, 1)

        @block.vector
        def _(dve):
            for j in range(0, total, 2):
                dve.wait_ge(s.ready, j + 1)
                nc.vector.tensor_copy(*job_out(j)).then_inc(s.out_dve, 1)

        @block.scalar
        def _(act):
            for j in range(1, total, 2):
                act.wait_ge(s.ready, j + 1)
                nc.scalar.activation(*job_out(j), ACT.Copy).then_inc(s.out_act, 1)


def prototype_attention(nc, g, name, qT, kT, v, evT, also=()):
    tiles = cut(CTX, P)
    CH = 4
    chunks = cut(CTX, -(-CTX // CH))
    groups = cut(CT, 4)
    NG = len(groups)
    assert NG == CH
    QB = BANK // P
    NBLK = TT // QB
    SCALE = float(D) ** -0.5
    with stage(nc, name, ["scores", "maxed", "neg", "bias", "exped", "summed", "recip", "normed", "turned",
                          "pt_dve", "pt_act", "ev", "ev_out"],
               [("mx", [P, 2, CH], F32), ("nm", [P, 2], F32), ("nb", [P, 2], F32), ("sm", [P, 2, CH], F32), ("rs", [P, 2, 2], F32),
                ("p", [P, 2, CTX], F32), ("pt", [P, CT, BANK], F32)],
               [("s", [P, CH, BANK], F32), ("t", [P, 2, BANK], F32), ("e", [P, 2, BANK], F32)]) as (s, b, block):
        def after_block(t):
            return t > 1 and (t - 1) % QB == 0

        def copied(eng, n):
            if n > 0:
                eng.wait_ge(s.pt_dve, (n + 1) // 2)
            if n > 1:
                eng.wait_ge(s.pt_act, n // 2)

        def copy_turned(eng, t, i):
            n = t * NG + i
            k0, m = groups[i]
            eng.wait_ge(s.turned, n + 1)
            if t % QB == 0 and t:
                eng.wait_ge(s.ev, KC * (t // QB))
            q = (t % QB) * P
            full = sum(1 for _, r in tiles[k0:k0 + m] if r == P)
            outs = []
            if full:
                outs.append((b.pt[:, k0:k0 + full, q:q + P], b.t[:, n % 2, 0:full * P].rearrange("p (k c) -> p k c", k=full)))
            if full < m:
                r = tiles[k0 + full][1]
                outs.append((b.pt[0:r, k0 + full, q:q + P], b.t[0:r, n % 2, full * P:(full + 1) * P]))
            return outs

        @block.sync
        def _(sp):
            for group in also:
                start_loads(nc, sp, group)

        @block.tensor
        def _(pe):
            def scores(t, c):
                c0, cs = chunks[c]
                if t:
                    pe.wait_ge(s.exped, CH * (t - 1) + c + 1)
                for k in range(KC):
                    mm = nc.tensor.matmul(b.s[:, c, 0:cs], qT[:, k, t * P:(t + 1) * P], kT[:, k, c0:c0 + cs],
                                          start=(k == 0), stop=(k == KC - 1))
                mm.then_inc(s.scores, 1)

            def turn(t, i):
                pe.wait_ge(s.normed, t + 1)
                copied(pe, t * NG + i - 1)
                k0, m = groups[i]
                for q in range(m):
                    c0, r = tiles[k0 + q]
                    mm = nc.tensor.transpose(b.t[0:r, (t * NG + i) % 2, q * P:(q + 1) * P], b.p[:, t % 2, c0:c0 + r], g.ident[:, :])
                mm.then_inc(s.turned, 1)

            def evidence(blk):
                copied(pe, (blk + 1) * QB * NG)
                for m in range(KC):
                    if blk:
                        pe.wait_ge(s.ev_out, KC * (blk - 1) + m + 1)
                    for k, (_, r) in enumerate(tiles):
                        mm = nc.tensor.matmul(b.e[:, m, :], v[0:r, k, m * P:(m + 1) * P], b.pt[0:r, k, :], start=(k == 0), stop=(k == CT - 1))
                    mm.then_inc(s.ev, 1)

            for t in range(TT + 1):
                for c in range(CH):
                    if t < TT:
                        scores(t, c)
                    if c == 2 and after_block(t):
                        evidence((t - 1) // QB - 1)
                    if t and c >= 2:
                        for i in ([0] if c == 2 else range(1, NG)):
                            turn(t - 1, i)
            evidence(NBLK - 1)

        @block.vector
        def _(dve):
            def maximum(t, c):
                dve.wait_ge(s.scores, CH * t + c + 1)
                nc.vector.tensor_reduce(b.mx[:, t % 2, c:c + 1], b.s[:, c, 0:chunks[c][1]], AX.X, ALU.max).then_inc(s.maxed, 1)

            def copy_out(t, n):
                for o, src in copy_turned(dve, t, n):
                    ins = nc.vector.tensor_copy(o, src)
                ins.then_inc(s.pt_dve, 1)

            def block_out(blk):
                for m in range(KC):
                    dve.wait_ge(s.ev, KC * blk + m + 1)
                    nc.vector.tensor_copy(evT[:, m, blk * BANK:(blk + 1) * BANK], b.e[:, m, :]).then_inc(s.ev_out, 1)

            for t in range(TT + 1):
                i = t % 2
                if t < TT:
                    maximum(t, 0)
                    maximum(t, 1)
                    maximum(t, 2)
                if after_block(t):
                    block_out((t - 1) // QB - 1)
                if t:
                    copy_out(t - 1, 0)
                if t < TT:
                    maximum(t, 3)
                    dve.wait_ge(s.maxed, CH * (t + 1))
                    nc.vector.tensor_reduce(b.nm[:, i:i + 1], b.mx[:, i, :], AX.X, ALU.max, negate=True).then_inc(s.neg, 1)
                    dve.wait_ge(s.neg, t + 1)
                    nc.vector.tensor_scalar(b.nb[:, i:i + 1], b.nm[:, i:i + 1], SCALE, None, ALU.mult).then_inc(s.bias, 1)
                if t:
                    copy_out(t - 1, 2)
                if t < TT:
                    dve.wait_ge(s.exped, CH * (t + 1))
                    nc.vector.tensor_reduce(b.rs[:, i, 0:1], b.sm[:, i, :], AX.X, ALU.add).then_inc(s.summed, 1)
                    dve.wait_ge(s.summed, t + 1)
                    nc.vector.reciprocal(b.rs[:, i, 1:2], b.rs[:, i, 0:1]).then_inc(s.recip, 1)
                    dve.wait_ge(s.recip, t + 1)
                    nc.vector.tensor_scalar(b.p[:, i, :], b.p[:, i, :], b.rs[:, i, 1:2], None, ALU.mult).then_inc(s.normed, 1)
            block_out(NBLK - 1)

        @block.scalar
        def _(act):
            def copy_out(t, n):
                for o, src in copy_turned(act, t, n):
                    ins = nc.scalar.activation(o, src, ACT.Copy)
                ins.then_inc(s.pt_act, 1)

            for t in range(TT + 1):
                i = t % 2
                if t:
                    copy_out(t - 1, 1)
                if t < TT:
                    act.wait_ge(s.bias, t + 1)
                    if t >= 2:
                        act.wait_ge(s.turned, NG * (t - 1))
                    for c, (c0, cs) in enumerate(chunks):
                        nc.scalar.activation(b.p[:, i, c0:c0 + cs], b.s[:, c, 0:cs], ACT.Exp, bias=b.nb[:, i:i + 1], scale=SCALE,
                                             accum_out=b.sm[:, i, c:c + 1]).then_inc(s.exped, 1)
                if t:
                    copy_out(t - 1, 3)


def experts(nc, g, name, nxT, evT, routed, g1T, w1, w2, gw, rw, b1, b2, rb, early, w2_in, late, also):
    E, RH = 3, 512
    CK = 3 * D // P
    XK = 2 * D // P
    MC = RH // P
    NBLK = TOK // BANK
    TB = BANK // P
    comb = [nxT[:, 0], nxT[:, 1], evT[:, 0], evT[:, 1]]
    NCOL = E * MC + KC
    units = [(nb, e) for nb in range(NBLK) for e in range(E + 1)]
    rows_of = lambda e: MC if e < E else KC
    hidden = [(u, m) for u in range(len(units)) for m in range(rows_of(units[u][1]))]
    outs = [(u, q) for u in range(len(units)) if units[u][1] < E for q in range(TB)]
    HB, OB = 3, 3
    hid_end = [sum(rows_of(e) for _, e in units[:u + 1]) for u in range(len(units))]
    out_end = [TB * sum(1 for _, e in units[:u + 1] if e < E) for u in range(len(units))]
    exp_units = [u for u in range(len(units)) if units[u][1] < E]
    with stage(nc, name, ["cols", "bias_set", "init", "row_set", "anchor_b", "rows_ready", "rows_out", "logits", "dve", "exped", "hid", "act_out", "ready", "done"],
               [("bias", [P, NCOL], F32), ("anchor", [P, KC, P], F32), ("row", [P, E], F32), ("rows", [P, BANK], F32), ("lg", [P, TT, E], F32), ("red", [P, 3, TT], F32),
                ("prob", [P, TT, E], F32), ("h", [P, 2, MC, BANK], F32)],
               [("hp", [P, HB, BANK], F32), ("op", [P, OB, BANK], F32), ("sp", [P, BANK], F32), ("cp", [P, BANK], F32)]) as (s, b, block):
        @block.sync
        def _(sp):
            for group in (w2_in, *late, *also):
                start_loads(nc, sp, group)

        @block.tensor
        def _(pe):
            def anchor_columns(e):
                for m in range(rows_of(e)):
                    c = e * MC + m
                    w = (w1[e] if e < E else gw)[:, :, m * P:(m + 1) * P]
                    for k in range(XK, CK):
                        mm = nc.tensor.matmul(b.cp[:, c:c + 1], w[:, k, :], g.cond[:, k - XK:k - XK + 1], start=(k == XK), stop=(k == CK - 1))
                mm.then_inc(s.cols, 1)

            loaded(pe, early)
            pe.wait_ge(s.anchor_b, KC)
            for k in range(XK, CK):
                nc.tensor.matmul(b.sp[:, 0:E], b.anchor[:, k - XK, :], rw[:, k, 0:E], start=(k == XK), stop=False)
            nc.tensor.matmul(b.sp[:, 0:E], g.ones[0:1, :], rb[0:1, :], start=False, stop=True)
            for k in range(XK):
                for j in range(NBLK):
                    mm = nc.tensor.matmul(b.op[32 * j:32 * (j + 1), 0, :], rw[:, k, 0:32], comb[k][:, j * BANK:(j + 1) * BANK],
                                          start=(k == 0), stop=(k == XK - 1))
            mm.then_inc(s.rows_ready, 1)
            pe.wait_ge(s.rows_out, 1)
            for c in range(TB):
                mm = nc.tensor.transpose(b.op[:, 1, c * P:(c + 1) * P], b.rows[:, c * P:(c + 1) * P], g.ident[:, :])
            mm.then_inc(s.logits, 1)

            n_hid = 0
            n_out = 0

            def first_layer(u, n):
                nb, e = units[u]
                if nb == 0:
                    if e > 0:
                        loaded(pe, late[e - 1])
                    if e:
                        pe.wait_ge(s.bias_set, e)
                    anchor_columns(e)
                for m in range(rows_of(e)):
                    if n >= HB:
                        pe.wait_ge(s.act_out, n - HB + 1)
                    for k in range(XK):
                        w = (w1[e] if e < E else gw)[:, k, m * P:(m + 1) * P]
                        mm = nc.tensor.matmul(b.hp[:, n % HB, :], w, comb[k][:, nb * BANK:(nb + 1) * BANK], start=(k == 0), stop=(k == XK - 1))
                    mm.then_inc(s.hid, 1)
                    n += 1
                return n

            def second_layer(u, n):
                e = units[u][1]
                i = exp_units.index(u) % 2
                pe.wait_ge(s.act_out, hid_end[u])
                if n == 0:
                    loaded(pe, w2_in)
                for q in range(TB):
                    if n >= OB:
                        pe.wait_ge(s.done, n - OB + 1)
                    for k in range(MC):
                        mm = nc.tensor.matmul(b.op[:, n % OB, 0:D], b.h[:, i, k, q * P:(q + 1) * P], w2[:, e, k, :], start=(k == 0), stop=(k == MC - 1))
                    mm.then_inc(s.ready, 1)
                    n += 1
                return n

            for u in range(len(units)):
                n_hid = first_layer(u, n_hid)
                if u and units[u - 1][1] < E:
                    n_out = second_layer(u - 1, n_out)

        @block.scalar
        def _(act):
            act.wait_ge(s.dve, 3)
            nc.scalar.activation(b.lg[:, :, :], b.lg[:, :, :], ACT.Exp).then_inc(s.exped, 1)
            for n, (u, m) in enumerate(hidden):
                nb, e = units[u]
                if nb == 0 and m == 0:
                    act.wait_ge(s.bias_set, e + 1)
                act.wait_ge(s.hid, n + 1)
                if e < E:
                    i = exp_units.index(u)
                    if i >= 2:
                        act.wait_ge(s.ready, out_end[exp_units[i - 2]])
                    o = b.h[:, i % 2, m, :]
                else:
                    o = g1T[:, m, nb * BANK:(nb + 1) * BANK]
                c = e * MC + m
                nc.scalar.activation(o, b.hp[:, n % HB, :], ACT.Silu, bias=b.bias[:, c:c + 1]).then_inc(s.act_out, 1)

        @block.vector
        def _(dve):
            for k in range(KC):
                nc.vector.tensor_scalar(b.anchor[:, k, :], g.ones[:, :], g.cond[:, k:k + 1], None, ALU.mult).then_inc(s.anchor_b, 1)
            loaded(dve, early)
            dve.wait_ge(s.rows_ready, 1)
            nc.vector.tensor_copy(b.rows[:, :], b.op[:, 0, :]).then_inc(s.rows_out, 1)
            nc.vector.tensor_copy(b.row[:, :], b.sp[:, 0:E]).then_inc(s.row_set, 1)
            dve.wait_ge(s.row_set, 1)
            dve.wait_ge(s.logits, 1)
            def bias_columns(e):
                c0, c1 = e * MC, e * MC + rows_of(e)
                dve.wait_ge(s.cols, e + 1)
                nc.vector.tensor_tensor(b.bias[:, c0:c1], b1[:, c0:c1], b.cp[:, c0:c1], ALU.add).then_inc(s.bias_set, 1)

            nc.vector.tensor_tensor(b.lg[:, :, :].rearrange("p (j c) e -> p j c e", c=TB),
                                    b.op[:, 1, :].rearrange("p (c j d) -> p j c d", c=TB, j=NBLK)[:, :, :, 0:E],
                                    b.row[:, :].unsqueeze(1).unsqueeze(1).broadcast_to([P, NBLK, TB, E]), ALU.add).then_inc(s.dve, 1)
            dve.wait_ge(s.dve, 1)
            nc.vector.tensor_reduce(b.red[:, 0, :], b.lg[:, :, :], AX.X, ALU.max).then_inc(s.dve, 1)
            dve.wait_ge(s.dve, 2)
            nc.vector.tensor_tensor(b.lg[:, :, :], b.lg[:, :, :], b.red[:, 0, :].unsqueeze(2).broadcast_to([P, TT, E]), ALU.subtract).then_inc(s.dve, 1)
            dve.wait_ge(s.exped, 1)
            nc.vector.tensor_reduce(b.red[:, 1, :], b.lg[:, :, :], AX.X, ALU.add).then_inc(s.dve, 1)
            dve.wait_ge(s.dve, 4)
            nc.vector.reciprocal(b.red[:, 2, :], b.red[:, 1, :]).then_inc(s.dve, 1)
            dve.wait_ge(s.dve, 5)
            nc.vector.tensor_tensor(b.prob[:, :, :], b.lg[:, :, :], b.red[:, 2, :].unsqueeze(2).broadcast_to([P, TT, E]), ALU.mult).then_inc(s.dve, 1)
            dve.wait_ge(s.dve, 6)
            bias_columns(0)
            for e in range(E):
                if e == E - 1:
                    bias_columns(1)
                for t in range(TT):
                    w = b.prob[:, t, e:e + 1]
                    if e == 0:
                        nc.vector.tensor_scalar(routed[:, t, :], b2[:, e, :], w, None, ALU.mult).then_inc(s.init, 1)
                    else:
                        dve.wait_ge(s.init, (e - 1) * TT + t + 1)
                        nc.vector.scalar_tensor_tensor(routed[:, t, :], b2[:, e, :], w, routed[:, t, :], ALU.mult, ALU.add).then_inc(s.init, 1)
            dve.wait_ge(s.init, E * TT)
            for n, (u, q) in enumerate(outs):
                nb, e = units[u]
                if nb == 0 and q == 0 and e:
                    bias_columns(e + 1)
                t = nb * TB + q
                dve.wait_ge(s.ready, n + 1)
                src, w = b.op[:, n % OB, 0:D], b.prob[:, t, e:e + 1]
                if e:
                    dve.wait_ge(s.done, n - TB + 1)
                nc.vector.scalar_tensor_tensor(routed[:, t, :], src, w, routed[:, t, :], ALU.mult, ALU.add).then_inc(s.done, 1)


def gated_output(nc, g, name, routedT, g1T, w, ob, gb, group, next_eps, also=()):
    NB = 4
    with stage(nc, name, ["ready", "gate", "biased", "prod", "done"] + STAT_SEMS,
               [("sg", [P, 2, D], F32), ("ro", [P, 2, D], F32), ("pr", [P, 2, D], F32)],
               [("o", [P, NB, BANK], F32), ("z", [P, NB, BANK], F32)]) as (s, b, block):
        @block.sync
        def _(sp):
            for other in also:
                start_loads(nc, sp, other)

        @block.tensor
        def _(pe):
            loaded(pe, group)
            for t in range(TT):
                if t >= NB:
                    pe.wait_ge(s.prod, t - NB + 1)
                for k in range(KC):
                    nc.tensor.matmul(b.z[:, t % NB, 0:D], g1T[:, k, t * P:(t + 1) * P], w[:, 1, k, :], start=(k == 0), stop=False)
                nc.tensor.matmul(b.z[:, t % NB, 0:D], g.ones[0:1, :], gb[0:1, :], start=False, stop=True)
                for k in range(KC):
                    mm = nc.tensor.matmul(b.o[:, t % NB, 0:D], routedT[:, k, t * P:(t + 1) * P], w[:, 0, k, :], start=(k == 0), stop=(k == KC - 1))
                mm.then_inc(s.ready, 1)

        @block.scalar
        def _(act):
            for t in range(TT):
                act.wait_ge(s.ready, t + 1)
                if t >= 2:
                    act.wait_ge(s.prod, t - 1)
                nc.scalar.activation(b.sg[:, t % 2, :], b.z[:, t % NB, 0:D], ACT.Sigmoid).then_inc(s.gate, 1)
            finish_statistics_act(nc, g, act, s)

        @block.vector
        def _(dve):
            loaded(dve, group)
            for t in range(TT + 2):
                if t < TT:
                    dve.wait_ge(s.ready, t + 1)
                    if t >= 2:
                        dve.wait_ge(s.done, t - 1)
                    nc.vector.tensor_tensor(b.ro[:, t % 2, :], b.o[:, t % NB, 0:D], ob[:, :], ALU.add).then_inc(s.biased, 1)
                    dve.wait_ge(s.biased, t + 1)
                    dve.wait_ge(s.gate, t + 1)
                    nc.vector.tensor_tensor(b.pr[:, t % 2, :], b.sg[:, t % 2, :], b.ro[:, t % 2, :], ALU.mult).then_inc(s.prod, 1)
                    dve.wait_ge(s.prod, t + 1)
                    nc.vector.tensor_tensor(g.x[:, t, :], g.x[:, t, :], b.pr[:, t % 2, :], ALU.add).then_inc(s.done, 1)
                tile_statistics(nc, g, dve, s, t)
            finish_statistics_dve(nc, g, dve, s, next_eps)


def expert_block(nc, g, a, ctxT, next_eps):
    E, RH = 3, 512
    CK, MC = 3 * D // P, RH // P
    with ExitStack() as ctx:
        def t(name, shape, where=ctx):
            return where.enter_context(tile(nc, "L1_" + name, shape))
        nxT, evT, qT, keys = t("nxT", [P, KC, TOK]), t("evT", [P, KC, TOK]), t("qT", [P, KC, TOK]), t("keys", [P, KC * TOK])
        kT = keys[:, 0:KC * CTX].rearrange("p (k n) -> p k n", k=KC)
        routed, g1T = keys[:, :].rearrange("p (t d) -> p t d", d=D), qT
        wo, ob, gb = t("wo", [P, 2, KC, D]), t("ob", [P, D]), t("gb2", [1, D])
        w_out = loads(ctx, nc, "L1_out_in", [(wo[:, 0], by_rows(a.L1_xcond_out_w)), (wo[:, 1], by_rows(a.L1_xcond_gate_w2)),
                                             (ob[:, :], a.L1_xcond_out_b.partition_broadcast(P)), (gb[:, :], as_row(a.L1_xcond_gate_b2))])
        with ExitStack() as ex:
            w1_0, gw = t("w1_0", [P, CK, RH], ex), t("gw", [P, CK, D], ex)
            rw, b1, b2, rb = t("rw", [P, CK, 32], ex), t("b1", [P, E * MC + KC], ex), t("b2", [P, E, D], ex), t("rb", [1, E], ex)
            w_in = loads(ex, nc, "L1_qkv_in", [(gw[:, KC * i:KC * (i + 1)], by_rows(m)) for i, m in enumerate([a.L1_xcond_Wq, a.L1_xcond_Wk, a.L1_xcond_Wv])])
            early = loads(ex, nc, "L1_early", [(w1_0[:, :, :], by_rows(a.L1_xcond_e_w1[0]))]
                          + [(rw[:, :, 0:E], by_rows(a.L1_xcond_router_W)), (b1[:, 0:E * MC], a.L1_xcond_e_b1.rearrange("e (k p) -> p (e k)", p=P)),
                             (b1[:, E * MC:], as_columns(a.L1_xcond_gate_b1)), (rb[:, :], as_row(a.L1_xcond_router_b))]
                          + [(b2[:, e, :], a.L1_xcond_e_b2[e].partition_broadcast(P)) for e in range(E)])
            norm_transpose(nc, g, "L1nx", zeroed=rw, sources=[(g.x, TOK, nxT, (g.mv, g.rs, None), g.affine[:, 0], g.affine[:, 1]),
                                           (g.ctx, CTX, ctxT, None, None, None)], also=[w_in])
            with ExitStack() as inner:
                v = t("v", [P, CT, D], inner)
                plain_projections(nc, g, "L1qkv", [(nxT, TOK, qT), (ctxT, CTX, kT)], ctxT, CTX, v,
                                  gw[:, :, :].rearrange("p (i k) d -> p i k d", k=KC), w_in)
                prototype_attention(nc, g, "L1at", qT, kT, v, evT, also=[early])
            w2, w1_1, w1_2 = t("w2", [P, E, MC, D], ex), t("w1_1", [P, CK, RH], ex), t("w1_2", [P, CK, RH], ex)
            w2_in = loads(ex, nc, "L1_w2_in", [(w2[:, e], by_rows(a.L1_xcond_e_w2[e])) for e in range(E)])
            late = [loads(ex, nc, f"L1_late{i}", [(dst[:, :, :], by_rows(src))])
                    for i, (dst, src) in enumerate([(w1_1, a.L1_xcond_e_w1[1]), (w1_2, a.L1_xcond_e_w1[2]), (gw, a.L1_xcond_gate_w1)])]
            experts(nc, g, "L1ex", nxT, evT, routed, g1T, [w1_0, w1_1, w1_2], w2, gw, rw, b1, b2, rb, early, w2_in, late, [w_out])
        norm_transpose(nc, g, "L1rt", [(routed, TOK, nxT, None, None, None)])
        gated_output(nc, g, "L1go", nxT, g1T, wo, ob, gb, w_out, next_eps)



def mlp(nc, g, name, xT, w1, b1, w2, b2, group, gate, func, next_eps=None):
    FC = w2.shape[1]
    NBLK, TB = TOK // BANK, BANK // P
    HB = OB = 4
    with stage(nc, name, ["hid", "act_out", "ready", "done", "gated", "biased"] + STAT_SEMS,
               [("h", [P, 2, FC, BANK], F32)],
               [("hp", [P, HB, BANK], F32), ("op", [P, OB, BANK], F32)]) as (s, b, block):
        @block.tensor
        def _(pe):
            loaded(pe, group)

            def first_layer(nb):
                for m in range(FC):
                    n = nb * FC + m
                    if n >= HB:
                        pe.wait_ge(s.act_out, n - HB + 1)
                    for k in range(KC):
                        mm = nc.tensor.matmul(b.hp[:, n % HB, :], w1[:, k, m * P:(m + 1) * P], xT[:, k, nb * BANK:(nb + 1) * BANK],
                                              start=(k == 0), stop=(k == KC - 1))
                    mm.then_inc(s.hid, 1)

            def second_layer(nb):
                pe.wait_ge(s.act_out, (nb + 1) * FC)
                for q in range(TB):
                    t = nb * TB + q
                    if t >= OB:
                        pe.wait_ge(s.done, t - OB + 1)
                    for k in range(FC):
                        mm = nc.tensor.matmul(b.op[:, t % OB, 0:D], b.h[:, nb % 2, k, q * P:(q + 1) * P], w2[:, k, :], start=(k == 0), stop=(k == FC - 1))
                    mm.then_inc(s.ready, 1)

            for nb in range(NBLK):
                first_layer(nb)
                if nb == 0:
                    pe.wait_ge(s.gated, FC + 1)
                if nb:
                    second_layer(nb - 1)
            second_layer(NBLK - 1)

        @block.scalar
        def _(act):
            loaded(act, group)
            for n in range(NBLK * FC):
                nb, m = n // FC, n % FC
                act.wait_ge(s.hid, n + 1)
                if nb >= 2:
                    act.wait_ge(s.ready, (nb - 1) * TB)
                nc.scalar.activation(b.h[:, nb % 2, m, :], b.hp[:, n % HB, :], func, bias=b1[:, m:m + 1]).then_inc(s.act_out, 1)
            if next_eps is not None:
                finish_statistics_act(nc, g, act, s)

        @block.vector
        def _(dve):
            loaded(dve, group)
            for k in range(FC):
                nc.vector.tensor_tensor(w2[:, k, :], w2[:, k, :], gate[:, :], ALU.mult).then_inc(s.gated, 1)
            nc.vector.tensor_tensor(b2[:, :], b2[:, :], gate[:, :], ALU.mult).then_inc(s.gated, 1)
            dve.wait_ge(s.gated, FC + 1)
            nc.vector.tensor_tensor(g.x[:, :, :], g.x[:, :, :], b2[:, :].unsqueeze(1).broadcast_to([P, TT, D]), ALU.add).then_inc(s.biased, 1)
            dve.wait_ge(s.biased, 1)
            for t in range(TT + 2):
                if t < TT:
                    dve.wait_ge(s.ready, t + 1)
                    nc.vector.tensor_tensor(g.x[:, t, :], g.x[:, t, :], b.op[:, t % OB, 0:D], ALU.add).then_inc(s.done, 1)
                if next_eps is not None:
                    tile_statistics(nc, g, dve, s, t)
            if next_eps is not None:
                finish_statistics_dve(nc, g, dve, s, next_eps)


def modulated_mlp(nc, g, name, mod, w1, b1, w2, b2, gate, func, next_eps=None, also=()):
    F = w1.shape[1]
    with ExitStack() as ctx:
        xT = ctx.enter_context(tile(nc, name + "_xT", [P, KC, TOK]))
        w1s, w2s = ctx.enter_context(tile(nc, name + "_w1", [P, KC, F])), ctx.enter_context(tile(nc, name + "_w2", [P, F // P, D]))
        b1s, b2s = ctx.enter_context(tile(nc, name + "_b1", [P, F // P])), ctx.enter_context(tile(nc, name + "_b2", [P, D]))
        w_in = loads(ctx, nc, name + "_in", [(w1s[:, :, :], by_rows(w1)), (b1s[:, :], as_columns(b1)),
                                             (w2s[:, :, :], by_rows(w2)), (b2s[:, :], b2.partition_broadcast(P))])
        norm_transpose(nc, g, name + "nx", [(g.x, TOK, xT, (g.mv, g.rs, None), *mod)], also=[w_in, *also])
        mlp(nc, g, name + "ml", xT, w1s, b1s, w2s, b2s, w_in, gate, func, next_eps)


def store(nc, g, out):
    with stage(nc, "out", ["stored"]) as (s, b, block):
        @block.sync
        def _(sp):
            sp.dma_start(out[0].rearrange("(t p) d -> p t d", p=P), g.x[:, :, :]).then_inc(s.stored, 16)
            sp.wait_ge(s.stored, 16)


@contextmanager
def tile(nc, name, shape, dt=F32):
    with nc.sbuf_tensor(name, shape, dt) as t:
        yield t


def attend(nc, g, name, mod_q, kv, n, wq, bq, wk, bk, wv, bv, wp, bp, next_eps, gate=None, keep=None, mask_row=None, also=()):
    with ExitStack() as ctx:
        def t(name_, shape, dt=F32, where=ctx):
            return where.enter_context(tile(nc, name + name_, shape, dt))
        stored, retire = semaphores(nc, [f"{name}_stored_{n}" for n in ("k0", "q0", "k1", "q1")])
        ctx.callback(retire)
        w, bias, vbias = t("_w", [P, 4, KC, D]), t("_bias", [P, 2, KC]), t("_vb", [1, D])
        pbias = t("_pb", [P, D])
        xT = t("_xT", [P, KC, TOK])
        w_in = loads(ctx, nc, name + "_w_in", [(w[:, 0], by_rows(wk)), (w[:, 1], by_rows(wq)), (bias[:, 0], as_columns(bk)), (bias[:, 1], as_columns(bq)),
                                               (w[:, 2], by_rows(wv)), (vbias[:, :], as_row(bv))])
        p_in = loads(ctx, nc, name + "_p_in", [(w[:, 3], by_rows(wp)), (pbias[:, :], bp.partition_broadcast(P))])
        sources = [(g.x, TOK, xT, (g.mv, g.rs, None), *mod_q)]
        kvT = xT if kv is None else kv
        inner = ctx.enter_context(ExitStack())
        if isinstance(kv, tuple):
            src, mv, eps, *mod_kv = kv
            kvT = t("_cT", [P, KC, CTX], F32, inner)
            sources.append((src, n, kvT, (mv, None, eps), *mod_kv))
        norm_transpose(nc, g, name + "nx", sources, also=[w_in])
        part = t("_part", [P, 2, 3, TOK], BF16, inner)
        jobs_in = [(kvT, n, g.k_scr), (xT, TOK, g.q_scr)]
        split_projections(nc, g, name + "qk", jobs_in, w, bias, w_in, part, stored)
        v_all = t("_v", [P, NH, -(-n // P), DH], F32, inner)
        o = xT[:, :, :].rearrange("p k n -> p (k n)").rearrange("p (t d) -> p t d", d=D)
        attention(nc, g, name + "at", n, o, jobs_in, w, bias, vbias, w_in, part, v_all, stored, keep, mask_row, also=[p_in])
        inner.close()
        project_heads(nc, g, name + "pr", o, w[:, 3], pbias, p_in, next_eps, gate, also)


def program(nc, a, out):
    RETIRED.clear()
    with ExitStack() as ctx:
        lasting = [("x", [P, TT, D], F32), ("ctx", [P, CT, D], F32), ("ident", [P, P], F32), ("ident_b", [P, P], BF16),
                   ("ones", [P, P], F32), ("cond", [P, KC], F32), ("silu", [P, KC], F32), ("silu_b", [P, KC, P], F32), ("mod", [P, 32], F32),
                   ("gate", [P, 4, D], F32), ("affine", [P, 2, KC], F32), ("keep", [P, CT], F32), ("mv_ctx", [P, CT, 2], F32),
                   ("st", [P, TT, 6], F32), ("mv", [P, TT, 2], F32), ("sd", [P, TT], F32), ("rs", [P, TT], F32)]
        scratch = [("q_scr", [3, D, TOK]), ("k_scr", [3, D, TOK]), ("mask_row", [1, CTX])]
        g = named([n for n, _, _ in lasting] + [n for n, _ in scratch],
                  [ctx.enter_context(nc.sbuf_tensor("g_" + n, shape, dt)) for n, shape, dt in lasting]
                  + [nc.dram_tensor(n, shape, BF16, kind="Internal").ap() for n, shape in scratch])

        def vec(i):
            return g.mod[:, i * KC:(i + 1) * KC]

        with ExitStack() as mods:
            w, bcol = mods.enter_context(tile(nc, "m0_w", [P, KC, 4 * D])), mods.enter_context(tile(nc, "m0_b", [P, 8]))
            m_in = loads(mods, nc, "m0_in", [(w[:, :, 0:2 * D], by_rows(a.L0_xcond_Wss_q)), (w[:, :, 2 * D:], by_rows(a.L0_xcond_Wss_kv)),
                                             (bcol[:, 0:4], as_columns(a.L0_xcond_bss_q)), (bcol[:, 4:8], as_columns(a.L0_xcond_bss_kv))])
            start(nc, g, a, [m_in])
            modulation(nc, g, "m0", w, bcol, m_in, 8, 0, [0, 4])

        with ExitStack() as mods:
            w, bcol = mods.enter_context(tile(nc, "m2_w", [P, KC, 6 * D])), mods.enter_context(tile(nc, "m2_b", [P, 12]))
            brow = mods.enter_context(tile(nc, "m2_r", [1, 2, D]))
            m2_in = loads(mods, nc, "m2_in", [(w[:, :, :], by_rows(a.L2_xcond_W_mod)), (bcol[:, :], as_columns(a.L2_xcond_b_mod))]
                          + [(brow[:, i, :], as_row(a.L2_xcond_b_mod[v * D:(v + 1) * D])) for i, v in ((0, 2), (1, 5))])
            attend(nc, g, "L0", (vec(0), vec(1)), (g.ctx, g.mv_ctx, 1e-5, vec(2), vec(3)), CTX, a.L0_xcond_Wq, a.L0_xcond_bq,
                   a.L0_xcond_Wkv[:, 0:D], a.L0_xcond_bkv[0:D], a.L0_xcond_Wkv[:, D:2 * D], a.L0_xcond_bkv[D:2 * D],
                   a.L0_xcond_Wp, a.L0_xcond_bp, next_eps=1e-5, also=[m2_in])
            modulation(nc, g, "m2", w, bcol, m2_in, 12, 8, [2, 8], [4, 10], brow, 0)

        ctxT = ctx.enter_context(tile(nc, "ctxT", [P, KC, CTX]))
        expert_block(nc, g, a, ctxT, next_eps=1e-6)

        def vec2(i):
            return vec(4 + i)

        attend(nc, g, "L2s", (vec2(1), vec2(0)), None, TOK, a.L2_xcond_W_qkv[:, 0:D], a.L2_xcond_b_qkv[0:D],
               a.L2_xcond_W_qkv[:, D:2 * D], a.L2_xcond_b_qkv[D:2 * D], a.L2_xcond_W_qkv[:, 2 * D:3 * D], a.L2_xcond_b_qkv[2 * D:3 * D],
               a.L2_xcond_W_proj, a.L2_xcond_b_proj, next_eps=1e-6, gate=g.gate[:, 0])
        attend(nc, g, "L2c", (None, None), (g.ctx, g.mv_ctx, 1e-6, None, None), CTX, a.L2_xcond_W_qc, a.L2_xcond_b_qc,
               a.L2_xcond_W_kvc[:, 0:D], a.L2_xcond_b_kvc[0:D], a.L2_xcond_W_kvc[:, D:2 * D], a.L2_xcond_b_kvc[D:2 * D],
               a.L2_xcond_W_cproj, a.L2_xcond_b_cproj, next_eps=1e-6)
        with ExitStack() as mods:
            w, bcol = mods.enter_context(tile(nc, "m3_w", [P, KC, 6 * D])), mods.enter_context(tile(nc, "m3_b", [P, 12]))
            brow = mods.enter_context(tile(nc, "m3_r", [1, 2, D]))
            m3_in = loads(mods, nc, "m3_in", [(w[:, :, :], by_rows(a.L3_xcond_ada_w)), (bcol[:, :], as_columns(a.L3_xcond_ada_b))]
                          + [(brow[:, i, :], as_row(a.L3_xcond_ada_b[v * D:(v + 1) * D])) for i, v in ((0, 2), (1, 5))])
            modulated_mlp(nc, g, "L2m", (vec2(4), vec2(3)), a.L2_xcond_W_mlp1, a.L2_xcond_b_mlp1,
                          a.L2_xcond_W_mlp2, a.L2_xcond_b_mlp2, g.gate[:, 1], ACT.Gelu_apprx_tanh, next_eps=1e-6, also=[m3_in])
            modulation(nc, g, "m3", w, bcol, m3_in, 12, 20, [2, 8], [4, 10], brow, 2)

        def vec3(i):
            return vec(10 + i)

        attend(nc, g, "L3s", (vec3(1), vec3(0)), None, TOK, a.L3_xcond_qkv_w[:, 0:D], a.L3_xcond_qkv_b[0:D],
               a.L3_xcond_qkv_w[:, D:2 * D], a.L3_xcond_qkv_b[D:2 * D], a.L3_xcond_qkv_w[:, 2 * D:3 * D], a.L3_xcond_qkv_b[2 * D:3 * D],
               a.L3_xcond_sa_proj_w, a.L3_xcond_sa_proj_b, next_eps=1e-6, gate=g.gate[:, 2])
        attend(nc, g, "L3c", (None, None), ctxT, CTX, a.L3_xcond_q_w, a.L3_xcond_q_b,
               a.L3_xcond_kv_w[:, 0:D], a.L3_xcond_kv_b[0:D], a.L3_xcond_kv_w[:, D:2 * D], a.L3_xcond_kv_b[D:2 * D],
               a.L3_xcond_ca_proj_w, a.L3_xcond_ca_proj_b, next_eps=1e-6, keep=g.keep, mask_row=g.mask_row)
        modulated_mlp(nc, g, "L3m", (vec3(4), vec3(3)), a.L3_xcond_fc1_w, a.L3_xcond_fc1_b,
                      a.L3_xcond_fc2_w, a.L3_xcond_fc2_b, g.gate[:, 3], ACT.Gelu)
        store(nc, g, out)



def kernel(**inputs):
    import numpy as _np
    import concourse.bacc as _bacc
    from concourse import mybir as _mybir
    from concourse.bass_utils import run_bass_kernel_spmd as _run

    nc = _bacc.Bacc("TRN2", target_bir_lowering=False, num_devices=1)
    arrays, args = {}, {}
    for name, value in inputs.items():
        a = _np.ascontiguousarray(value)
        arrays[f"in_{name}"] = a
        args[name] = nc.dram_tensor(f"in_{name}", a.shape, _mybir.dt.from_np(a.dtype), kind="ExternalInput").ap()
    out = nc.dram_tensor("out_0", (1, 2048, 256), _mybir.dt.float32, kind="ExternalOutput").ap()
    program(nc, named(list(args), list(args.values())), out)
    r = _run(nc, [arrays], core_ids=[0])
    return r.results[0]["out_0"]
```
